# Optimizing a Trainium2 kernel written in Bass

```python
import numpy as np
import jax
import jax.numpy as jnp

def _softmax(x, axis=-1):
    return jax.nn.softmax(x, axis=axis)

def _gelu(x):
    return jax.nn.gelu(x, approximate=True)

def _silu(x):
    return jax.nn.silu(x)

def _sigmoid(x):
    return jax.nn.sigmoid(x)

def _layernorm(x, axis=-1, eps=1e-05):
    m = jnp.mean(x, axis=axis, keepdims=True)
    v = jnp.var(x, axis=axis, keepdims=True)
    return (x - m) / jnp.sqrt(v + eps)

def _scatter_add(tgt, idx, src, axis=0):
    return tgt.at[idx].add(src)

def _segment_sum(src, seg, n):
    return jax.ops.segment_sum(src, seg, n)
kernel_name = 'mk_seq_postln_d2_jaxref_r8_9fad40'

def setup_inputs(seed: int=0):
    np.random.seed(seed)
    _w = jnp.asarray

    def _L0_attn_setup():
        import jax, jax.numpy as jnp
        import numpy as np
        B, N, D, NH, MAXLEN = (2, 256, 128, 16, 256)
        HD = D // NH

        def srel_skew(x):
            b, h, n, _ = x.shape
            v = jnp.pad(x, ((0, 0), (0, 0), (0, 0), (1, 0)))
            return v.reshape(b, h, n + 1, n)[:, :, :n, :]

        def split_head(x):
            b, n, _ = x.shape
            return x.reshape(b, n, NH, HD).transpose(0, 2, 1, 3)
        key = jax.random.key(seed)
        ks = jax.random.split(key, 7)
        scale = 0.02
        return {'x': jax.random.normal(ks[0], (B, N, D), dtype=jnp.float32), 'Wq': jax.random.normal(ks[1], (D, D), dtype=jnp.float32) * scale, 'Wk': jax.random.normal(ks[2], (D, D), dtype=jnp.float32) * scale, 'Wv': jax.random.normal(ks[3], (D, D), dtype=jnp.float32) * scale, 'Wp': jax.random.normal(ks[4], (D, D), dtype=jnp.float32) * scale, 'bp': jnp.zeros((D,), dtype=jnp.float32), 'rel_embed': jax.random.normal(ks[5], (MAXLEN, D), dtype=jnp.float32) * scale}
    _L0_attn_in = _L0_attn_setup()

    def _L0_ffn_setup():
        import jax, jax.numpy as jnp
        import numpy as np
        D_MODEL = 128
        HIDDEN = 256
        E_ROUTED = 14
        E_SHARED = 2
        TOP_K = 2
        EPS = 1e-09
        RMS_EPS = 1.1920929e-07

        def _ffn(xn, rw, W1, W2):
            ms = jnp.mean(xn * xn, axis=-1, keepdims=True)
            h = xn * jax.lax.rsqrt(ms + RMS_EPS) * rw
            return jax.nn.silu(h @ W1) @ W2
        key = jax.random.key(seed)
        ks = jax.random.split(key, 9)
        B, T = (2, 128)
        x = jax.random.normal(ks[0], (B, T, D_MODEL), dtype=jnp.float32)
        router_w = jax.random.normal(ks[1], (D_MODEL, E_ROUTED), dtype=jnp.float32) * 0.006
        rms_w = jnp.ones((E_ROUTED, D_MODEL), dtype=jnp.float32)
        w1 = jax.random.normal(ks[2], (E_ROUTED, D_MODEL, HIDDEN), dtype=jnp.float32) * 0.02
        w2 = jax.random.normal(ks[3], (E_ROUTED, HIDDEN, D_MODEL), dtype=jnp.float32) * 0.02
        rms_w_s = jnp.ones((E_SHARED, D_MODEL), dtype=jnp.float32)
        w1_s = jax.random.normal(ks[4], (E_SHARED, D_MODEL, HIDDEN), dtype=jnp.float32) * 0.02
        w2_s = jax.random.normal(ks[5], (E_SHARED, HIDDEN, D_MODEL), dtype=jnp.float32) * 0.02
        return {'x': x, 'router_w': router_w, 'rms_w': rms_w, 'w1': w1, 'w2': w2, 'rms_w_s': rms_w_s, 'w1_s': w1_s, 'w2_s': w2_s}
    _L0_ffn_in = _L0_ffn_setup()

    def _L1_attn_setup():
        import jax, jax.numpy as jnp
        import numpy as np
        B, L, D = (8, 256, 128)
        LN_EPS = 1e-05
        WKV_EPS = 1e-08

        def _ln(x, g, b):
            m = x.mean(-1, keepdims=True)
            v = x.var(-1, keepdims=True)
            return (x - m) * jax.lax.rsqrt(v + LN_EPS) * g + b

        def _shift(x):
            return jnp.pad(x, ((0, 0), (1, 0), (0, 0)))[:, :-1]

        def _wkv(k, v, time_decay, time_first):
            ew = jnp.exp(-jnp.exp(time_decay))
            e0 = jnp.exp(time_first + k[:, 0])
            a0 = e0 * v[:, 0]
            b0 = e0

            def step(carry, kv):
                a, b = carry
                kt, vt = kv
                ek = jnp.exp(kt)
                a = ew * a + ek * vt
                b = ew * b + ek
                return ((a, b), a / (b + WKV_EPS))
            xs = (jnp.swapaxes(k[:, 1:], 0, 1), jnp.swapaxes(v[:, 1:], 0, 1))
            _, outs = jax.lax.scan(step, (a0, b0), xs)
            out0 = (a0 / (b0 + WKV_EPS))[:, None]
            return jnp.concatenate([out0, jnp.swapaxes(outs, 0, 1)], axis=1)
        key = jax.random.key(seed)
        ks = jax.random.split(key, 10)
        s = 1.0 / np.sqrt(D)

        def w(k, shape, scale):
            return jax.random.normal(k, shape, jnp.float32) * scale
        return {'x': jax.random.normal(ks[0], (B, L, D), jnp.float32), 'ln1_g': jnp.ones((D,), jnp.float32), 'ln1_b': jnp.zeros((D,), jnp.float32), 'Wk': w(ks[1], (D, D), s), 'Wv': w(ks[2], (D, D), s), 'Wr': w(ks[3], (D, D), s), 'Wo': w(ks[4], (D, D), s), 'time_decay': w(ks[5], (D,), 0.1), 'time_first': w(ks[6], (D,), 0.1), 'mix_k': jnp.full((D,), 0.5, jnp.float32), 'mix_v': jnp.full((D,), 0.5, jnp.float32), 'mix_r': jnp.full((D,), 0.5, jnp.float32), 'ln2_g': jnp.ones((D,), jnp.float32), 'ln2_b': jnp.zeros((D,), jnp.float32), 'Wfk': w(ks[7], (D, 4 * D), s), 'Wfv': w(ks[8], (4 * D, D), 1.0 / np.sqrt(4 * D)), 'Wfr': w(ks[9], (D, D), s)}
    _L1_attn_in = _L1_attn_setup()

    def _L1_ffn_setup():
        import jax, jax.numpy as jnp
        import numpy as np
        S, B, H = (256, 1, 128)
        N_HEADS = 16
        HEAD_DIM = H // N_HEADS
        E, K, F = (8, 2, 256)
        EPS = 1e-05

        def layernorm(x, w, b):
            mu = jnp.mean(x, axis=-1, keepdims=True)
            var = jnp.mean(jnp.square(x - mu), axis=-1, keepdims=True)
            return (x - mu) * jax.lax.rsqrt(var + EPS) * w + b
        key = jax.random.key(seed)
        ks = jax.random.split(key, 8)
        std = 0.02
        return {'x': jax.random.normal(ks[0], (S, B, H), dtype=jnp.float32), 'ln1_w': jnp.ones((H,), jnp.float32), 'ln1_b': jnp.zeros((H,), jnp.float32), 'in_proj_w': jax.random.normal(ks[1], (3 * H, H), jnp.float32) * std, 'in_proj_b': jnp.zeros((3 * H,), jnp.float32), 'out_proj_w': jax.random.normal(ks[2], (H, H), jnp.float32) * std, 'out_proj_b': jnp.zeros((H,), jnp.float32), 'ln2_w': jnp.ones((H,), jnp.float32), 'ln2_b': jnp.zeros((H,), jnp.float32), 'router_w': jax.random.normal(ks[3], (E, H), jnp.float32) * std, 'w1': jax.random.normal(ks[4], (E, H, F), jnp.float32) * std, 'w2': jax.random.normal(ks[5], (E, F, H), jnp.float32) * std}
    _L1_ffn_in = _L1_ffn_setup()
    _d = {'L0_attn_x': _L0_attn_in['x'], 'L0_attn_Wq': _L0_attn_in['Wq'], 'L0_attn_Wk': _L0_attn_in['Wk'], 'L0_attn_Wv': _L0_attn_in['Wv'], 'L0_attn_Wp': _L0_attn_in['Wp'], 'L0_attn_bp': _L0_attn_in['bp'], 'L0_attn_rel_embed': _L0_attn_in['rel_embed'], 'L0_ffn_router_w': _L0_ffn_in['router_w'], 'L0_ffn_rms_w': _L0_ffn_in['rms_w'], 'L0_ffn_w1': _L0_ffn_in['w1'], 'L0_ffn_w2': _L0_ffn_in['w2'], 'L0_ffn_rms_w_s': _L0_ffn_in['rms_w_s'], 'L0_ffn_w1_s': _L0_ffn_in['w1_s'], 'L0_ffn_w2_s': _L0_ffn_in['w2_s'], 'L1_attn_ln1_g': _L1_attn_in['ln1_g'], 'L1_attn_ln1_b': _L1_attn_in['ln1_b'], 'L1_attn_Wk': _L1_attn_in['Wk'], 'L1_attn_Wv': _L1_attn_in['Wv'], 'L1_attn_Wr': _L1_attn_in['Wr'], 'L1_attn_Wo': _L1_attn_in['Wo'], 'L1_attn_time_decay': _L1_attn_in['time_decay'], 'L1_attn_time_first': _L1_attn_in['time_first'], 'L1_attn_mix_k': _L1_attn_in['mix_k'], 'L1_attn_mix_v': _L1_attn_in['mix_v'], 'L1_attn_mix_r': _L1_attn_in['mix_r'], 'L1_attn_ln2_g': _L1_attn_in['ln2_g'], 'L1_attn_ln2_b': _L1_attn_in['ln2_b'], 'L1_attn_Wfk': _L1_attn_in['Wfk'], 'L1_attn_Wfv': _L1_attn_in['Wfv'], 'L1_attn_Wfr': _L1_attn_in['Wfr'], 'L1_ffn_ln1_w': _L1_ffn_in['ln1_w'], 'L1_ffn_ln1_b': _L1_ffn_in['ln1_b'], 'L1_ffn_in_proj_w': _L1_ffn_in['in_proj_w'], 'L1_ffn_in_proj_b': _L1_ffn_in['in_proj_b'], 'L1_ffn_out_proj_w': _L1_ffn_in['out_proj_w'], 'L1_ffn_out_proj_b': _L1_ffn_in['out_proj_b'], 'L1_ffn_ln2_w': _L1_ffn_in['ln2_w'], 'L1_ffn_ln2_b': _L1_ffn_in['ln2_b'], 'L1_ffn_router_w': _L1_ffn_in['router_w'], 'L1_ffn_w1': _L1_ffn_in['w1'], 'L1_ffn_w2': _L1_ffn_in['w2']}
    _x0 = _d['L0_attn_x']
    _d['L0_attn_x'] = jax.random.normal(jax.random.fold_in(jax.random.key(seed), 1), (32, 256, 128), dtype=_x0.dtype)
    del _x0
    return _d

def reference(L0_attn_x, L0_attn_Wq, L0_attn_Wk, L0_attn_Wv, L0_attn_Wp, L0_attn_bp, L0_attn_rel_embed, L0_ffn_router_w, L0_ffn_rms_w, L0_ffn_w1, L0_ffn_w2, L0_ffn_rms_w_s, L0_ffn_w1_s, L0_ffn_w2_s, L1_attn_ln1_g, L1_attn_ln1_b, L1_attn_Wk, L1_attn_Wv, L1_attn_Wr, L1_attn_Wo, L1_attn_time_decay, L1_attn_time_first, L1_attn_mix_k, L1_attn_mix_v, L1_attn_mix_r, L1_attn_ln2_g, L1_attn_ln2_b, L1_attn_Wfk, L1_attn_Wfv, L1_attn_Wfr, L1_ffn_ln1_w, L1_ffn_ln1_b, L1_ffn_in_proj_w, L1_ffn_in_proj_b, L1_ffn_out_proj_w, L1_ffn_out_proj_b, L1_ffn_ln2_w, L1_ffn_ln2_b, L1_ffn_router_w, L1_ffn_w1, L1_ffn_w2):

    def _L0_attn_ref(x, Wq, Wk, Wv, Wp, bp, rel_embed):
        import jax, jax.numpy as jnp
        import numpy as np
        B, N, D, NH, MAXLEN = (2, 256, 128, 16, 256)
        HD = D // NH

        def srel_skew(x):
            b, h, n, _ = x.shape
            v = jnp.pad(x, ((0, 0), (0, 0), (0, 0), (1, 0)))
            return v.reshape(b, h, n + 1, n)[:, :, :n, :]

        def split_head(x):
            b, n, _ = x.shape
            return x.reshape(b, n, NH, HD).transpose(0, 2, 1, 3)
        b, n, d = x.shape
        qx = split_head(x @ Wq.T)
        kx = split_head(x @ Wk.T)
        vx = split_head(x @ Wv.T)
        ns = jnp.arange(n) + (MAXLEN - n)
        ex = rel_embed[ns].reshape(n, NH, HD).transpose(1, 0, 2)
        srel = srel_skew(jnp.einsum('bhnd,hmd->bhnm', qx, ex))
        inv_dim = 1.0 / np.sqrt(d / NH)
        qk = (jnp.einsum('bhnd,bhmd->bhnm', qx, kx) + srel) * inv_dim
        mask = 1000000000.0 * jnp.triu(jnp.ones((n, n), dtype=x.dtype), 1)
        atten = jax.nn.softmax(qk - mask, axis=-1)
        out = jnp.einsum('bhnm,bhmd->bhnd', atten, vx).transpose(0, 2, 1, 3).reshape(b, n, d)
        return out @ Wp.T + bp

    def _L0_ffn_ref(x, router_w, rms_w, w1, w2, rms_w_s, w1_s, w2_s):
        import jax, jax.numpy as jnp
        import numpy as np
        D_MODEL = 128
        HIDDEN = 256
        E_ROUTED = 14
        E_SHARED = 2
        TOP_K = 2
        EPS = 1e-09
        RMS_EPS = 1.1920929e-07

        def _ffn(xn, rw, W1, W2):
            ms = jnp.mean(xn * xn, axis=-1, keepdims=True)
            h = xn * jax.lax.rsqrt(ms + RMS_EPS) * rw
            return jax.nn.silu(h @ W1) @ W2
        B, T, D = x.shape
        N = B * T
        xf = x.reshape(N, D)
        gates = jax.nn.softmax(xf @ router_w, axis=-1)
        top_v, top_i = jax.lax.top_k(gates, TOP_K)
        masked = jnp.zeros_like(gates).at[jnp.arange(N)[:, None], top_i].set(top_v)
        masked = masked / (masked.sum(axis=-1, keepdims=True) + EPS)
        routed = jax.vmap(lambda rw_, W1_, W2_: _ffn(xf, rw_, W1_, W2_))(rms_w, w1, w2)
        routed_out = jnp.einsum('end,ne->nd', routed, masked)
        shared = jax.vmap(lambda rw_, W1_, W2_: _ffn(xf, rw_, W1_, W2_))(rms_w_s, w1_s, w2_s).sum(0)
        return (routed_out + shared).reshape(B, T, D)

    def _L1_attn_ref(x, ln1_g, ln1_b, Wk, Wv, Wr, Wo, time_decay, time_first, mix_k, mix_v, mix_r, ln2_g, ln2_b, Wfk, Wfv, Wfr):
        import jax, jax.numpy as jnp
        import numpy as np
        B, L, D = (8, 256, 128)
        LN_EPS = 1e-05
        WKV_EPS = 1e-08

        def _ln(x, g, b):
            m = x.mean(-1, keepdims=True)
            v = x.var(-1, keepdims=True)
            return (x - m) * jax.lax.rsqrt(v + LN_EPS) * g + b

        def _shift(x):
            return jnp.pad(x, ((0, 0), (1, 0), (0, 0)))[:, :-1]

        def _wkv(k, v, time_decay, time_first):
            ew = jnp.exp(-jnp.exp(time_decay))
            e0 = jnp.exp(time_first + k[:, 0])
            a0 = e0 * v[:, 0]
            b0 = e0

            def step(carry, kv):
                a, b = carry
                kt, vt = kv
                ek = jnp.exp(kt)
                a = ew * a + ek * vt
                b = ew * b + ek
                return ((a, b), a / (b + WKV_EPS))
            xs = (jnp.swapaxes(k[:, 1:], 0, 1), jnp.swapaxes(v[:, 1:], 0, 1))
            _, outs = jax.lax.scan(step, (a0, b0), xs)
            out0 = (a0 / (b0 + WKV_EPS))[:, None]
            return jnp.concatenate([out0, jnp.swapaxes(outs, 0, 1)], axis=1)
        xn = _ln(x, ln1_g, ln1_b)
        xp = _shift(xn)
        k = (xn * mix_k + xp * (1.0 - mix_k)) @ Wk
        v = (xn * mix_v + xp * (1.0 - mix_v)) @ Wv
        r = jax.nn.sigmoid((xn * mix_r + xp * (1.0 - mix_r)) @ Wr)
        wkv = _wkv(k, v, time_decay, time_first)
        x = x + r * wkv @ Wo
        yn = _ln(x, ln2_g, ln2_b)
        yp = _shift(yn)
        kk = jnp.square(jax.nn.relu((0.5 * yn + 0.5 * yp) @ Wfk))
        rr = jax.nn.sigmoid(yn @ Wfr)
        return x + rr * (kk @ Wfv)

    def _L1_ffn_ref(x, ln1_w, ln1_b, in_proj_w, in_proj_b, out_proj_w, out_proj_b, ln2_w, ln2_b, router_w, w1, w2):
        import jax, jax.numpy as jnp
        import numpy as np
        S, B, H = (256, 1, 128)
        N_HEADS = 16
        HEAD_DIM = H // N_HEADS
        E, K, F = (8, 2, 256)
        EPS = 1e-05

        def layernorm(x, w, b):
            mu = jnp.mean(x, axis=-1, keepdims=True)
            var = jnp.mean(jnp.square(x - mu), axis=-1, keepdims=True)
            return (x - mu) * jax.lax.rsqrt(var + EPS) * w + b
        s, b, h = x.shape
        hn = layernorm(x, ln1_w, ln1_b)
        qkv = hn @ in_proj_w.T + in_proj_b
        q, k, v = jnp.split(qkv, 3, axis=-1)
        q = q.reshape(s, b, N_HEADS, HEAD_DIM)
        k = k.reshape(s, b, N_HEADS, HEAD_DIM)
        v = v.reshape(s, b, N_HEADS, HEAD_DIM)
        scores = jnp.einsum('sbnd,tbnd->bnst', q, k) / np.sqrt(HEAD_DIM)
        causal = jnp.tril(jnp.ones((s, s), bool))
        scores = jnp.where(causal[None, None], scores, -jnp.inf)
        probs = jax.nn.softmax(scores, axis=-1)
        attn = jnp.einsum('bnst,tbnd->sbnd', probs, v).reshape(s, b, h)
        attn = attn @ out_proj_w.T + out_proj_b
        x1 = x + attn
        hn2 = layernorm(x1, ln2_w, ln2_b).reshape(s * b, h)
        logits = hn2 @ router_w.T
        rp = jax.nn.softmax(logits, axis=-1)
        topw, topi = jax.lax.top_k(rp, K)
        gates = jnp.sum(jax.nn.one_hot(topi, E, dtype=hn2.dtype) * topw[..., None], axis=1)
        hmid = jax.nn.gelu(jnp.einsum('th,ehf->tef', hn2, w1), approximate=False)
        y = jnp.einsum('tef,efh->th', hmid * gates[:, :, None], w2)
        return x1 + y.reshape(s, b, h)
    x = L0_attn_x
    x = _layernorm(x + _L0_attn_ref(x, L0_attn_Wq, L0_attn_Wk, L0_attn_Wv, L0_attn_Wp, L0_attn_bp, L0_attn_rel_embed), axis=-1)
    x = _layernorm(x + _L0_ffn_ref(x, L0_ffn_router_w, L0_ffn_rms_w, L0_ffn_w1, L0_ffn_w2, L0_ffn_rms_w_s, L0_ffn_w1_s, L0_ffn_w2_s), axis=-1)
    x = _layernorm(x + _L1_attn_ref(x, L1_attn_ln1_g, L1_attn_ln1_b, L1_attn_Wk, L1_attn_Wv, L1_attn_Wr, L1_attn_Wo, L1_attn_time_decay, L1_attn_time_first, L1_attn_mix_k, L1_attn_mix_v, L1_attn_mix_r, L1_attn_ln2_g, L1_attn_ln2_b, L1_attn_Wfk, L1_attn_Wfv, L1_attn_Wfr), axis=-1)
    x = _layernorm(x + _L1_ffn_ref(x, L1_ffn_ln1_w, L1_ffn_ln1_b, L1_ffn_in_proj_w, L1_ffn_in_proj_b, L1_ffn_out_proj_w, L1_ffn_out_proj_b, L1_ffn_ln2_w, L1_ffn_ln2_b, L1_ffn_router_w, L1_ffn_w1, L1_ffn_w2), axis=-1)
    return x

_drawn_inputs = setup_inputs


def setup_inputs(seed=0):
    import zlib

    import numpy as np

    out = dict(_drawn_inputs(seed))
    spreads = {'L0_attn_bp': (0.0, 0.1),
     'L0_ffn_rms_w': (1.0, 0.6),
     'L0_ffn_rms_w_s': (1.0, 0.6),
     'L1_attn_ln1_g': (1.0, 0.2),
     'L1_attn_ln1_b': (0.0, 0.304),
     'L1_attn_mix_k': (0.5, 0.6),
     'L1_attn_mix_v': (0.5, 0.6),
     'L1_attn_mix_r': (0.5, 0.6),
     'L1_attn_ln2_g': (1.0, 0.2),
     'L1_attn_ln2_b': (0.0, 0.1),
     'L1_ffn_ln1_w': (1.0, 0.6),
     'L1_ffn_ln1_b': (0.0, 0.8),
     'L1_ffn_in_proj_b': (0.0, 0.616),
     'L1_ffn_out_proj_b': (0.0, 0.1),
     'L1_ffn_ln2_w': (1.0, 0.6),
     'L1_ffn_ln2_b': (0.0, 0.8)}
    factors = {'L0_attn_Wq': 8.0,
     'L0_attn_Wk': 8.0,
     'L0_attn_Wv': 6.419,
     'L0_attn_Wp': 6.502,
     'L0_attn_rel_embed': 8.0,
     'L1_attn_time_decay': 5.529,
     'L1_attn_time_first': 60.462,
     'L1_ffn_in_proj_w': 5.384,
     'L1_ffn_out_proj_w': 3.497,
     'L1_ffn_router_w': 8.0,
     'L1_ffn_w1': 8.0,
     'L1_ffn_w2': 8.0}
    for name, (base, spread) in spreads.items():
        noise = np.random.default_rng([zlib.crc32(name.encode()), seed]).standard_normal(out[name].shape)
        drawn = base * np.exp(spread * noise) if base else spread * noise
        out[name] = jnp.asarray(drawn.astype(out[name].dtype))
    for name, factor in factors.items():
        out[name] = (out[name] * factor).astype(out[name].dtype)
    return out
```

```python
from contextlib import ExitStack

import concourse.bass as bass
from concourse import mybir

ALU = mybir.AluOpType
ACT = mybir.ActivationFunctionType
AX = mybir.AxisListType
F32 = mybir.dt.float32
BF16 = mybir.dt.bfloat16
I32 = mybir.dt.int32

P = 128
B, T, D = 32, 256, 128
TOK = B * T
BLK = T // P
NPG = P // B
NT = TOK // P
NH, HD = 16, 8
W = P + T
QUAD = 4
NQ = NH // QUAD
NPART = 8
BIG = 1.0e30
LN_EPS = 1e-5
SM_SCALE = HD ** -0.5


def bcast(ap, n):
    return ap.unsqueeze(2).broadcast_to([ap.shape[0], ap.shape[1], n])


def scope(nc, ctx, tag):
    def sb(name, shape, dt=F32):
        return ctx.enter_context(nc.sbuf_tensor(f"{tag}_{name}", shape, dt))

    def psum(name):
        return ctx.enter_context(nc.psum_tensor(f"{tag}_{name}", [P, 512], F32))

    numbers = []

    def sem(name):
        handle = ctx.enter_context(nc.semaphore(f"{tag}_{name}"))
        numbers.append(handle.num)
        return handle

    def clear():
        runs = []
        for number in sorted(numbers):
            if runs and number == runs[-1].stop:
                runs[-1] = range(runs[-1].start, number + 1)
            else:
                runs.append(range(number, number + 1))
        if runs:
            with nc.Block() as block:
                @block.sync
                def _(sp):
                    for run in runs:
                        sp.sem_clear(run)

    ctx.callback(clear)
    return sb, psum, sem


class Core:

    def __init__(self, nc, ctx, a):
        self.nc, self.a = nc, a
        sb = lambda name, shape, dt=F32: ctx.enter_context(nc.sbuf_tensor(name, shape, dt))
        dr = lambda name, shape, dt=F32: nc.dram_tensor(name, shape, dt, kind="Internal").ap()
        self.ident = sb("ident", [P, P])
        self.neg_half = sb("neg_half", [P, 2])
        self.rows = sb("rows", [P, NT, D])
        self.q_stack = dr("q_stack", [B + 1, D * NPART, T], BF16)
        self.k_stack = dr("k_stack", [B + 1, D * NPART, T], BF16)
        self.e_stack = dr("e_stack", [D * NPART, T], BF16)
        self.expert_in = dr("expert_in", [SLOT_TILES * P, D])
        self.expert_out = dr("expert_out", [SLOT_TILES * P, D])
        self.x3 = dr("x3", [B, T, D])
        self.zeros = sb("zeros", [P, D])
        self.vector_passed, self.pool_passed, self.sync_passed = (
            ctx.enter_context(nc.semaphore(x)) for x in ("vector_passed", "pool_passed", "sync_passed"))
        self.cleared = ctx.enter_context(nc.semaphore("cleared"))
        self.shear = dr("shear", [NQ, P, QUAD, W + 2 * P])


def setup(nc, c):
    with ExitStack() as ctx:
        sb, psum, sem = scope(nc, ctx, "setup")
        pads = sb("pads", [P, QUAD, P])
        zeros = sb("zeros", [P, NPART * T], BF16)
        filled, diagonal, written = sem("filled"), sem("diagonal"), sem("pads_written")
        block = ctx.enter_context(nc.Block())

        @block.gpsimd
        def _(pool):
            nc.gpsimd.memset(c.ident[:, :], 0.0).then_inc(filled, 1)
            nc.gpsimd.memset(c.neg_half[:, :], -0.5)
            pool.wait_ge(filled, 1)
            nc.gpsimd.affine_select(out=c.ident[:, :], in_=c.ident[:, :], compare_op=ALU.not_equal,
                                    fill=1.0, base=0, pattern=[[-1, P]], channel_multiplier=1)

        @block.vector
        def _(dve):
            nc.vector.memset(pads[:, :, 0:1], 0.0).then_inc(diagonal, 1)
            nc.vector.memset(pads[:, :, 1:], -BIG).then_inc(diagonal, 1)
            nc.vector.memset(zeros[:, :], 0.0).then_inc(diagonal, 1)
            nc.vector.memset(c.zeros[:, :], 0.0).then_inc(diagonal, 1)

        @block.sync
        def _(sp):
            sp.wait_ge(diagonal, 4)
            sp.dma_start(c.expert_in.rearrange("(p s) d -> p s d", p=P), c.zeros[:, :].unsqueeze(1).broadcast_to(
                [P, SLOT_TILES, D])).then_inc(c.cleared, 16)
            for slot in range(NQ):
                sp.dma_start(c.shear[slot, :, :, P:2 * P], pads[:, :, :]).then_inc(written, 16)
                sp.dma_start(c.shear[slot, :, :, W + P:], pads[:, :, :]).then_inc(written, 16)
            for stack in (c.q_stack, c.k_stack):
                sp.dma_start(stack[B].rearrange("(p s) t -> p (s t)", p=P), zeros[:, :]).then_inc(written, 16)
            sp.wait_ge(written, 16 * (2 * NQ + 2))


def write_stack(sp, dst, parts, in_q, done):
    rows = dst.rearrange("(c s) t -> c s t", s=NPART)
    for j, (a, b) in enumerate(((0, 3), (3, 6), (6, 8))):
        src = parts[:, j:j + 1, :].broadcast_to([P, b - a, T]) if in_q else parts[:, 0:b - a, :]
        sp.dma_start(rows[:, a:b, :], src).then_inc(done, 16)


def project_heads(nc, c, values):
    a = c.a
    with ExitStack() as ctx:
        sb, psum, sem = scope(nc, ctx, "project")
        wq, wk, wv = (sb(n, [P, D]) for n in ("w_query", "w_key", "w_value"))
        rel = sb("rel_embed", [P, T])
        xt = [sb(f"xt{u}", [P, T]) for u in range(2)]
        parts = [[sb(f"parts_{n}{u}", [P, 3, T], BF16) for n in "qk"] for u in range(2)]
        rest = [[sb(f"rest_{n}{u}", [P, T]) for n in "qk"] for u in range(2)]
        rel_parts, rel_rest = sb("rel_parts", [P, 3, T], BF16), sb("rel_rest", [P, T])
        ps = [[psum(f"{n}{u}") for n in "qkv"] for u in range(2)]
        weights_in, x_in = sem("weights_in"), [sem(f"x_in{u}") for u in range(2)]
        projected, high, rest_done, mid, low = (sem(n) for n in ("projected", "high", "rest_done", "mid", "low"))
        rel_done, stacked = sem("rel_done"), [sem(f"stacked{u}") for u in range(2)]
        rel_stacked, ones_set, values_out = sem("rel_stacked"), sem("ones_set"), sem("values_out")
        block = ctx.enter_context(nc.Block())
        NI = B // 2

        @block.sync
        def _(sp):
            for w, name in ((wq, "wq_t"), (wk, "wk_t"), (wv, "wv_t"), (rel, "rel_t")):
                sp.dma_start(w[:, :], a[name]).then_inc(weights_in, 16)
            sp.wait_ge(low, 1)
            write_stack(sp, c.e_stack, rel_parts, False, rel_stacked)
            with sp.Fori(0, NI) as i:
                for u in range(2):
                    sp.wait_ge(projected, 6 * i + 3 * u)
                    sp.dma_start(xt[u][:, :], a["x_t"][:, bass.ds((2 * i + u) * T, T)]).then_inc(x_in[u], 16)
                for u in range(2):
                    sp.wait_ge(low, 4 * i + 2 * u + 3)
                    for n, stack in enumerate((c.q_stack, c.k_stack)):
                        dst = stack[bass.ds(2 * i + u, 1)].rearrange("o r t -> (o r) t")
                        write_stack(sp, dst, parts[u][n], n == 0, stacked[u])
            for u in range(2):
                sp.wait_ge(stacked[u], 96 * NI)
            sp.wait_ge(rel_stacked, 48)

        @block.tensor
        def _(pe):
            pe.wait_ge(weights_in, 64)
            with pe.Fori(0, NI) as i:
                for u in range(2):
                    pe.wait_ge(x_in[u], 16 * i + 16)
                    pe.wait_ge(rest_done, 4 * i + 1)
                    nc.tensor.matmul(ps[u][0][:, 0:T], wq[:, :], xt[u][:, :], start=True, stop=True).then_inc(projected, 1)
                    nc.tensor.matmul(ps[u][1][:, 0:T], wk[:, :], xt[u][:, :], start=True, stop=True).then_inc(projected, 1)
                    pe.wait_ge(values_out, 2 * i + u)
                    for j in range(BLK):
                        mm = nc.tensor.matmul(ps[u][2][:, j * D:(j + 1) * D], xt[u][:, j * P:(j + 1) * P], wv[:, :],
                                              start=True, stop=True)
                    mm.then_inc(projected, 1)

        @block.scalar
        def _(act):
            act.wait_ge(ones_set, 1)
            with act.Fori(0, NI) as i:
                for u in range(2):
                    act.wait_ge(stacked[u], 96 * i)
                    for n in range(2):
                        act.wait_ge(projected, 6 * i + 3 * u + n + 1)
                        nc.scalar.copy(parts[u][n][:, 0, :], ps[u][n][:, 0:T]).then_inc(high, 1)
                    act.wait_ge(projected, 6 * i + 3 * u + 3)
                    src = ps[u][2][:, 0:BLK * D].rearrange("p (j h d) -> p j h d", j=BLK, h=NH)
                    nc.scalar.copy(values[:, bass.ds((2 * i + u) * BLK, BLK), :, 0:HD], src).then_inc(values_out, 1)

        @block.vector
        def _(dve):
            nc.vector.memset(values[:, :, :, HD:HD + 1], 1.0).then_inc(ones_set, 1)
            dve.wait_ge(weights_in, 64)
            nc.vector.tensor_copy(rel_parts[:, 0, :], rel[:, :]).then_inc(rel_done, 1)
            dve.wait_ge(rel_done, 1)
            nc.vector.tensor_tensor(rel_rest[:, :], rel[:, :], rel_parts[:, 0, :], ALU.subtract).then_inc(rest_done, 1)
            dve.wait_ge(rest_done, 1)
            nc.vector.tensor_copy(rel_parts[:, 1, :], rel_rest[:, :]).then_inc(mid, 1)
            with dve.Fori(0, NI) as i:
                for u in range(2):
                    for n in range(2):
                        dve.wait_ge(high, 4 * i + 2 * u + n + 1)
                        dve.wait_ge(low, 4 * i + 1)
                        nc.vector.tensor_tensor(rest[u][n][:, :], ps[u][n][:, 0:T], parts[u][n][:, 0, :],
                                                ALU.subtract).then_inc(rest_done, 1)
                    for n in range(2):
                        dve.wait_ge(rest_done, 4 * i + 2 * u + n + 2)
                        nc.vector.tensor_copy(parts[u][n][:, 1, :], rest[u][n][:, :]).then_inc(mid, 1)

        @block.gpsimd
        def _(pool):
            pool.wait_ge(mid, 1)
            nc.gpsimd.tensor_tensor(rel_parts[:, 2, :], rel_rest[:, :], rel_parts[:, 1, :], ALU.subtract).then_inc(low, 1)
            with pool.Fori(0, NI) as i:
                for u in range(2):
                    for n in range(2):
                        pool.wait_ge(mid, 4 * i + 2 * u + n + 2)
                        nc.gpsimd.tensor_tensor(parts[u][n][:, 2, :], rest[u][n][:, :], parts[u][n][:, 1, :],
                                                ALU.subtract).then_inc(low, 1)


def attend_relative(nc, c, values):
    a = c.a
    with ExitStack() as ctx:
        sb, psum, sem = scope(nc, ctx, "attend")
        wp, bias = sb("w_out", [P, D]), sb("b_out", [P, D])
        q_st = sb("q_heads", [P, NQ, 2, 2 + T], BF16)
        k_st = sb("k_heads", [P, NQ, 2, T], BF16)
        e_st = sb("e_heads", [P, NH // 2, T], BF16)
        raw = sb("raw_relative", [P, 2, QUAD, W])
        rel = sb("relative", [P, NQ, QUAD, W])
        score, prob, prob_t = (sb(n, [P, 2, W]) for n in ("score", "prob", "prob_t"))
        least = sb("least", [P, 2, BLK])
        x_in_sb = sb("x_rows", [P, BLK, D])
        xb = sb("x_plus_bias", [P, BLK, D])
        recip = sb("recip", [P, BLK, NH])
        heads, heads_t = sb("heads", [P, BLK, NH, HD]), sb("heads_t", [P, T])
        y = sb("y", [P, BLK, D])
        stats, moments = sb("stats", [P, BLK, 6]), sb("moments", [P, BLK, 2])
        shifted, rstd = sb("shifted", [P, BLK]), sb("rstd", [P, BLK])
        e_bank, s_bank, t_bank = ([psum(f"{n}{j}") for j in range(2)] for n in ("rel_bank", "score_bank", "turn_bank"))
        o_bank, m_bank = psum("out_bank"), psum("mixed_bank")
        o_view = o_bank[:, 0:BLK * NH * (HD + 1)].rearrange("p (j h d) -> p j h d", j=BLK, h=NH)

        consts_in, x_in, first_set = sem("consts_in"), sem("x_in"), sem("first_set")
        q_in, k_in = ([sem(f"{n}_in{s}") for s in range(NQ)] for n in "qk")
        sheared_out, sheared_in = ([sem(f"sheared_{n}{s}") for s in range(NQ)] for n in ("out", "in"))
        rel_made, rel_moved = sem("rel_made"), sem("rel_moved")
        qk_made, summed = sem("qk_made"), sem("summed")
        exped, turned, turned_out = sem("exped"), sem("turned"), sem("turned_out")
        pv_done = sem("pv_done")
        recip_done, normed, heads_turned, heads_out = (sem(n) for n in ("recip_done", "normed", "heads_turned", "heads_out"))
        projected, biased, added = sem("projected"), sem("biased"), sem("added")
        stats_done, moments_done, eps_added, rstd_done, rows_done = (
            sem(n) for n in ("stats_done", "moments_done", "eps_added", "rstd_done", "rows_done"))
        block = ctx.enter_context(nc.Block())

        def load_stacks(sp, batch, quad):
            for stack, dst, done in ((c.q_stack, q_st[:, :, :, 2:], q_in), (c.k_stack, k_st, k_in)):
                rows = stack[bass.ds(batch, 1)].rearrange("o (g r) t -> r (o g) t", r=P)
                sp.dma_start(dst[:, quad, :, :], rows[:, 2 * quad:2 * quad + 2, :]).then_inc(done[quad], 16)

        def write_shear(sp, slot, half, times):
            src, dst = raw[:, half, :, :], c.shear[slot]
            sp.dma_start(dst[:, :, 0:P], src[:, :, 0:P]).then_inc(sheared_out[slot], 16)
            sp.dma_start(dst[:, :, 2 * P:P + W], src[:, :, P:W]).then_inc(sheared_out[slot], 16)

        def read_shear(sp, slot):
            pitch = QUAD * (W + 2 * P)
            base = slot * P * pitch
            for off, lo, n in ((P, 0, P), (3 * P, P, T)):
                src = bass.AP(c.shear.tensor, base + off, [[pitch - 1, P], [W + 2 * P, QUAD], [1, n]])
                sp.dma_start(rel[:, slot, :, lo:lo + n], src).then_inc(sheared_in[slot], 16)

        @block.sync
        def _(sp):
            sp.dma_start(wp[:, :], a["wp_t"]).then_inc(consts_in, 16)
            sp.dma_start(bias[:, :], a["bp"].broadcast_to([P, D])).then_inc(consts_in, 16)
            sp.dma_start(e_st[:, :, :], c.e_stack.rearrange("(g r) t -> r g t", r=P)).then_inc(consts_in, 16)
            for quad in range(3):
                load_stacks(sp, 0, quad)
            for slot in range(2):
                sp.wait_ge(rel_moved, QUAD * (slot + 1))
                write_shear(sp, slot, slot, 0)
            for slot in range(2):
                sp.wait_ge(sheared_out[slot], 32)
                read_shear(sp, slot)
            with sp.Fori(0, B) as t:
                sp.wait_ge(biased, t)
                sp.dma_start(x_in_sb[:, :, :], a["x"][bass.ds(t, 1)].rearrange("o (j p) d -> p (o j) d", p=P)
                             ).then_inc(x_in, 16)
                for quad in range(NQ):
                    sp.wait_ge(qk_made, 16 * t + QUAD * quad)
                    load_stacks(sp, t + (quad + 3) // NQ, (quad + 3) % NQ)
                    slot, turn = (quad + 2) % NQ, t + (quad + 2) // NQ
                    sp.wait_ge(sheared_in[slot], 32 * turn)
                    sp.sem_inc(c.sync_passed, 1)
                    sp.wait_ge(rel_moved, 16 * t + QUAD * (quad + 3))
                    sp.sem_inc(c.sync_passed, 1)
                    write_shear(sp, slot, quad % 2, turn)
                    sp.wait_ge(sheared_out[slot], 32 * turn + 32)
                    read_shear(sp, slot)
            for slot in range(NQ):
                sp.wait_ge(sheared_in[slot], 32 * (B + (slot < 2)))
                sp.wait_ge(q_in[slot], 16 * (B + (slot < 3)))
                sp.wait_ge(k_in[slot], 16 * (B + (slot < 3)))

        def relative(m, quad, r, first=False):
            if not first:
                nc.tensor.wait_ge(rel_moved, m - 1)
            lo, q, e = 64 * (r % 2), q_st[:, quad, r // 2, 1:], e_st[:, 2 * quad + r // 2, :]
            bank = e_bank[r % 2]
            nc.tensor.matmul(bank[:, 0:P], q[lo:lo + 64, 0:P], e[lo:lo + 64, P:T], start=True, stop=True)
            nc.tensor.matmul(bank[:, P:W], q[lo:lo + 64, P:T], e[lo:lo + 64, 0:T], start=True, stop=True
                             ).then_inc(rel_made, 1)

        @block.tensor
        def _(pe):
            pe.wait_ge(consts_in, 48)
            pe.wait_ge(first_set, 1)
            for quad in range(2):
                pe.wait_ge(q_in[quad], 16)
                for r in range(QUAD):
                    relative(QUAD * quad + r, quad, r, first=quad == 0 and r < 2)

            def turn(n, h):
                pe.wait_ge(exped, n + 3)
                pe.wait_ge(turned_out, n + 1)
                for j in range(3):
                    mm = nc.tensor.transpose(t_bank[h % 2][:, j * P:(j + 1) * P], prob[:, h % 2, j * P:(j + 1) * P],
                                             c.ident[:, :])
                mm.then_inc(turned, 1)

            def mix_values(n, h, t):
                pe.wait_ge(turned_out, n + 3)
                pt = prob_t[:, h % 2, :]
                v = [values[:, bass.ds(BLK * t + j, 1), h, :].rearrange("p o d -> p (o d)") for j in range(BLK)]
                nc.tensor.matmul(o_view[:, 0, h, :], pt[:, 0:P], v[0], start=True, stop=True)
                nc.tensor.matmul(o_view[:, 1, h, :], pt[:, P:2 * P], v[0], start=True, stop=False)
                nc.tensor.matmul(o_view[:, 1, h, :], pt[:, 2 * P:W], v[1], start=False, stop=True).then_inc(pv_done, 1)

            with pe.Fori(0, B) as t:
                for quad in range(NQ):
                    ahead = (quad + 2) % NQ
                    pe.wait_ge(q_in[ahead], 16 * (t + (quad + 2) // NQ) + 16)
                    pe.wait_ge(k_in[quad], 16 * t + 16)
                    for r in range(QUAD):
                        h = QUAD * quad + r
                        n = 16 * t + h
                        relative(n + 2 * QUAD, ahead, r)
                        pe.wait_ge(summed, n + 1)
                        lo, q, k = 64 * (r % 2), q_st[:, quad, r // 2, 2:], k_st[:, quad, r // 2, :]
                        nc.tensor.matmul(s_bank[r % 2][:, 0:P], q[lo:lo + 64, 0:P], k[lo:lo + 64, 0:P],
                                         start=True, stop=True)
                        nc.tensor.matmul(s_bank[r % 2][:, P:W], q[lo:lo + 64, P:T], k[lo:lo + 64, 0:T],
                                         start=True, stop=True).then_inc(qk_made, 1)
                        if h >= 1:
                            turn(n - 1, h - 1)
                        if h == 2:
                            pe.wait_ge(normed, t)
                        if h >= 2:
                            mix_values(n - 2, h - 2, t)
                turn(16 * t + 15, 15)
                mix_values(16 * t + 14, 14, t)
                mix_values(16 * t + 15, 15, t)
                pe.wait_ge(normed, t + 1)
                pe.wait_ge(added, t)
                for j in range(BLK):
                    mm = nc.tensor.transpose(m_bank[:, j * P:(j + 1) * P],
                                             heads[:, j, :, :].rearrange("p h d -> p (h d)"), c.ident[:, :])
                mm.then_inc(heads_turned, 1)
                pe.wait_ge(heads_out, t + 1)
                for j in range(BLK):
                    mm = nc.tensor.matmul(m_bank[:, T + j * D:T + (j + 1) * D], heads_t[:, j * P:(j + 1) * P], wp[:, :],
                                          start=True, stop=True)
                mm.then_inc(projected, 1)

        @block.scalar
        def _(act):
            def move_relative(m, half, r):
                act.wait_ge(rel_made, m + 1)
                nc.scalar.copy(raw[:, half, r, :], e_bank[r % 2][:, 0:W]).then_inc(rel_moved, 1)

            for quad in range(2):
                for r in range(QUAD):
                    move_relative(QUAD * quad + r, quad, r)
            with act.Fori(0, B) as t:
                for quad in range(NQ):
                    act.wait_ge(sheared_out[quad], 32 * t + 32)
                    for r in range(QUAD):
                        n = 16 * t + QUAD * quad + r
                        move_relative(n + 2 * QUAD, quad % 2, r)
                        act.wait_ge(summed, n + 3)
                        act.wait_ge(turned, n + 1)
                        for j, (lo, hi) in enumerate(((0, P), (P, W))):
                            e = nc.scalar.activation(prob[:, r % 2, lo:hi], score[:, r % 2, lo:hi], ACT.Exp,
                                                     bias=least[:, r % 2, j:j + 1], scale=-1.0)
                        e.then_inc(exped, 1)
                act.wait_ge(heads_turned, t + 1)
                act.wait_ge(projected, t)
                nc.scalar.copy(heads_t[:, :], m_bank[:, 0:T]).then_inc(heads_out, 1)

        @block.vector
        def _(dve):
            nc.vector.memset(q_st[:, :, :, 0:2], 0.0).then_inc(first_set, 1)
            for credit in (summed, exped, turned, turned_out, pv_done):
                dve.sem_inc(credit, 2)

            def turn_out(n, h):
                dve.wait_ge(turned, n + 3)
                dve.wait_ge(pv_done, n + 1)
                nc.vector.tensor_copy(prob_t[:, h % 2, :], t_bank[h % 2][:, 0:W]).then_inc(turned_out, 1)

            with dve.Fori(0, B) as t:
                for h in range(NH):
                    n, quad, r = 16 * t + h, h // QUAD, h % QUAD
                    if r == 0:
                        dve.wait_ge(sheared_in[quad], 32 * t + 32)
                    dve.wait_ge(qk_made, n + 1)
                    dve.wait_ge(exped, n + 1)
                    dve.sem_inc(c.vector_passed, 1)
                    dve.wait_ge(sheared_in[0], 32)
                    for j, (lo, hi) in enumerate(((0, P), (P, W))):
                        s = nc.vector.tensor_tensor_reduce(
                            score[:, r % 2, lo:hi], s_bank[r % 2][:, lo:hi], rel[:, quad, r, lo:hi],
                            -SM_SCALE, 3.0e38, ALU.add, ALU.min, least[:, r % 2, j:j + 1])
                    s.then_inc(summed, 1)
                    if h >= 1:
                        turn_out(n - 1, h - 1)
                turn_out(16 * t + 15, 15)
                dve.wait_ge(pv_done, 16 * t + 18)
                dve.wait_ge(heads_turned, t)
                nc.vector.reciprocal(recip[:, :, :], o_view[:, :, :, HD]).then_inc(recip_done, 1)
                dve.wait_ge(recip_done, t + 1)
                for j in range(BLK):
                    m = nc.vector.tensor_tensor(heads[:, j, :, :], o_view[:, j, :, 0:HD], bcast(recip[:, j, :], HD), ALU.mult)
                m.then_inc(normed, 1)
                dve.wait_ge(projected, t + 1)
                dve.wait_ge(biased, t + 1)
                dve.wait_ge(rows_done, t)
                nc.vector.tensor_tensor(y[:, :, :], m_bank[:, T:T + BLK * D].rearrange("p (j d) -> p j d", j=BLK),
                                        xb[:, :, :], ALU.add).then_inc(added, 1)
                layernorm(nc, dve, c, t, y, added, stats, moments, stats_done, moments_done, rstd, rstd_done,
                          lambda j: c.rows[:, bass.ds(BLK * t + j, 1), :].rearrange("p o d -> p (o d)"), rows_done)

        @block.gpsimd
        def _(pool):
            with pool.Fori(0, B) as t:
                pool.wait_ge(x_in, 16 * t + 16)
                pool.wait_ge(added, t)
                pool.wait_ge(consts_in, 48)
                nc.gpsimd.tensor_tensor(xb[:, :, :], x_in_sb[:, :, :],
                                        bias[:, :].unsqueeze(1).broadcast_to([P, BLK, D]), ALU.add).then_inc(biased, 1)
                inverse_root(nc, pool, c, t, moments[:, :, 1], moments_done, 1.0, LN_EPS, shifted, eps_added, rstd, rstd_done)


def layernorm(nc, dve, c, t, y, y_ready, stats, moments, stats_done, moments_done, rstd, rstd_done, out, out_done):
    dve.wait_ge(y_ready, t + 1)
    for j in range(BLK):
        s = nc.vector.bn_stats(stats[:, j, :], y[:, j, :])
    s.then_inc(stats_done, 1)
    dve.wait_ge(stats_done, t + 1)
    dve.sem_inc(c.vector_passed, 1)
    dve.wait_ge(stats_done, 1)
    for j in range(BLK):
        s = nc.vector.bn_aggr(moments[:, j, :], stats[:, j, :])
    s.then_inc(moments_done, 1)
    dve.wait_ge(rstd_done, t + 1)
    for j in range(BLK):
        s = nc.vector.tensor_scalar(out(j), y[:, j, :], moments[:, j, 0:1], rstd[:, j:j + 1], ALU.subtract, ALU.mult)
    s.then_inc(out_done, 1)


def inverse_root(nc, pool, c, t, value, ready, scale, eps, shifted, eps_added, out, out_done):
    pool.wait_ge(ready, t + 1)
    pool.sem_inc(c.pool_passed, 1)
    pool.wait_ge(ready, 1)
    nc.gpsimd.tensor_scalar(shifted[:, :], value, scale, eps, ALU.mult, ALU.add).then_inc(eps_added, 1)
    pool.wait_ge(eps_added, t + 1)
    nc.gpsimd.tensor_tensor(out[:, :], shifted[:, :], c.neg_half[:, :], ALU.pow).then_inc(out_done, 1)


TOPK = 2
H2 = 2 * P
GATE_EPS = 1e-9
RMS_EPS = 1.1920929e-07
WKV_EPS = 1e-8
GRP = 4
SLOT_TILES = 2 * NT + 16


class Count:

    def __init__(self, *names):
        self.names = names

    def __call__(self, i, name):
        return i * len(self.names) + (self.names.index(name) + 1)

    def before(self, i):
        return i * len(self.names)


def flat(ap):
    return ap.rearrange("p o d -> p (o d)")


def along(ap, k):
    return ap.unsqueeze(1).broadcast_to([ap.shape[0], k, ap.shape[1]])


class Experts:

    def __init__(self, nc, ctx, name, n, w1, w2):
        sb = lambda what, shape, dt=F32: ctx.enter_context(nc.sbuf_tensor(f"{name}_{what}", shape, dt))
        self.name, self.n = name, n
        self.steps = TOPK * NT + n
        self.table_len = self.steps + 2
        self.w1 = sb("w1", [P, n, H2 + 2])
        self.w2 = sb("w2", [P, n, 2, D])
        self.w1_dram, self.w2_dram = w1, w2
        self.slots = sb("slots", [P, NT * TOPK], I32)
        self.gates = sb("gates", [P, NT, TOPK])
        self.mean, self.rstd = sb("mean", [P, NT]), sb("rstd", [P, NT])
        self.table = sb("table", [1, self.table_len], I32)


def row_stats(nc, c, tag, rows, mean, rstd, eps, rms=False, std=None):
    steps = ("sum_means", "spread", "halves", "mean", "inner", "square", "mean_square", "var", "moment", "rstd")
    with ExitStack() as ctx:
        sb, psum, sem = scope(nc, ctx, tag)
        stats = sb("stats", [P, NT, 6])
        sum_means, spread, halves, inner, square, mean_square, var, moment, root = (
            sb(x, [P, NT]) for x in ("sum_means", "spread", "halves", "inner", "square", "mean_square", "var", "moment", "root"))
        eps_sb = sb("eps", [P, 1])
        root = root if std is None else std
        stats_done, did, rooted = sem("stats_done"), sem("did"), sem("rooted")
        block = ctx.enter_context(nc.Block())
        vec = Count(*steps)

        @block.scalar
        def _(act):
            act.wait_ge(did, vec(0, "moment"))
            nc.scalar.activation(root[:, :], moment[:, :], ACT.Sqrt, bias=eps_sb[:, 0:1]).then_inc(rooted, 1)

        @block.vector
        def _(dve):
            nc.vector.memset(eps_sb[:, :], eps)
            with dve.Fori(0, NT // 4) as i:
                for u in range(4):
                    nc.vector.bn_stats(flat(stats[:, bass.ds(4 * i + u, 1), :]), flat(rows[:, bass.ds(4 * i + u, 1), :])
                                       ).then_inc(stats_done, 1)
            dve.wait_ge(stats_done, NT)
            nc.vector.tensor_tensor(sum_means[:, :], stats[:, :, 1], stats[:, :, 4], ALU.add).then_inc(did, 1)
            nc.vector.tensor_tensor(spread[:, :], stats[:, :, 1], stats[:, :, 4], ALU.subtract).then_inc(did, 1)
            nc.vector.tensor_tensor(halves[:, :], stats[:, :, 2], stats[:, :, 5], ALU.add).then_inc(did, 1)
            dve.wait_ge(did, vec(0, "halves"))
            nc.vector.tensor_scalar(mean, sum_means[:, :], 0.5, None, ALU.mult).then_inc(did, 1)
            nc.vector.tensor_scalar(inner[:, :], halves[:, :], 1.0 / D, None, ALU.mult).then_inc(did, 1)
            nc.vector.tensor_tensor(square[:, :], spread[:, :], spread[:, :], ALU.mult).then_inc(did, 1)
            dve.wait_ge(did, vec(0, "square"))
            nc.vector.tensor_tensor(mean_square[:, :], mean, mean, ALU.mult).then_inc(did, 1)
            nc.vector.scalar_tensor_tensor(out=var[:, :], in0=square[:, :], scalar=0.25, in1=inner[:, :],
                                           op0=ALU.mult, op1=ALU.add).then_inc(did, 1)
            dve.wait_ge(did, vec(0, "var"))
            if rms:
                nc.vector.tensor_tensor(moment[:, :], var[:, :], mean_square[:, :], ALU.add).then_inc(did, 1)
            else:
                nc.vector.tensor_copy(moment[:, :], var[:, :]).then_inc(did, 1)
            dve.wait_ge(rooted, 1)
            nc.vector.reciprocal(rstd, root[:, :]).then_inc(did, 1)


def send_to_experts(nc, c, ex, shared):
    with ExitStack() as ctx:
        sb, psum, sem = scope(nc, ctx, f"{ex.name}_gate")
        logit, std = sb("logit", [P, NT, ex.n]), sb("std", [P, NT])
        row_stats(nc, c, f"{ex.name}_stats", c.rows, ex.mean[:, :], ex.rstd[:, :], RMS_EPS if shared else LN_EPS, shared, std)
        score_tokens(nc, c, ex, logit, std, shared)
        choose_experts(nc, c, ex, logit, shared)
    send_rows(nc, c, ex, shared)


def load_experts(nc, c, ex, scale, bias):
    n = ex.n
    with ExitStack() as ctx:
        sb, psum, sem = scope(nc, ctx, f"{ex.name}_load")
        per = scale.shape[1] // n
        factor = sb("factor", [P, scale.shape[1]])
        shift = sb("shift", [P, 1])
        hidden = psum("hidden_bias")[:, 0:2 * n].rearrange("p (e k) -> p e k", k=2)
        w_in, multiplied = sem("w_in"), sem("multiplied")
        block = ctx.enter_context(nc.Block())

        @block.sync
        def _(sp):
            sp.dma_start(ex.w1[:, :, 0:H2], ex.w1_dram.rearrange("e c h -> c e h")).then_inc(w_in, 16)
            sp.dma_start(ex.w2[:, :, :, :].rearrange("p e k d -> p (e k) d"),
                         ex.w2_dram.rearrange("e (k p) d -> p (e k) d", p=P)).then_inc(w_in, 16)
            sp.dma_start(factor[:, :], scale).then_inc(w_in, 16)
            if bias is not None:
                sp.dma_start(shift[:, :], bias).then_inc(w_in, 16)

        loads = 48 + 16 * (bias is not None)

        @block.tensor
        def _(pe):
            if bias is not None:
                pe.wait_ge(w_in, loads)
                for e in range(n):
                    for k in range(2):
                        mm = nc.tensor.matmul(hidden[:, e, k:k + 1], ex.w1[:, e, k * P:(k + 1) * P], shift[:, :],
                                              start=True, stop=True)
                mm.then_inc(multiplied, 1)

        @block.vector
        def _(dve):
            dve.wait_ge(w_in, loads)
            if bias is not None:
                dve.wait_ge(multiplied, 1)
                nc.vector.tensor_copy(ex.w1[:, :, H2:], hidden[:, :, :])
            else:
                nc.vector.memset(ex.w1[:, :, H2:], 0.0)
            for e in range(n):
                nc.vector.tensor_scalar(ex.w1[:, e, 0:H2], ex.w1[:, e, 0:H2], factor[:, e * per:e * per + 1], None, ALU.mult)


def normalise(nc, c, ex, out, t, count, shared):
    for j in range(count):
        x, rstd = flat(c.rows[:, bass.ds(t + j, 1), :]), ex.rstd[:, bass.ds(t + j, 1)]
        if shared:
            s = nc.vector.tensor_scalar(out[:, j, :], x, rstd, None, ALU.mult)
        else:
            s = nc.vector.tensor_scalar(out[:, j, :], x, ex.mean[:, bass.ds(t + j, 1)], rstd, ALU.subtract, ALU.mult)
    return s


def score_tokens(nc, c, ex, logit, std, shared):
    a, n = c.a, ex.n
    with ExitStack() as ctx:
        sb, psum, sem = scope(nc, ctx, f"{ex.name}_score")
        router, router_bias = sb("router", [P, n]), sb("router_bias", [P, n])
        factor, shift = sb("factor", [P, 1]), sb("shift", [P, 1])
        z = [sb(f"z{u}", [P, GRP, D]) for u in range(2)]
        zt = [sb(f"zt{u}", [P, GRP * P]) for u in range(2)]
        turn_bank, logit_bank = ([psum(f"{x}{u}") for u in range(2)] for x in ("turn_bank", "logit_bank"))
        fold_bank = psum("fold_bank")
        weights_in, biased, folded = sem("weights_in"), sem("biased"), sem("folded")
        z_ready, turned, zt_done, scored, kept = (
            sem(x) for x in ("z_ready", "turned", "zt_done", "scored", "kept"))
        block = ctx.enter_context(nc.Block())
        loads = 16 if shared else 48
        groups = NT // GRP

        @block.sync
        def _(sp):
            if shared:
                sp.dma_start(router[:, :], a["router0"]).then_inc(weights_in, 16)
            else:
                sp.dma_start(router[:, :], a["router1_t"]).then_inc(weights_in, 16)
                sp.dma_start(factor[:, :], a["ln2_w"]).then_inc(weights_in, 16)
                sp.dma_start(shift[:, :], a["ln2_b"]).then_inc(weights_in, 16)

        @block.tensor
        def _(pe):
            pe.wait_ge(weights_in, loads)
            if not shared:
                nc.tensor.matmul(fold_bank[:, 0:n], shift[:, :].broadcast_to([P, P]), router[:, :],
                                 start=True, stop=True).then_inc(biased, 1)
            pe.wait_ge(folded, 1)

            def turn(g, u):
                pe.wait_ge(z_ready, g + 1)
                for j in range(GRP):
                    mm = nc.tensor.transpose(turn_bank[u][:, j * P:(j + 1) * P], z[u][:, j, :], c.ident[:, :])
                mm.then_inc(turned, 1)

            def score(g, u):
                pe.wait_ge(zt_done, g + 1)
                pe.wait_ge(kept, g)
                for j in range(GRP):
                    mm = nc.tensor.matmul(logit_bank[u][:, j * n:(j + 1) * n], zt[u][:, j * P:(j + 1) * P], router[:, :],
                                          start=True, stop=True)
                mm.then_inc(scored, 1)

            with pe.Fori(0, groups // 2) as i:
                for u in range(2):
                    pe.wait_ge(zt_done, 2 * i + u)
                    turn(2 * i + u, u)
                    score(2 * i + u, u)

        @block.scalar
        def _(act):
            with act.Fori(0, groups // 2) as i:
                for u in range(2):
                    act.wait_ge(turned, 2 * i + u + 1)
                    act.wait_ge(scored, 2 * i + u)
                    nc.scalar.copy(zt[u][:, :], turn_bank[u][:, :]).then_inc(zt_done, 1)

        @block.vector
        def _(dve):
            dve.wait_ge(weights_in, loads)
            if not shared:
                dve.wait_ge(biased, 1)
                nc.vector.tensor_copy(router_bias[:, :], fold_bank[:, 0:n])
                nc.vector.tensor_scalar(router[:, :], router[:, :], factor[:, 0:1], None, ALU.mult).then_inc(folded, 1)
            else:
                dve.sem_inc(folded, 1)
            def keep(g, u):
                dve.wait_ge(scored, g + 1)
                for j in range(GRP):
                    out = flat(logit[:, bass.ds(GRP * g + j, 1), :])
                    if shared:
                        s = nc.vector.tensor_scalar(out, logit_bank[u][:, j * n:(j + 1) * n],
                                                    std[:, bass.ds(GRP * g + j, 1)], None, ALU.mult)
                    else:
                        s = nc.vector.tensor_tensor(out, logit_bank[u][:, j * n:(j + 1) * n], router_bias[:, :], ALU.add)
                s.then_inc(kept, 1)

            def prepare(g, u):
                normalise(nc, c, ex, z[u], GRP * g, GRP, shared).then_inc(z_ready, 1)

            prepare(0, 0)
            with dve.Fori(0, groups // 2 - 1) as i:
                for u in range(2):
                    dve.wait_ge(turned, 2 * i + u)
                    prepare(2 * i + u + 1, 1 - u)
                    keep(2 * i + u, u)
            dve.wait_ge(turned, groups - 2)
            prepare(groups - 1, 1)
            keep(groups - 2, 0)
            keep(groups - 1, 1)


def choose_experts(nc, c, ex, logit, renormalise):
    n = ex.n
    names = ("peak", "centred", "total", "recip", "gate", "g0", "is0", "score0", "best0", "first0", "rest",
             "g1", "is1", "score1", "best1", "first1", "either", "per_tile", "scan", "count", "count_up", "count_int",
             "full", "tiles", "until", "begin", "gap", "gap_all", "earlier_tiles", "place", "placed0", "slot0",
             "placed1", "slot1", "gate_sum", "gate_eps", "gate_inv", "past", "expert", "last_expert")
    vec = Count(*names)
    with ExitStack() as ctx:
        sb, psum, sem = scope(nc, ctx, f"{ex.name}_choose")
        earlier_f, earlier, every = sb("earlier_f", [P, P]), sb("earlier", [P, P], BF16), sb("every", [P, P], BF16)
        rank_i, rank_f = sb("rank_int", [P, n], I32), sb("rank", [P, n])
        tile_i, tile_f = sb("tile_int", [1, ex.table_len], I32), sb("tile_no", [1, ex.table_len])
        peak, total, recip = (sb(x, [P, NT]) for x in ("peak", "total", "recip"))
        centred, e_x, gate, hit, score = (sb(x, [P, NT, n]) for x in ("centred", "e_x", "gate", "hit", "score"))
        best = sb("best", [P, NT])
        top = sb("top", [P, TOPK, NT])
        first = [sb(f"first{k}", [P, NT, n]) for k in range(TOPK)]
        either = sb("either", [P, NT, n], BF16)
        per_tile, scan, ones = (sb(x, [P, n, NT]) for x in ("per_tile", "scan", "ones"))
        count, count_up, tiles, until, begin, gap = (sb(x, [P, n]) for x in ("count", "count_up", "tiles", "until", "begin", "gap"))
        count_int, full = sb("count_int", [P, n], I32), sb("full", [P, n], I32)
        place, placed = sb("place", [P, NT, n]), sb("placed", [P, NT, n])
        slot_f = sb("slot_f", [P, NT])
        gate_sum, gate_inv = sb("gate_sum", [P, NT]), sb("gate_inv", [P, NT])
        past, expert = sb("past", [1, ex.table_len, n]), sb("expert", [1, ex.table_len])
        half = NT // 2
        rank_bank, tile_bank = ([psum(f"{x}{u}") for u in range(2)] for x in ("rank_bank", "tile_bank"))
        filled, made, vector_did, exped, ranked = sem("filled"), sem("made"), sem("vector_did"), sem("exped"), sem("ranked")
        block = ctx.enter_context(nc.Block())

        @block.gpsimd
        def _(pool):
            nc.gpsimd.iota(rank_i[:, :], pattern=[[-1, n]], base=n, channel_multiplier=0).then_inc(made, 1)
            nc.gpsimd.iota(tile_i[:, :], pattern=[[1, ex.table_len]], base=0, channel_multiplier=0).then_inc(made, 1)
            nc.gpsimd.memset(ones[:, :, :], 1.0).then_inc(made, 1)
            nc.gpsimd.memset(earlier_f[:, :], 1.0).then_inc(filled, 1)
            pool.wait_ge(filled, 1)
            nc.gpsimd.affine_select(out=earlier_f[:, :], in_=earlier_f[:, :], compare_op=ALU.is_ge, fill=0.0,
                                    base=-1, pattern=[[1, P]], channel_multiplier=-1).then_inc(made, 1)

        @block.scalar
        def _(act):
            act.wait_ge(vector_did, vec(0, "centred"))
            nc.scalar.activation(e_x[:, :, :], centred[:, :, :], ACT.Exp).then_inc(exped, 1)

        @block.tensor
        def _(pe):
            pe.wait_ge(vector_did, vec(0, "either"))
            for u in range(2):
                chosen = either[:, u * half:(u + 1) * half, :].rearrange("p j e -> p (j e)")
                nc.tensor.matmul(tile_bank[u][:, 0:half * n], every[:, :], chosen, start=True, stop=True)
                mm = nc.tensor.matmul(rank_bank[u][:, 0:half * n], earlier[:, :], chosen, start=True, stop=True)
            mm.then_inc(ranked, 1)

        @block.vector
        def _(dve):
            did = lambda name: dve.wait_ge(vector_did, vec(0, name))
            nc.vector.memset(every[:, :], 1.0)
            dve.wait_ge(made, 4)
            nc.vector.tensor_copy(earlier[:, :], earlier_f[:, :])
            nc.vector.tensor_copy(tile_f[:, :], tile_i[:, :])
            nc.vector.tensor_copy(rank_f[:, :], rank_i[:, :])
            nc.vector.tensor_reduce(peak[:, :], logit[:, 0:NT, :], AX.X, ALU.max).then_inc(vector_did, 1)
            did("peak")
            nc.vector.tensor_tensor(centred[:, :, :], logit[:, 0:NT, :], bcast(peak[:, :], n), ALU.subtract
                                    ).then_inc(vector_did, 1)
            dve.wait_ge(exped, 1)
            nc.vector.tensor_reduce(total[:, :], e_x[:, :, :], AX.X, ALU.add).then_inc(vector_did, 1)
            did("total")
            nc.vector.reciprocal(recip[:, :], total[:, :]).then_inc(vector_did, 1)
            did("recip")
            nc.vector.tensor_tensor(gate[:, :, :], e_x[:, :, :], bcast(recip[:, :], n), ALU.mult).then_inc(vector_did, 1)
            did("gate")
            for k in range(TOPK):
                nc.vector.tensor_reduce(top[:, k, :], gate[:, :, :], AX.X, ALU.max).then_inc(vector_did, 1)
                did(f"g{k}")
                nc.vector.tensor_tensor(hit[:, :, :], gate[:, :, :], bcast(top[:, k, :], n), ALU.is_equal
                                        ).then_inc(vector_did, 1)
                did(f"is{k}")
                nc.vector.tensor_tensor(score[:, :, :], hit[:, :, :], along(rank_f[:, :], NT), ALU.mult
                                        ).then_inc(vector_did, 1)
                did(f"score{k}")
                nc.vector.tensor_reduce(best[:, :], score[:, :, :], AX.X, ALU.max).then_inc(vector_did, 1)
                did(f"best{k}")
                nc.vector.tensor_tensor(first[k][:, :, :], along(rank_f[:, :], NT), bcast(best[:, :], n), ALU.is_equal
                                        ).then_inc(vector_did, 1)
                did(f"first{k}")
                if k == 0:
                    nc.vector.scalar_tensor_tensor(out=gate[:, :, :], in0=first[0][:, :, :], scalar=-2.0, in1=gate[:, :, :],
                                                   op0=ALU.mult, op1=ALU.add).then_inc(vector_did, 1)
                    did("rest")
            nc.vector.tensor_tensor(either[:, :, :], first[0][:, :, :], first[1][:, :, :], ALU.add).then_inc(vector_did, 1)
            dve.wait_ge(ranked, 1)
            for u in range(2):
                s = nc.vector.tensor_copy(per_tile[:, :, u * half:(u + 1) * half],
                                          tile_bank[u][:, 0:half * n].rearrange("p (j e) -> p e j", e=n))
            s.then_inc(vector_did, 1)
            did("per_tile")
            nc.vector.tensor_tensor_scan(scan[:, :, :].rearrange("p e j -> p (e j)"), ones[:, :, :].rearrange("p e j -> p (e j)"),
                                         per_tile[:, :, :].rearrange("p e j -> p (e j)"), 0.0, ALU.mult, ALU.add
                                         ).then_inc(vector_did, 1)
            nc.vector.tensor_reduce(count[:, :], per_tile[:, :, :], AX.X, ALU.add).then_inc(vector_did, 1)
            did("count")
            nc.vector.tensor_scalar(count_up[:, :], count[:, :], float(P - 1), None, ALU.add).then_inc(vector_did, 1)
            did("count_up")
            nc.vector.tensor_copy(count_int[:, :], count_up[:, :]).then_inc(vector_did, 1)
            did("count_int")
            nc.vector.tensor_scalar(full[:, :], count_int[:, :], P.bit_length() - 1, None, ALU.arith_shift_right
                                    ).then_inc(vector_did, 1)
            did("full")
            nc.vector.tensor_copy(tiles[:, :], full[:, :]).then_inc(vector_did, 1)
            did("tiles")
            nc.vector.tensor_tensor_scan(until[:, :], ones[:, 0, 0:n], tiles[:, :], 0.0, ALU.mult, ALU.add
                                         ).then_inc(vector_did, 1)
            did("until")
            nc.vector.tensor_tensor(begin[:, :], until[:, :], tiles[:, :], ALU.subtract).then_inc(vector_did, 1)
            did("begin")
            nc.vector.tensor_tensor(gap[:, :], scan[:, :, NT - 1], count[:, :], ALU.subtract).then_inc(vector_did, 1)
            did("gap")
            nc.vector.scalar_tensor_tensor(out=gap[:, :], in0=begin[:, :], scalar=float(P), in1=gap[:, :],
                                           op0=ALU.mult, op1=ALU.subtract).then_inc(vector_did, 1)
            nc.vector.tensor_tensor(scan[:, :, :], scan[:, :, :], per_tile[:, :, :], ALU.subtract).then_inc(vector_did, 1)
            did("earlier_tiles")
            for u in range(2):
                s = nc.vector.tensor_tensor(place[:, u * half:(u + 1) * half, :],
                                            rank_bank[u][:, 0:half * n].rearrange("p (j e) -> p j e", e=n),
                                            scan[:, :, u * half:(u + 1) * half].rearrange("p e j -> p j e"), ALU.add)
            s.then_inc(vector_did, 1)
            did("place")
            nc.vector.tensor_tensor(place[:, :, :], place[:, :, :], along(gap[:, :], NT), ALU.add).then_inc(made, 1)
            dve.wait_ge(made, 5)
            for k in range(TOPK):
                nc.vector.tensor_tensor(placed[:, :, :], first[k][:, :, :], place[:, :, :], ALU.mult).then_inc(vector_did, 1)
                did(f"placed{k}")
                nc.vector.tensor_reduce(slot_f[:, :], placed[:, :, :], AX.X, ALU.add).then_inc(vector_did, 1)
                did(f"slot{k}")
                nc.vector.tensor_copy(ex.slots[:, :].rearrange("p (j k) -> p j k", k=TOPK)[:, :, k], slot_f[:, :]
                                      ).then_inc(made, 1)
                dve.wait_ge(made, 6 + k)
            nc.vector.tensor_tensor(gate_sum[:, :], top[:, 0, :], top[:, 1, :], ALU.add).then_inc(vector_did, 1)
            did("gate_sum")
            nc.vector.tensor_scalar(gate_sum[:, :], gate_sum[:, :], GATE_EPS, None, ALU.add).then_inc(vector_did, 1)
            did("gate_eps")
            nc.vector.reciprocal(gate_inv[:, :], gate_sum[:, :]).then_inc(vector_did, 1)
            did("gate_inv")
            for k in range(TOPK):
                if renormalise:
                    nc.vector.tensor_tensor(ex.gates[:, :, k], top[:, k, :], gate_inv[:, :], ALU.mult)
                else:
                    nc.vector.tensor_copy(ex.gates[:, :, k], top[:, k, :])
            nc.vector.tensor_tensor(past[:, :, :], along(until[0:1, :], ex.table_len), bcast(tile_f[:, :], n), ALU.is_le
                                    ).then_inc(vector_did, 1)
            did("past")
            nc.vector.tensor_reduce(expert[:, :], past[:, :, :], AX.X, ALU.add).then_inc(vector_did, 1)
            did("expert")
            nc.vector.tensor_scalar(expert[:, :], expert[:, :], float(n - 1), None, ALU.min).then_inc(vector_did, 1)
            did("last_expert")
            nc.vector.tensor_copy(ex.table[:, :], expert[:, :])


def send_rows(nc, c, ex, shared):
    a = c.a
    with ExitStack() as ctx:
        sb, psum, sem = scope(nc, ctx, f"{ex.name}_send")
        at = [sb(f"at{u}", [P, BLK * TOPK], I32) for u in range(2)]
        z = [sb(f"z{u}", [P, BLK, D]) for u in range(2)]
        w1s, w2s, rms_w = sb("w1_shared", [P, 2, H2]), sb("w2_shared", [P, 4, D]), sb("rms_shared", [P, 2])
        zt = [sb(f"zt{u}", [P, T]) for u in range(2)]
        half_tanh, hid = sb("half_tanh", [P, 4, T]), [sb(f"hid{u}", [P, 4, T]) for u in range(2)]
        turn_bank = [psum(f"turn_bank{u}") for u in range(2)]
        acc_bank = [psum(f"acc_bank{u}") for u in range(2)]
        hid_bank = [psum(f"hid_bank{k}") for k in range(4)]
        weights_in, folded, at_set, z_ready, sent = sem("weights_in"), sem("folded"), sem("at_set"), sem("z_ready"), [sem(f"sent{u}") for u in range(2)]
        turned, zt_done, hid_done, tanhed, hid_out, acc_done, acc_out = (
            sem(x) for x in ("turned", "zt_done", "hid_done", "tanhed", "hid_out", "acc_done", "acc_out"))
        block = ctx.enter_context(nc.Block())

        @block.gpsimd
        def _(pool):
            pool.wait_ge(c.cleared, 16)
            with pool.Fori(0, B // 2) as i:
                for u in range(2):
                    t = 2 * i + u
                    pool.wait_ge(sent[u], 16 * BLK * TOPK * i)
                    nc.gpsimd.tensor_copy(at[u][:, :], ex.slots[:, bass.ds(BLK * TOPK * t, BLK * TOPK)]).then_inc(at_set, 1)
                    pool.wait_ge(at_set, t + 1)
                    pool.wait_ge(z_ready, t + 1)
                    pool.sem_inc(c.pool_passed, 1)
                    pool.wait_ge(c.cleared, 16)
                    for m in range(BLK * TOPK):
                        nc.gpsimd.indirect_dma_start(c.expert_in, bass.IndirectOffsetOnAxis(at[u][:, m:m + 1], 0),
                                                     z[u][:, m // TOPK, :], None
                                                     ).then_inc(sent[u], 16)
            for u in range(2):
                pool.wait_ge(sent[u], 8 * BLK * TOPK * B)

        if not shared:
            @block.vector
            def _(dve):
                with dve.Fori(0, B // 2) as i:
                    for u in range(2):
                        dve.wait_ge(sent[u], 16 * BLK * TOPK * i)
                        normalise(nc, c, ex, z[u], BLK * (2 * i + u), BLK, shared).then_inc(z_ready, 1)
            return

        @block.sync
        def _(sp):
            sp.dma_start(w1s[:, :, :], a["w1_s"].rearrange("e c h -> c e h")).then_inc(weights_in, 16)
            sp.dma_start(w2s[:, :, :], a["w2_s"].rearrange("e (k p) d -> p (e k) d", p=P)).then_inc(weights_in, 16)
            sp.dma_start(rms_w[:, :], a["rms_w_s_t"]).then_inc(weights_in, 16)

        @block.tensor
        def _(pe):
            def turn(t, u):
                pe.wait_ge(z_ready, t + 1)
                for j in range(BLK):
                    mm = nc.tensor.transpose(turn_bank[u][:, j * P:(j + 1) * P], z[u][:, j, :], c.ident[:, :])
                mm.then_inc(turned, 1)

            pe.wait_ge(folded, 2)
            turn(0, 0)

            def products(t, u):
                pe.wait_ge(hid_out, t)
                for k in range(4):
                    nc.tensor.matmul(hid_bank[k][:, 0:T], w1s[:, k // 2, k % 2 * P:(k % 2 + 1) * P], zt[u][:, :],
                                     start=True, stop=True).then_inc(hid_done, 1)
                pe.wait_ge(acc_out, t)
                pe.wait_ge(hid_out, t + 1)
                for j in range(BLK):
                    for k in range(4):
                        mm = nc.tensor.matmul(acc_bank[u][:, j * D:(j + 1) * D], hid[u][:, k, j * P:(j + 1) * P],
                                              w2s[:, k, :], start=k == 0, stop=k == 3)
                mm.then_inc(acc_done, 1)

            with pe.Fori(0, B // 2 - 1) as i:
                for u in range(2):
                    pe.wait_ge(zt_done, 2 * i + u + 1)
                    turn(2 * i + u + 1, 1 - u)
                    products(2 * i + u, u)
            pe.wait_ge(zt_done, B - 1)
            turn(B - 1, 1)
            products(B - 2, 0)
            pe.wait_ge(zt_done, B)
            products(B - 1, 1)

        @block.scalar
        def _(act):
            with act.Fori(0, B // 2) as i:
                for u in range(2):
                    t = 2 * i + u
                    act.wait_ge(turned, t + 1)
                    act.wait_ge(hid_out, t)
                    nc.scalar.copy(zt[u][:, :], turn_bank[u][:, 0:T]).then_inc(zt_done, 1)
                    for k in range(4):
                        act.wait_ge(hid_done, 4 * t + k + 1)
                        nc.scalar.activation(half_tanh[:, k, :], hid_bank[k][:, 0:T], ACT.Tanh, scale=0.5).then_inc(tanhed, 1)

        @block.vector
        def _(dve):
            dve.wait_ge(weights_in, 48)
            for e in range(2):
                s = nc.vector.tensor_scalar(w1s[:, e, :], w1s[:, e, :], rms_w[:, e:e + 1], None, ALU.mult)
            s.then_inc(folded, 1)
            nc.vector.tensor_scalar(w2s[:, :, :], w2s[:, :, :], 0.5, None, ALU.mult).then_inc(folded, 1)

            def add(t, u):
                dve.wait_ge(acc_done, t + 1)
                rows = c.rows[:, bass.ds(BLK * t, BLK), :].rearrange("p j d -> p (j d)")
                nc.vector.tensor_tensor(rows, rows, acc_bank[u][:, 0:BLK * D], ALU.add).then_inc(acc_out, 1)

            def hidden(t, u):
                dve.wait_ge(acc_done, t)
                for k in range(4):
                    dve.wait_ge(tanhed, 4 * t + k + 1)
                    s = nc.vector.scalar_tensor_tensor(out=hid[u][:, k, :], in0=half_tanh[:, k, :], scalar=1.0,
                                                       in1=hid_bank[k][:, 0:T], op0=ALU.add, op1=ALU.mult)
                s.then_inc(hid_out, 1)

            normalise(nc, c, ex, z[0], 0, BLK, shared).then_inc(z_ready, 1)
            with dve.Fori(0, B // 2 - 1) as i:
                for u in range(2):
                    t = 2 * i + u
                    dve.wait_ge(sent[1 - u], 16 * BLK * TOPK * (i + u))
                    dve.wait_ge(turned, t)
                    normalise(nc, c, ex, z[1 - u], BLK * (t + 1), BLK, shared).then_inc(z_ready, 1)
                    hidden(t, u)
                    add(t, u)
            dve.wait_ge(sent[1], 8 * BLK * TOPK * (B - 2))
            dve.wait_ge(turned, B - 2)
            normalise(nc, c, ex, z[1], BLK * (B - 1), BLK, shared).then_inc(z_ready, 1)
            for u in range(2):
                hidden(B - 2 + u, u)
                add(B - 2 + u, u)


def run_experts(nc, c, ex, func, hidden_bias):
    with ExitStack() as ctx:
        sb, psum, sem = scope(nc, ctx, f"{ex.name}_run")
        rows_sb, rows_t, w1, hid, y = ([sb(f"{x}{u}", shape) for u in range(2)] for x, shape in (
            ("rows_sb", [P, D]), ("rows_t", [P, P]), ("w1_now", [P, H2 + 2]), ("hid", [P, 2, P]), ("y", [P, D])))
        turn_bank, hid_bank, y_bank = ([psum(f"{x}{u}") for u in range(2)] for x in ("turn_bank", "hid_bank", "y_bank"))
        rows_in, rows_out = ([sem(f"{x}{u}") for u in range(2)] for x in ("rows_in", "rows_out"))
        turned, rows_ready, w1_ready, hid_made, hid_ready, y_made, y_ready = (
            sem(x) for x in ("turned", "rows_ready", "w1_ready", "hid_made", "hid_ready", "y_made", "y_ready"))
        block = ctx.enter_context(nc.Block())
        steps = ex.steps

        def expert(eng, s):
            return eng.value_load(ex.table[0:1, bass.ds(s, 1)], min_val=0, max_val=ex.n - 1)

        @block.sync
        def _(sp):
            def load(s, u):
                sp.dma_start(rows_sb[u][:, :], c.expert_in[bass.ds(P * s, P), :]).then_inc(rows_in[u], 16)

            for u in range(2):
                load(u, u)
            with sp.Fori(0, steps // 2) as i:
                for u in range(2):
                    s = 2 * i + u
                    sp.wait_ge(turned, s + 1)
                    load(s + 2, u)
            for u in range(2):
                sp.wait_ge(rows_in[u], 8 * steps + 16)

        @block.tensor
        def _(pe):
            def turn(s, u, loaded):
                pe.wait_ge(rows_in[u], loaded)
                nc.tensor.transpose(turn_bank[u][:, 0:P], rows_sb[u][:, :], c.ident[:, :]).then_inc(turned, 1)

            def hidden(s, u):
                pe.wait_ge(w1_ready, s + 1)
                pe.wait_ge(rows_ready, s + 1)
                for k in range(2):
                    mm = nc.tensor.matmul(hid_bank[u][:, k * P:(k + 1) * P], w1[u][:, k * P:(k + 1) * P], rows_t[u][:, :],
                                          start=True, stop=True)
                mm.then_inc(hid_made, 1)

            for u in range(2):
                turn(u, u, 16)
            hidden(0, 0)
            with pe.Fori(0, steps // 2) as i:
                for u in range(2):
                    s = 2 * i + u
                    pe.wait_ge(rows_ready, s + 1)
                    turn(s + 2, u, 16 * i + 32)
                    pe.wait_ge(hid_ready, s)
                    hidden(s + 1, 1 - u)
                    pe.wait_ge(hid_ready, s + 1)
                    pe.wait_ge(y_ready, s)
                    e = expert(pe, s)
                    for k in range(2):
                        w = ex.w2[:, bass.ds(e, 1), k, :].rearrange("p o d -> p (o d)")
                        mm = nc.tensor.matmul(y_bank[u][:, 0:D], hid[u][:, k, :], w, start=k == 0, stop=k == 1)
                    mm.then_inc(y_made, 1)

        @block.gpsimd
        def _(pool):
            def weights(s, u):
                e = expert(pool, s)
                nc.gpsimd.tensor_copy(w1[u][:, :], flat(ex.w1[:, bass.ds(e, 1), :])).then_inc(w1_ready, 1)

            for u in range(2):
                weights(u, u)
            with pool.Fori(0, steps // 2) as i:
                for u in range(2):
                    s = 2 * i + u
                    pool.wait_ge(hid_ready, s + 1)
                    weights(s + 2, u)

        @block.scalar
        def _(act):
            def activate(s, u):
                act.wait_ge(hid_made, s + 1)
                src = hid_bank[u][:, 0:2 * P].rearrange("p (k t) -> p k t", k=2)
                if hidden_bias:
                    for k in range(2):
                        e = nc.scalar.activation(hid[u][:, k, :], src[:, k, :], func, bias=w1[u][:, H2 + k:H2 + k + 1])
                else:
                    e = nc.scalar.activation(hid[u][:, :, :], src, func)
                e.then_inc(hid_ready, 1)

            activate(0, 0)
            with act.Fori(0, steps // 2) as i:
                for u in range(2):
                    s = 2 * i + u
                    act.wait_ge(y_made, s)
                    activate(s + 1, 1 - u)
                    act.wait_ge(y_ready, s + 1)
                    act.dma_start(c.expert_out[bass.ds(P * s, P), :], y[u][:, :]).then_inc(rows_out[u], 16)
            for u in range(2):
                act.wait_ge(rows_out[u], 8 * steps)

        @block.vector
        def _(dve):
            def rows_transposed(s, u):
                dve.wait_ge(turned, s + 1)
                nc.vector.tensor_copy(rows_t[u][:, :], turn_bank[u][:, 0:P]).then_inc(rows_ready, 1)

            for u in range(2):
                rows_transposed(u, u)
            with dve.Fori(0, steps // 2) as i:
                for u in range(2):
                    s = 2 * i + u
                    dve.wait_ge(hid_made, s + 1)
                    rows_transposed(s + 2, u)
                    dve.wait_ge(y_made, s + 1)
                    dve.wait_ge(rows_out[u], 16 * i)
                    nc.vector.tensor_copy(y[u][:, :], y_bank[u][:, 0:D]).then_inc(y_ready, 1)


def combine(nc, c, ex, extra, out):
    with ExitStack() as ctx:
        sb, psum, sem = scope(nc, ctx, f"{ex.name}_combine")
        at = [sb(f"at{u}", [P, BLK * TOPK], I32) for u in range(2)]
        got = [sb(f"got{u}", [P, BLK * TOPK, D]) for u in range(2)]
        y, y1 = sb("y", [P, BLK, D]), sb("y1", [P, BLK, D])
        stats, moments = sb("stats", [P, BLK, 6]), sb("moments", [P, BLK, 2])
        eps, std, rstd = sb("eps", [P, 1]), sb("std", [P, BLK]), sb("rstd", [P, BLK])
        gathered, stored = [sem(f"gathered{u}") for u in range(2)], sem("stored")
        at_set, eps_set, rooted, vector_did = (sem(x) for x in ("at_set", "eps_set", "rooted", "vector_did"))
        added = sem("added")
        block = ctx.enter_context(nc.Block())
        vec = Count("one", *(("two",) if extra is not None else ()), "stats", "moments", "rstd", "rows")

        @block.sync
        def _(sp):
            if out is None:
                return
            batches = 8
            chunk = batches * BLK
            view = out.rearrange("s (g n) d -> n s g d", n=NPG)
            for k in range(B // batches):
                sp.wait_ge(vector_did, vec(batches * (k + 1) - 1, "rows"))
                for n in range(NPG):
                    sp.dma_start(view[n][:, k * chunk:(k + 1) * chunk, :],
                                 c.rows[n * B:(n + 1) * B, k * chunk:(k + 1) * chunk, :]).then_inc(stored, 16)
            sp.wait_ge(stored, 16 * NPG * B // batches)

        @block.gpsimd
        def _(pool):
            with pool.Fori(0, B // 2) as i:
                t = 2 * i
                for u in range(2):
                    pool.wait_ge(added, t + u + 1)
                    nc.gpsimd.tensor_copy(at[u][:, :], ex.slots[:, bass.ds(BLK * TOPK * (t + u), BLK * TOPK)]
                                          ).then_inc(at_set, 1)
                    pool.wait_ge(at_set, t + u + 1)
                    pool.sem_inc(c.pool_passed, 1)
                    pool.wait_ge(added, 2)
                    for i in range(BLK * TOPK):
                        nc.gpsimd.indirect_dma_start(got[u][:, i, :], None, c.expert_out[0:ex.steps * P, :],
                                                     bass.IndirectOffsetOnAxis(at[u][:, i:i + 1], 0)
                                                     ).then_inc(gathered[u], 16)

        @block.scalar
        def _(act):
            act.wait_ge(eps_set, 1)
            with act.Fori(0, B // 2) as i:
                t = 2 * i
                for u in range(2):
                    act.wait_ge(vector_did, vec(t + u, "moments"))
                    nc.scalar.activation(std[:, :], moments[:, :, 1], ACT.Sqrt, bias=eps[:, 0:1]).then_inc(rooted, 1)

        @block.vector
        def _(dve):
            did = lambda now, name: dve.wait_ge(vector_did, vec(now, name))
            nc.vector.memset(eps[:, :], LN_EPS).then_inc(eps_set, 1)
            dve.sem_inc(added, 2)
            with dve.Fori(0, B // 2) as i:
                t = 2 * i
                for u in range(2):
                    now = t + u
                    dve.wait_ge(gathered[u], 8 * BLK * TOPK * t + 16 * BLK * TOPK)
                    dve.wait_ge(vector_did, vec.before(now))
                    for k in range(TOPK):
                        for j in range(BLK):
                            base = flat(c.rows[:, bass.ds(BLK * now + j, 1), :]) if k == 0 else y1[:, j, :]
                            s = nc.vector.scalar_tensor_tensor(
                                out=(y1 if k == 0 else y)[:, j, :], in0=got[u][:, TOPK * j + k, :],
                                scalar=ex.gates[:, bass.ds(BLK * now + j, 1), k], in1=base, op0=ALU.mult, op1=ALU.add)
                        if k == 0:
                            s.then_inc(vector_did, 1)
                            did(now, "one")
                    if extra is not None:
                        s.then_inc(vector_did, 1)
                        did(now, "two")
                        s = nc.vector.tensor_tensor(y[:, :, :], y[:, :, :], extra[:, bass.ds(BLK * now, BLK), :], ALU.add)
                    s.then_inc(added, 1)
                    dve.wait_ge(added, now + 3)
                    for j in range(BLK):
                        s = nc.vector.bn_stats(stats[:, j, :], y[:, j, :])
                    s.then_inc(vector_did, 1)
                    did(now, "stats")
                    dve.sem_inc(c.vector_passed, 1)
                    dve.wait_ge(added, 3)
                    for j in range(BLK):
                        s = nc.vector.bn_aggr(moments[:, j, :], stats[:, j, :])
                    s.then_inc(vector_did, 1)
                    dve.wait_ge(rooted, now + 1)
                    nc.vector.reciprocal(rstd[:, :], std[:, :]).then_inc(vector_did, 1)
                    did(now, "rstd")
                    for j in range(BLK):
                        row = flat(c.rows[:, bass.ds(BLK * now + j, 1), :])
                        s = nc.vector.tensor_scalar(row, y[:, j, :], moments[:, j, 0:1], rstd[:, j:j + 1],
                                                    ALU.subtract, ALU.mult)
                    s.then_inc(vector_did, 1)


def load_columns(sp, a, names, dst, done):
    for k, name in enumerate(names):
        sp.dma_start(dst[:, k:k + 1], a[name]).then_inc(done, 16)


def mix_time(nc, c, mean, rstd, twice):
    a = c.a
    names = ("mix_k", "mix_v", "mix_r", "rwkv_ln1_g", "rwkv_ln1_b", "time_decay", "time_first")
    vec = Count("ekv", "scan_a", "scan_b", "b_eps", "b_inv", "ratio", "gated")
    with ExitStack() as ctx:
        sb, psum, sem = scope(nc, ctx, "time")
        raw, w_now, w_old = (sb(x, [P, 3, D]) for x in ("w_raw", "w_now", "w_old"))
        w_out = sb("w_out", [P, D])
        cols, rest = sb("cols", [P, len(names)]), sb("rest", [P, 3])
        decay, keep = sb("decay", [P, 1]), sb("keep", [P, 1])
        decay_row = sb("decay_row", [P, T])
        z = [sb(f"z{u}", [P, BLK, D]) for u in range(2)]
        xn = [sb(f"xn{u}", [P, 1 + T]) for u in range(2)]
        e_k, half_tanh, gated = ([sb(f"{x}{u}", [P, T]) for u in range(2)] for x in ("e_k", "half_tanh", "gated"))
        ekv, scan_a, scan_b, b_eps, b_inv, ratio = (sb(x, [P, T]) for x in ("ekv", "scan_a", "scan_b", "b_eps", "b_inv", "ratio"))
        turn_bank, k_bank, v_bank, ro_bank = (
            [psum(f"{x}{u}") for u in range(2)] for x in ("turn_bank", "k_bank", "v_bank", "ro_bank"))
        loaded, decayed, folded, zero_set = sem("loaded"), sem("decayed"), sem("folded"), sem("zero_set")
        z_ready, turned, xn_ready, made, exped, tanhed, vector_did, o_made, o_out = (
            sem(x) for x in ("z_ready", "turned", "xn_ready", "made", "exped", "tanhed", "vector_did", "o_made", "o_out"))
        block = ctx.enter_context(nc.Block())
        gain, shift = cols[:, 3:4], cols[:, 4:5]
        first = cols[:, 6:7]
        loads = 16 * (4 + len(names))

        @block.sync
        def _(sp):
            for k, name in enumerate(("rwkv_wk", "rwkv_wv", "rwkv_wr")):
                sp.dma_start(raw[:, k, :], a[name]).then_inc(loaded, 16)
            sp.dma_start(w_out[:, :], a["rwkv_wo"]).then_inc(loaded, 16)
            load_columns(sp, a, names, cols, loaded)

        @block.tensor
        def _(pe):
            pe.wait_ge(folded, 3)

            def turn(t, u):
                pe.wait_ge(z_ready, t + 1)
                for j in range(BLK):
                    mm = nc.tensor.transpose(turn_bank[u][:, j * P:(j + 1) * P], z[u][:, j, :], c.ident[:, :])
                mm.then_inc(turned, 1)

            def project(t, u):
                pe.wait_ge(xn_ready, t + 1)
                for k, out in enumerate((k_bank[u][:, 0:T], v_bank[u][:, 0:T], ro_bank[u][:, 0:T])):
                    nc.tensor.matmul(out, w_now[:, k, :], xn[u][:, 1:], start=True, stop=False)
                    nc.tensor.matmul(out, w_old[:, k, :], xn[u][:, 0:T], start=False, stop=True).then_inc(made, 1)

            def output(t, u):
                pe.wait_ge(vector_did, vec(t, "gated"))
                for j in range(BLK):
                    mm = nc.tensor.matmul(ro_bank[u][:, T + j * D:T + (j + 1) * D], gated[u][:, j * P:(j + 1) * P],
                                          w_out[:, :], start=True, stop=True)
                mm.then_inc(o_made, 1)

            turn(0, 0)
            project(0, 0)
            turn(1, 1)
            with pe.Fori(0, B // 2 - 1) as i:
                for u in range(2):
                    t = 2 * i + u
                    pe.wait_ge(o_out, t)
                    project(t + 1, 1 - u)
                    turn(t + 2, u)
                    output(t, u)
            pe.wait_ge(o_out, B - 2)
            project(B - 1, 1)
            output(B - 2, 0)
            output(B - 1, 1)

        @block.scalar
        def _(act):
            act.wait_ge(loaded, loads)
            act.wait_ge(zero_set, 1)
            nc.scalar.activation(decay[:, :], cols[:, 5:6], ACT.Exp).then_inc(decayed, 1)
            act.wait_ge(decayed, 1)
            nc.scalar.activation(keep[:, :], decay[:, :], ACT.Exp, scale=-1.0).then_inc(decayed, 1)

            def affine(t, u):
                act.wait_ge(turned, t + 1)
                nc.scalar.activation(xn[u][:, 1:], turn_bank[u][:, 0:T], ACT.Identity, bias=shift, scale=gain).then_inc(xn_ready, 1)

            def exponents(t, u):
                act.wait_ge(made, 3 * t + 1)
                nc.scalar.activation(e_k[u][:, 0:1], k_bank[u][:, 0:1], ACT.Exp, bias=first)
                nc.scalar.activation(e_k[u][:, 1:], k_bank[u][:, 1:T], ACT.Exp).then_inc(exped, 1)
                act.wait_ge(made, 3 * t + 3)
                nc.scalar.activation(half_tanh[u][:, :], ro_bank[u][:, 0:T], ACT.Tanh, scale=0.5).then_inc(tanhed, 1)

            affine(0, 0)
            affine(1, 1)
            with act.Fori(0, B // 2 - 1) as i:
                for u in range(2):
                    t = 2 * i + u
                    act.wait_ge(vector_did, vec.before(t))
                    exponents(t, u)
                    affine(t + 2, u)
            for u in range(2):
                act.wait_ge(vector_did, vec.before(B - 2 + u))
                exponents(B - 2 + u, u)

        @block.vector
        def _(dve):
            did = lambda t, name: dve.wait_ge(vector_did, vec(t, name))
            nc.vector.memset(xn[0][:, 0:1], 0.0)
            nc.vector.memset(xn[1][:, 0:1], 0.0).then_inc(zero_set, 1)
            dve.wait_ge(loaded, loads)
            nc.vector.tensor_scalar(rest[:, :], cols[:, 0:3], -1.0, 1.0, ALU.mult, ALU.add).then_inc(folded, 1)
            dve.wait_ge(folded, 1)
            for k in range(3):
                nc.vector.tensor_scalar(w_now[:, k, :], raw[:, k, :], cols[:, k:k + 1], None, ALU.mult)
                nc.vector.tensor_scalar(w_old[:, k, :], raw[:, k, :], rest[:, k:k + 1], None, ALU.mult)
            nc.vector.tensor_scalar(w_out[:, :], w_out[:, :], 0.5, None, ALU.mult).then_inc(folded, 1)
            dve.wait_ge(decayed, 2)
            nc.vector.tensor_copy(decay_row[:, :], keep[:, 0:1].broadcast_to([P, T])).then_inc(folded, 1)
            dve.wait_ge(folded, 3)

            def prepare(t, u):
                normalise_rows(nc, c.rows, mean, rstd, z[u], BLK * t, BLK).then_inc(z_ready, 1)

            def mix(t, u):
                dve.wait_ge(exped, t + 1)
                dve.wait_ge(made, 3 * t + 2)
                nc.vector.tensor_tensor(ekv[:, :], e_k[u][:, :], v_bank[u][:, 0:T], ALU.mult).then_inc(vector_did, 1)
                did(t, "ekv")
                nc.vector.tensor_tensor_scan(scan_a[:, :], decay_row[:, :], ekv[:, :], 0.0, ALU.mult, ALU.add
                                             ).then_inc(vector_did, 1)
                nc.vector.tensor_tensor_scan(scan_b[:, :], decay_row[:, :], e_k[u][:, :], 0.0, ALU.mult, ALU.add
                                             ).then_inc(vector_did, 1)
                did(t, "scan_b")
                nc.vector.tensor_scalar(b_eps[:, :], scan_b[:, :], WKV_EPS, None, ALU.add).then_inc(vector_did, 1)
                did(t, "b_eps")
                nc.vector.reciprocal(b_inv[:, :], b_eps[:, :]).then_inc(vector_did, 1)
                did(t, "b_inv")
                nc.vector.tensor_tensor(ratio[:, :], scan_a[:, :], b_inv[:, :], ALU.mult).then_inc(vector_did, 1)
                dve.wait_ge(tanhed, t + 1)
                did(t, "ratio")
                nc.vector.scalar_tensor_tensor(out=gated[u][:, :], in0=half_tanh[u][:, :], scalar=1.0, in1=ratio[:, :],
                                               op0=ALU.add, op1=ALU.mult).then_inc(vector_did, 1)

            def add(t, u):
                dve.wait_ge(o_made, t + 1)
                out = ro_bank[u][:, T:T + BLK * D]
                rows = c.rows[:, bass.ds(BLK * t, BLK), :].rearrange("p j d -> p (j d)")
                nc.vector.scalar_tensor_tensor(out=twice[:, bass.ds(BLK * t, BLK), :].rearrange("p j d -> p (j d)"), in0=rows,
                                               scalar=2.0, in1=out, op0=ALU.mult, op1=ALU.add)
                nc.vector.tensor_tensor(rows, rows, out, ALU.add).then_inc(o_out, 1)

            prepare(0, 0)
            prepare(1, 1)
            mix(0, 0)
            with dve.Fori(0, B // 2 - 1) as i:
                for u in range(2):
                    t = 2 * i + u
                    dve.wait_ge(turned, t + 1)
                    prepare(t + 2, u)
                    add(t, u)
                    mix(t + 1, 1 - u)
            add(B - 2, 0)
            mix(B - 1, 1)
            add(B - 1, 1)


def normalise_rows(nc, rows, mean, rstd, out, t, count):
    for j in range(count):
        s = nc.vector.tensor_scalar(out[:, j, :], flat(rows[:, bass.ds(t + j, 1), :]), mean[:, bass.ds(t + j, 1)],
                                    rstd[:, bass.ds(t + j, 1)], ALU.subtract, ALU.mult)
    return s


def mix_channels(nc, c, mean, rstd, total):
    a = c.a
    NK = 4 * D // P
    names = ("rwkv_ln2_g", "rwkv_ln2_b")
    with ExitStack() as ctx:
        sb, psum, sem = scope(nc, ctx, "channel")
        w_k, w_v, w_r = sb("w_k", [P, NK * P]), sb("w_v", [P, NK, D]), sb("w_r", [P, D])
        cols = sb("cols", [P, len(names)])
        z = [sb(f"z{u}", [P, BLK, D]) for u in range(2)]
        yn = [sb(f"yn{u}", [P, 1 + T]) for u in range(2)]
        both = [sb(f"both{u}", [P, T]) for u in range(2)]
        kk = [sb(f"kk{u}", [P, NK, T]) for u in range(2)]
        relu = sb("relu", [P, NK, T])
        half_tanh, gated = sb("half_tanh", [P, T]), sb("gated", [P, T])
        turn_bank = [psum(f"turn_bank{u}") for u in range(2)]
        k_bank = [psum(f"k_bank{k}") for k in range(NK)]
        r_bank, o_bank = psum("r_bank"), psum("o_bank")
        loaded, folded, zero_set = sem("loaded"), sem("folded"), sem("zero_set")
        z_ready, turned, yn_ready, both_ready, r_made, k_made, rectified, squared, tanhed, o_made, gated_done, o_out = (
            sem(x) for x in ("z_ready", "turned", "yn_ready", "both_ready", "r_made", "k_made", "rectified", "squared", "tanhed", "o_made",
                             "gated_done", "o_out"))
        block = ctx.enter_context(nc.Block())
        loads = 16 * (3 + len(names))

        @block.sync
        def _(sp):
            sp.dma_start(w_k[:, :], a["rwkv_wfk"]).then_inc(loaded, 16)
            sp.dma_start(w_v[:, :, :], a["rwkv_wfv"].rearrange("(k p) d -> p k d", p=P)).then_inc(loaded, 16)
            sp.dma_start(w_r[:, :], a["rwkv_wfr"]).then_inc(loaded, 16)
            load_columns(sp, a, names, cols, loaded)

        @block.tensor
        def _(pe):
            pe.wait_ge(folded, 2)

            def turn(t, u):
                pe.wait_ge(z_ready, t + 1)
                for j in range(BLK):
                    mm = nc.tensor.transpose(turn_bank[u][:, j * P:(j + 1) * P], z[u][:, j, :], c.ident[:, :])
                mm.then_inc(turned, 1)

            def keys(t, u):
                pe.wait_ge(tanhed, t)
                pe.wait_ge(yn_ready, t + 1)
                for j in range(BLK):
                    mm = nc.tensor.matmul(r_bank[:, j * D:(j + 1) * D], yn[u][:, 1 + j * P:1 + (j + 1) * P], w_r[:, :],
                                          start=True, stop=True)
                mm.then_inc(r_made, 1)
                pe.wait_ge(both_ready, t + 1)
                for k in range(NK):
                    pe.wait_ge(rectified, NK * t)
                    nc.tensor.matmul(k_bank[k][:, 0:T], w_k[:, k * P:(k + 1) * P], both[u][:, :], start=True, stop=True
                                     ).then_inc(k_made, 1)

            def values(t, u):
                pe.wait_ge(o_out, t)
                pe.wait_ge(squared, t + 1)
                for j in range(BLK):
                    for k in range(NK):
                        mm = nc.tensor.matmul(o_bank[:, j * D:(j + 1) * D], kk[u][:, k, j * P:(j + 1) * P], w_v[:, k, :],
                                              start=k == 0, stop=k == NK - 1)
                mm.then_inc(o_made, 1)

            turn(0, 0)
            turn(1, 1)
            keys(0, 0)
            with pe.Fori(0, B // 2 - 1) as i:
                for u in range(2):
                    t = 2 * i + u
                    turn(t + 2, u)
                    keys(t + 1, 1 - u)
                    values(t, u)
            keys(B - 1, 1)
            values(B - 2, 0)
            values(B - 1, 1)

        @block.scalar
        def _(act):
            act.wait_ge(loaded, loads)
            act.wait_ge(zero_set, 1)

            def affine(t, u):
                act.wait_ge(turned, t + 1)
                nc.scalar.activation(yn[u][:, 1:], turn_bank[u][:, 0:T], ACT.Identity, bias=cols[:, 1:2],
                                     scale=cols[:, 0:1]).then_inc(yn_ready, 1)

            def gate(t):
                act.wait_ge(squared, t)
                for k in range(NK):
                    act.wait_ge(k_made, NK * t + k + 1)
                    nc.scalar.activation(relu[:, k, :], k_bank[k][:, 0:T], ACT.Relu).then_inc(rectified, 1)
                act.wait_ge(r_made, t + 1)
                act.wait_ge(gated_done, t)
                nc.scalar.activation(half_tanh[:, :], r_bank[:, 0:BLK * D], ACT.Tanh, scale=0.5).then_inc(tanhed, 1)

            affine(0, 0)
            affine(1, 1)
            gate(0)
            with act.Fori(0, B // 2 - 1) as i:
                for u in range(2):
                    t = 2 * i + u
                    act.wait_ge(both_ready, t + 1)
                    affine(t + 2, u)
                    gate(t + 1)
            gate(B - 1)

        @block.gpsimd
        def _(pool):
            def add_old(t, u):
                pool.wait_ge(yn_ready, t + 1)
                nc.gpsimd.tensor_tensor(both[u][:, :], yn[u][:, 1:], yn[u][:, 0:T], ALU.add).then_inc(both_ready, 1)

            add_old(0, 0)
            add_old(1, 1)
            with pool.Fori(0, B // 2 - 1) as i:
                for u in range(2):
                    pool.wait_ge(k_made, NK * (2 * i + u) + NK)
                    add_old(2 * i + u + 2, u)

        @block.vector
        def _(dve):
            nc.vector.memset(yn[0][:, 0:1], 0.0)
            nc.vector.memset(yn[1][:, 0:1], 0.0).then_inc(zero_set, 1)
            dve.wait_ge(loaded, loads)
            nc.vector.tensor_scalar(w_k[:, :], w_k[:, :], 0.5, None, ALU.mult).then_inc(folded, 1)
            nc.vector.tensor_scalar(w_v[:, :, :], w_v[:, :, :], 0.5, None, ALU.mult).then_inc(folded, 1)

            def prepare(t, u):
                normalise_rows(nc, c.rows, mean, rstd, z[u], BLK * t, BLK).then_inc(z_ready, 1)

            def square(t, u):
                dve.wait_ge(rectified, NK * t + NK)
                nc.vector.tensor_tensor(kk[u][:, :, :], relu[:, :, :], relu[:, :, :], ALU.mult).then_inc(squared, 1)

            def add(t, u):
                dve.wait_ge(tanhed, t + 1)
                dve.wait_ge(o_made, t + 1)
                nc.vector.scalar_tensor_tensor(out=gated[:, :], in0=half_tanh[:, :], scalar=1.0, in1=o_bank[:, 0:BLK * D],
                                               op0=ALU.add, op1=ALU.mult).then_inc(gated_done, 1)
                dve.wait_ge(gated_done, t + 1)
                sums = total[:, bass.ds(BLK * t, BLK), :].rearrange("p j d -> p (j d)")
                nc.vector.tensor_tensor(sums, sums, gated[:, :], ALU.add).then_inc(o_out, 1)

            prepare(0, 0)
            prepare(1, 1)
            square(0, 0)
            with dve.Fori(0, B // 2 - 1) as i:
                for u in range(2):
                    t = 2 * i + u
                    dve.wait_ge(turned, t + 1)
                    prepare(t + 2, u)
                    square(t + 1, 1 - u)
                    dve.wait_ge(o_out, t)
                    add(t, u)
            square(B - 1, 1)
            add(B - 2, 0)
            dve.wait_ge(o_out, B - 1)
            add(B - 1, 1)


def keep_rows(nc, c, total, mean, rstd):
    CH = 8
    with ExitStack() as ctx:
        sb, psum, sem = scope(nc, ctx, "keep")
        ready, stored = sem("ready"), sem("stored")
        block = ctx.enter_context(nc.Block())
        x3 = c.x3.rearrange("b (j p) d -> p (b j) d", p=P)

        @block.vector
        def _(dve):
            with dve.Fori(0, NT // CH) as i:
                for j in range(CH):
                    at = CH * i + j
                    s = nc.vector.tensor_scalar(flat(c.rows[:, bass.ds(at, 1), :]), flat(total[:, bass.ds(at, 1), :]),
                                                mean[:, bass.ds(at, 1)], rstd[:, bass.ds(at, 1)], ALU.subtract, ALU.mult)
                s.then_inc(ready, 1)

        @block.sync
        def _(sp):
            for i in range(NT // CH):
                sp.wait_ge(ready, i + 1)
                sp.dma_start(x3[:, i * CH:(i + 1) * CH, :], c.rows[:, i * CH:(i + 1) * CH, :]).then_inc(stored, 16)
            sp.wait_ge(stored, 16 * (NT // CH))


def recur(nc, c):
    with ExitStack() as ctx:
        sb, psum, sem = scope(nc, ctx, "recur")
        twice = sb("twice", [P, NT, D])
        mean, rstd = sb("mean", [P, NT]), sb("rstd", [P, NT])
        row_stats(nc, c, "recur1", c.rows, mean[:, :], rstd[:, :], LN_EPS)
        mix_time(nc, c, mean, rstd, twice)
        row_stats(nc, c, "recur2", c.rows, mean[:, :], rstd[:, :], LN_EPS)
        mix_channels(nc, c, mean, rstd, twice)
        row_stats(nc, c, "recur3", twice, mean[:, :], rstd[:, :], LN_EPS)
        keep_rows(nc, c, twice, mean, rstd)


def load_groups(nc, dst, src, tag):
    with ExitStack() as ctx:
        sb, psum, sem = scope(nc, ctx, tag)
        loaded = sem("loaded")
        block = ctx.enter_context(nc.Block())
        view = src.rearrange("s (g n) d -> n s g d", n=NPG)

        @block.sync
        def _(sp):
            for n in range(NPG):
                sp.dma_start(dst[n * B:(n + 1) * B, :, :], view[n]).then_inc(loaded, 16)
            sp.wait_ge(loaded, 16 * NPG)


def attend_batches(nc, c, mean, rstd):
    a = c.a
    HB = 4
    SLOTS = 4
    STEPS = NT // SLOTS
    C = SLOTS * P
    soft = Count("peak", "centred")
    with ExitStack() as ctx:
        sb, psum, sem = scope(nc, ctx, "batch")
        w_in, w_out = sb("w_in", [P, 3 * D]), sb("w_out", [P, D])
        w_out_b = sb("w_out_b", [P, HB, D])
        b_in, cols = sb("b_in", [P, 3]), sb("cols", [P, 2])
        out_bias, row_bias = sb("out_bias", [P, D]), sb("row_bias", [P, D])
        of_b, of_a = sb("of_b", [P, HB]), sb("of_a", [P, HB])
        q_shift, k_shift = sb("q_shift", [P, HB]), sb("k_shift", [P, HB])
        column_a = sb("column_a", [P, NH, HD])
        causal_f, causal = sb("causal_f", [P, NPG * P]), sb("causal", [P, NPG * P], BF16)
        ident_bf = sb("ident_bf", [P, P], BF16)
        of_head = sb("of_head", [P, HB, HB])
        z = sb("z", [P, SLOTS, D])
        hn = [sb(f"hn{v}", [P, C]) for v in range(2)]
        q_blocks, k_blocks, hn_blocks = ([sb(f"{x}{v}", [P, SLOTS * NPG, HB, B]) for v in range(2)]
                                         for x in ("q_blocks", "k_blocks", "hn_blocks"))
        v_blocks = [sb(f"v_blocks{s}", [P, NPG, D]) for s in range(SLOTS)]
        centred, e_x, prob = ([sb(f"{x}{u}", [P, NPG * HB, B]) for u in range(2)] for x in ("centred", "e_x", "prob"))
        peak, total = sb("peak", [P, NPG * HB]), sb("total", [P, NPG * HB])
        recip = [sb(f"recip_{u}", [P, NPG * HB]) for u in range(2)]
        prob_t, out_t = sb("prob_t", [P, NPG * P]), sb("out_t", [P, HB, NPG, B])
        fresh = sb("fresh", [P, D])
        turn_bank, q_bank, k_bank, v_bank, s_bank, p_bank, o_bank, x_bank = (
            psum(x) for x in ("turn_bank", "q_bank", "k_bank", "v_bank", "s_bank", "p_bank", "o_bank", "x_bank"))
        loaded, made, folded = sem("loaded"), sem("made"), sem("folded")
        hn_spread = sem("hn_spread")
        z_ready, turned, hn_ready, q_made, k_made, q_ready, k_ready = (
            sem(x) for x in ("z_ready", "turned", "hn_ready", "q_made", "k_made", "q_ready", "k_ready"))
        s_made, v_made, v_ready, softened, exped, totalled, recip_done, normed = (
            sem(x) for x in ("s_made", "v_made", "v_ready", "softened", "exped", "totalled", "recip_done", "normed"))
        p_turned, p_out, o_made, o_out, x_made, x_out, rows_done = (
            sem(x) for x in ("p_turned", "p_out", "o_made", "o_out", "x_made", "x_out", "rows_done"))
        block = ctx.enter_context(nc.Block())
        names = ("attn1_ln_w", "attn1_ln_b")
        loads = 16 * 6

        @block.sync
        def _(sp):
            sp.dma_start(w_in[:, :], a["in_proj_t"]).then_inc(loaded, 16)
            sp.dma_start(b_in[:, :], a["in_proj_b"]).then_inc(loaded, 16)
            sp.dma_start(w_out[:, :], a["out_proj_t"]).then_inc(loaded, 16)
            sp.dma_start(out_bias[:, :], a["out_proj_b"].broadcast_to([P, D])).then_inc(loaded, 16)
            load_columns(sp, a, names, cols, loaded)

        @block.gpsimd
        def _(pool):
            nc.gpsimd.memset(of_a[:, :], 1.0).then_inc(made, 1)
            pool.wait_ge(made, 1)
            nc.gpsimd.affine_select(out=of_a[:, :], in_=of_a[:, :], compare_op=ALU.is_ge, fill=0.0, base=0,
                                    pattern=[[-P // HB, HB]], channel_multiplier=1).then_inc(made, 1)
            pool.wait_ge(made, 2)
            nc.gpsimd.affine_select(out=of_a[:, :], in_=of_a[:, :], compare_op=ALU.is_ge, fill=0.0, base=P // HB - 1,
                                    pattern=[[P // HB, HB]], channel_multiplier=-1).then_inc(made, 1)
            work = of_head[:, :, :]
            nc.gpsimd.memset(work, 1.0).then_inc(made, 1)
            pool.wait_ge(made, 4)
            nc.gpsimd.affine_select(out=work, in_=work, compare_op=ALU.is_ge, fill=0.0, base=0,
                                    pattern=[[-HB * HD, HB], [-HD, HB]], channel_multiplier=1).then_inc(made, 1)
            pool.wait_ge(made, 5)
            nc.gpsimd.affine_select(out=work, in_=work, compare_op=ALU.is_ge, fill=0.0, base=HD - 1,
                                    pattern=[[HB * HD, HB], [HD, HB]], channel_multiplier=-1).then_inc(made, 1)
            nc.gpsimd.memset(column_a[:, :, :], 1.0).then_inc(made, 1)
            pool.wait_ge(made, 7)
            col = column_a[:, :, :].rearrange("p (x y) d -> p x (y d)", x=HB)
            nc.gpsimd.affine_select(out=col, in_=col, compare_op=ALU.is_ge, fill=0.0, base=0,
                                    pattern=[[-P // HB, HB], [0, P // HB]], channel_multiplier=1).then_inc(made, 1)
            pool.wait_ge(made, 8)
            nc.gpsimd.affine_select(out=col, in_=col, compare_op=ALU.is_ge, fill=0.0, base=P // HB - 1,
                                    pattern=[[P // HB, HB], [0, P // HB]], channel_multiplier=-1).then_inc(made, 1)
            nc.gpsimd.memset(causal_f[:, :], 0.0).then_inc(made, 1)
            pool.wait_ge(made, 10)
            for b in range(HB):
                s = nc.gpsimd.affine_select(out=causal_f[b * B:(b + 1) * B, :], in_=causal_f[b * B:(b + 1) * B, :],
                                            compare_op=ALU.is_ge, fill=-BIG, base=0, pattern=[[0, NPG * HB], [-1, B]],
                                            channel_multiplier=1)
            s.then_inc(made, 1)

            def normalise_probs(g, u):
                pool.wait_ge(recip_done, g + 1)
                nc.gpsimd.tensor_tensor(prob[u][:, :, :], e_x[u][:, :, :], bcast(recip[u][:, :], B), ALU.mult
                                        ).then_inc(normed, 1)

            def spread(f, v):
                pool.wait_ge(hn_ready, f + 1)
                pool.sem_inc(c.pool_passed, 1)
                pool.wait_ge(made, 11)
                rows = hn[v][:, :].rearrange("p (n s) -> p n s", s=B).unsqueeze(2).broadcast_to([P, SLOTS * NPG, HB, B])
                nc.gpsimd.tensor_copy(hn_blocks[v][:, :, :, :], rows).then_inc(hn_spread, 1)

            def step(f, v, first=False, last=False):
                for s in range(SLOTS):
                    g = SLOTS * f + s
                    if not first or s >= 2:
                        pool.wait_ge(p_turned, g - 1)
                    normalise_probs(g, s % 2)
                    if s == 1 and not last:
                        spread(f + 1, 1 - v)

            spread(0, 0)
            step(0, 0, first=True)
            with pool.Fori(0, (STEPS - 2) // 2) as i:
                step(2 * i + 1, 1)
                step(2 * i + 2, 0)
            step(STEPS - 1, 1, last=True)

        def positions(ap, s):
            return ap[:, s * P:(s + 1) * P]

        @block.tensor
        def _(pe):
            pe.wait_ge(loaded, loads)
            nc.tensor.matmul(x_bank[:, 0:D], b_in[:, 2:3].broadcast_to([P, P]), w_out[:, :], start=True, stop=True
                             ).then_inc(folded, 1)
            pe.wait_ge(folded, 4)

            def turn(f):
                pe.wait_ge(z_ready, f + 1)
                for s in range(SLOTS):
                    mm = nc.tensor.transpose(positions(turn_bank, s), z[:, s, :], c.ident[:, :])
                mm.then_inc(turned, 1)

            def project(f, v):
                pe.wait_ge(hn_ready, f + 1)
                pe.wait_ge(q_ready, f)
                nc.tensor.matmul(q_bank[:, :], w_in[:, 0:D], hn[v][:, :], start=True, stop=True).then_inc(q_made, 1)
                pe.wait_ge(k_ready, f)
                nc.tensor.matmul(k_bank[:, :], w_in[:, D:2 * D], hn[v][:, :], start=True, stop=True).then_inc(k_made, 1)

            def scores(g, s, v):
                pe.wait_ge(softened, soft.before(g))
                nc.tensor.matmul(s_bank[:, :], ident_bf[:, :], causal[:, :], start=True, stop=False)
                for n in range(NPG):
                    q, k = (x[v][:, s * NPG + n, :, :].rearrange("p h s -> p (h s)") for x in (q_blocks, k_blocks))
                    mm = nc.tensor.matmul(s_bank[:, n * P:(n + 1) * P], q, k, start=False, stop=n == NPG - 1)
                mm.then_inc(s_made, 1)

            def value(g, s, v):
                pe.wait_ge(v_ready, g)
                for n in range(NPG):
                    rows = hn_blocks[v][:, s * NPG + n, :, :].rearrange("p h s -> p (h s)")
                    mm = nc.tensor.matmul(v_bank[:, n * D:(n + 1) * D], rows, w_in[:, 2 * D:],
                                          start=True, stop=True)
                mm.then_inc(v_made, 1)

            def turn_probs(g, u):
                pe.wait_ge(normed, g + 1)
                pe.wait_ge(p_out, g)
                flat_p = prob[u][:, :, :].rearrange("p h s -> p (h s)")
                for n in range(NPG):
                    mm = nc.tensor.transpose(p_bank[:, n * P:(n + 1) * P], flat_p[:, n * P:(n + 1) * P], c.ident[:, :])
                mm.then_inc(p_turned, 1)

            def mix(g, s):
                pe.wait_ge(p_out, g + 1)
                pe.wait_ge(o_out, g)
                for n in range(NPG):
                    mm = nc.tensor.matmul(o_bank[:, n * P:(n + 1) * P], v_blocks[s][:, n, :], prob_t[:, n * P:(n + 1) * P],
                                          start=True, stop=True)
                mm.then_inc(o_made, 1)

            def output(g):
                pe.wait_ge(o_out, g + 1)
                pe.wait_ge(x_out, g)
                for b in range(HB):
                    mm = nc.tensor.matmul(x_bank[:, 0:D], out_t[:, b, :, :].rearrange("p n s -> p (n s)"), w_out_b[:, b, :],
                                          start=b == 0, stop=b == HB - 1)
                mm.then_inc(x_made, 1)

            def step(f, v, first=False, last=False):
                for s in range(SLOTS):
                    g = SLOTS * f + s
                    back = not first or s >= 2
                    if back:
                        turn_probs(g - 2, s % 2)
                    if s == 0:
                        pe.wait_ge(q_ready, f + 1)
                        pe.wait_ge(k_ready, f + 1)
                        pe.wait_ge(hn_spread, f + 1)
                    scores(g, s, v)
                    value(g, s, v)
                    if not last:
                        if s == 1:
                            turn(f + 1)
                        if s == 2:
                            project(f + 1, 1 - v)
                    if back:
                        mix(g - 2, (s - 2) % SLOTS)
                    if not first or s >= 3:
                        output(g - 3)

            turn(0)
            project(0, 0)
            step(0, 0, first=True)
            with pe.Fori(0, (STEPS - 2) // 2) as i:
                step(2 * i + 1, 1)
                step(2 * i + 2, 0)
            step(STEPS - 1, 1, last=True)
            for s in range(2):
                turn_probs(NT - 2 + s, s)
                mix(NT - 2 + s, SLOTS - 2 + s)
                output(NT - 3 + s)
            output(NT - 1)

        @block.scalar
        def _(act):
            act.wait_ge(loaded, loads)
            act.wait_ge(folded, 3)

            def affine(f, v):
                act.wait_ge(turned, f + 1)
                nc.scalar.activation(hn[v][:, :], turn_bank[:, :], ACT.Identity, bias=cols[:, 1:2], scale=cols[:, 0:1]
                                     ).then_inc(hn_ready, 1)

            def place_queries(f, v):
                act.wait_ge(q_made, f + 1)
                for b in range(HB):
                    e = nc.scalar.activation(q_blocks[v][:, :, b, :], q_bank[:, :].rearrange("p (n s) -> p n s", s=B),
                                             ACT.Identity, bias=q_shift[:, b:b + 1], scale=of_b[:, b:b + 1])
                e.then_inc(q_ready, 1)

            def probs_out(g):
                act.wait_ge(p_turned, g + 1)
                act.wait_ge(o_made, g)
                nc.scalar.copy(prob_t[:, :], p_bank[:, :]).then_inc(p_out, 1)

            def exponents(g, u):
                act.wait_ge(softened, soft(g, "centred"))
                nc.scalar.activation(e_x[u][:, :, :], centred[u][:, :, :], ACT.Exp, scale=SM_SCALE).then_inc(exped, 1)

            def outputs_out(g):
                act.wait_ge(o_made, g + 1)
                act.wait_ge(x_made, g)
                nc.scalar.copy(out_t[:, :, :, :], o_bank[:, :].rearrange("p (n h s) -> p h n s", n=NPG, h=HB)
                               ).then_inc(o_out, 1)

            def step(f, v, first=False, last=False):
                for s in range(SLOTS):
                    g = SLOTS * f + s
                    back = not first or s >= 2
                    if back:
                        probs_out(g - 2)
                        act.wait_ge(normed, g - 1)
                    exponents(g, s % 2)
                    if not last:
                        if s == 1:
                            affine(f + 1, 1 - v)
                        if s == 2:
                            place_queries(f + 1, 1 - v)
                    if back:
                        outputs_out(g - 2)

            affine(0, 0)
            place_queries(0, 0)
            step(0, 0, first=True)
            with act.Fori(0, (STEPS - 2) // 2) as i:
                step(2 * i + 1, 1)
                step(2 * i + 2, 0)
            step(STEPS - 1, 1, last=True)
            for s in range(2):
                probs_out(NT - 2 + s)
                outputs_out(NT - 2 + s)

        @block.vector
        def _(dve):
            dve.wait_ge(made, 11)
            nc.vector.tensor_reduce(of_b[:, :], of_head[:, :, :].rearrange("p x y -> p y x"), AX.X, ALU.add).then_inc(folded, 1)
            nc.vector.tensor_copy(causal[:, :], causal_f[:, :])
            nc.vector.tensor_copy(ident_bf[:, :], c.ident[:, :])
            dve.wait_ge(loaded, loads)
            dve.wait_ge(folded, 2)
            nc.vector.tensor_tensor(row_bias[:, :], x_bank[:, 0:D], out_bias[:, :], ALU.add)
            for b in range(HB):
                nc.vector.tensor_scalar(w_out_b[:, b, :], w_out[:, :], of_b[:, b:b + 1], None, ALU.mult)
            nc.vector.tensor_scalar(q_shift[:, :], of_b[:, :], b_in[:, 0:1], None, ALU.mult).then_inc(folded, 1)
            nc.vector.tensor_scalar(k_shift[:, :], of_a[:, :], b_in[:, 1:2], None, ALU.mult).then_inc(folded, 1)
            dve.wait_ge(folded, 4)

            def prepare(f):
                for s in range(SLOTS):
                    at = SLOTS * f + s
                    m = nc.vector.tensor_scalar(z[:, s, :], flat(c.rows[:, bass.ds(at, 1), :]), mean[:, bass.ds(at, 1)],
                                                rstd[:, bass.ds(at, 1)], ALU.subtract, ALU.mult)
                m.then_inc(z_ready, 1)

            def place_keys(f, v):
                dve.wait_ge(k_made, f + 1)
                for h in range(HB):
                    m = nc.vector.tensor_scalar(k_blocks[v][:, :, h, :], k_bank[:, :].rearrange("p (n s) -> p n s", s=B),
                                                of_a[:, h:h + 1], k_shift[:, h:h + 1], ALU.mult, ALU.add)
                m.then_inc(k_ready, 1)

            def sums(g, u):
                dve.wait_ge(exped, g + 1)
                nc.vector.tensor_reduce(total[:, :], e_x[u][:, :, :], AX.X, ALU.add).then_inc(totalled, 1)
                dve.wait_ge(totalled, g + 1)
                nc.vector.reciprocal(recip[u][:, :], total[:, :]).then_inc(recip_done, 1)

            def soften(g, u):
                dve.wait_ge(s_made, g + 1)
                s_view = s_bank[:, :].rearrange("p (h s) -> p h s", s=B)
                nc.vector.tensor_reduce(peak[:, :], s_view, AX.X, ALU.max).then_inc(softened, 1)
                dve.wait_ge(softened, soft(g, "peak"))
                nc.vector.tensor_tensor(centred[u][:, :, :], s_view, bcast(peak[:, :], B), ALU.subtract).then_inc(softened, 1)

            def place_values(g, s):
                dve.wait_ge(v_made, g + 1)
                nc.vector.tensor_tensor(v_blocks[s][:, :, :], v_bank[:, :].rearrange("p (n d) -> p n d", d=D),
                                        along(column_a[:, :, :].rearrange("p h d -> p (h d)"), NPG), ALU.mult
                                        ).then_inc(v_ready, 1)

            def add(g):
                dve.wait_ge(x_made, g + 1)
                dve.wait_ge(rows_done, g)
                nc.vector.tensor_tensor(fresh[:, :], x_bank[:, 0:D], row_bias[:, :], ALU.add).then_inc(x_out, 1)
                dve.wait_ge(x_out, g + 1)
                row = flat(c.rows[:, bass.ds(g, 1), :])
                nc.vector.tensor_tensor(row, row, fresh[:, :], ALU.add).then_inc(rows_done, 1)

            def step(f, v, first=False, last=False):
                for s in range(SLOTS):
                    g = SLOTS * f + s
                    if not first or s >= 1:
                        sums(g - 1, (s - 1) % 2)
                    soften(g, s % 2)
                    place_values(g, s)
                    if not last:
                        if s == 0:
                            dve.wait_ge(turned, f + 1)
                            prepare(f + 1)
                        if s == 3:
                            place_keys(f + 1, 1 - v)
                    if not first or s >= 3:
                        add(g - 3)

            prepare(0)
            place_keys(0, 0)
            step(0, 0, first=True)
            with dve.Fori(0, (STEPS - 2) // 2) as i:
                step(2 * i + 1, 1)
                step(2 * i + 2, 0)
            step(STEPS - 1, 1, last=True)
            sums(NT - 1, 1)
            for s in range(3):
                add(NT - 3 + s)


def build(nc, a, out):
    with ExitStack() as ctx:
        c = Core(nc, ctx, a)
        setup(nc, c)
        with nc.sbuf_tensor("values", [P, NT, NH, HD + 1], F32) as values:
            project_heads(nc, c, values)
            attend_relative(nc, c, values)
        with ExitStack() as first:
            ex = Experts(nc, first, "moe0", 14, a["w1_0"], a["w2_0"])
            load_experts(nc, c, ex, a["rms_w_t"], None)
            send_to_experts(nc, c, ex, True)
            run_experts(nc, c, ex, ACT.Silu, False)
            combine(nc, c, ex, None, None)
        recur(nc, c)
        load_groups(nc, c.rows, c.x3, "groups_in")
        with nc.sbuf_tensor("attend1_mean", [P, NT], F32) as mean, nc.sbuf_tensor("attend1_rstd", [P, NT], F32) as rstd:
            row_stats(nc, c, "attend1", c.rows, mean[:, :], rstd[:, :], LN_EPS)
            attend_batches(nc, c, mean, rstd)
        with ExitStack() as second:
            ex = Experts(nc, second, "moe1", 8, a["w1_1"], a["w2_1"])
            residual = second.enter_context(nc.sbuf_tensor("residual", [P, NT, D], F32))
            load_groups(nc, residual, c.x3, "residual_in")
            load_experts(nc, c, ex, a["ln2_w"], a["ln2_b"])
            send_to_experts(nc, c, ex, False)
            run_experts(nc, c, ex, ACT.Gelu, True)
            combine(nc, c, ex, residual, out)


def kernel(**inputs):
    import numpy as _np
    import concourse.bacc as _bacc
    from concourse import mybir as _mybir
    from concourse.bass_utils import run_bass_kernel_spmd as _run

    nc = _bacc.Bacc("TRN2", target_bir_lowering=False, num_devices=1)
    take = lambda name: _np.asarray(inputs[name])
    column = lambda name: take(name)[:, None]
    laid_out = {
        "x": take("L0_attn_x"), "x_t": take("L0_attn_x").reshape(TOK, D).T,
        "wq_t": take("L0_attn_Wq").T, "wk_t": take("L0_attn_Wk").T, "wv_t": take("L0_attn_Wv").T,
        "wp_t": take("L0_attn_Wp").T, "bp": take("L0_attn_bp")[None], "rel_t": take("L0_attn_rel_embed").T,
        "router0": take("L0_ffn_router_w"), "rms_w_t": take("L0_ffn_rms_w").T, "w1_0": take("L0_ffn_w1"),
        "w2_0": take("L0_ffn_w2"), "rms_w_s_t": take("L0_ffn_rms_w_s").T, "w1_s": take("L0_ffn_w1_s"),
        "w2_s": take("L0_ffn_w2_s"),
        "rwkv_ln1_g": column("L1_attn_ln1_g"), "rwkv_ln1_b": column("L1_attn_ln1_b"),
        "rwkv_wk": take("L1_attn_Wk"), "rwkv_wv": take("L1_attn_Wv"), "rwkv_wr": take("L1_attn_Wr"),
        "rwkv_wo": take("L1_attn_Wo"), "time_decay": column("L1_attn_time_decay"),
        "time_first": column("L1_attn_time_first"), "mix_k": column("L1_attn_mix_k"),
        "mix_v": column("L1_attn_mix_v"), "mix_r": column("L1_attn_mix_r"),
        "rwkv_ln2_g": column("L1_attn_ln2_g"), "rwkv_ln2_b": column("L1_attn_ln2_b"),
        "rwkv_wfk": take("L1_attn_Wfk"), "rwkv_wfv": take("L1_attn_Wfv"), "rwkv_wfr": take("L1_attn_Wfr"),
        "attn1_ln_w": column("L1_ffn_ln1_w"), "attn1_ln_b": column("L1_ffn_ln1_b"),
        "in_proj_t": take("L1_ffn_in_proj_w").T, "in_proj_b": take("L1_ffn_in_proj_b").reshape(3, D).T,
        "out_proj_t": take("L1_ffn_out_proj_w").T, "out_proj_b": take("L1_ffn_out_proj_b")[None],
        "ln2_w": column("L1_ffn_ln2_w"), "ln2_b": column("L1_ffn_ln2_b"), "router1_t": take("L1_ffn_router_w").T,
        "w1_1": take("L1_ffn_w1"), "w2_1": take("L1_ffn_w2"),
    }
    arrays = {f"in_{name}": _np.ascontiguousarray(x) for name, x in laid_out.items()}
    a = {name: nc.dram_tensor(f"in_{name}", x.shape, _mybir.dt.from_np(x.dtype), kind="ExternalInput").ap()
         for name, x in laid_out.items()}
    out = nc.dram_tensor("out_0", (B, T, D), F32, kind="ExternalOutput").ap()
    build(nc, a, out)
    r = _run(nc, [arrays], core_ids=[0])
    return r.results[0]["out_0"]
```

```python
from contextlib import ExitStack

import concourse.bass as bass
from concourse import mybir

ALU = mybir.AluOpType
ACT = mybir.ActivationFunctionType
AX = mybir.AxisListType
F32 = mybir.dt.float32
BF16 = mybir.dt.bfloat16
I32 = mybir.dt.int32

P = 128
B, T, D = 32, 256, 128
TOK = B * T
BLK = T // P
NPG = P // B
NT = TOK // P
NH, HD = 16, 8
W = P + T
QUAD = 4
NQ = NH // QUAD
NPART = 8
BIG = 1.0e30
LN_EPS = 1e-5
SM_SCALE = HD ** -0.5


def bcast(ap, n):
    return ap.unsqueeze(2).broadcast_to([ap.shape[0], ap.shape[1], n])


def scope(nc, ctx, tag):
    def sb(name, shape, dt=F32):
        return ctx.enter_context(nc.sbuf_tensor(f"{tag}_{name}", shape, dt))

    def psum(name):
        return ctx.enter_context(nc.psum_tensor(f"{tag}_{name}", [P, 512], F32))

    numbers = []

    def sem(name):
        handle = ctx.enter_context(nc.semaphore(f"{tag}_{name}"))
        numbers.append(handle.num)
        return handle

    def clear(failed, *_):
        runs = []
        for number in sorted(numbers):
            if runs and number == runs[-1].stop:
                runs[-1] = range(runs[-1].start, number + 1)
            else:
                runs.append(range(number, number + 1))
        if runs and not failed:
            with nc.Block() as block:
                @block.sync
                def _(sp):
                    for run in runs:
                        sp.sem_clear(run)

    ctx.push(clear)
    return sb, psum, sem


class Core:

    def __init__(self, nc, ctx, a):
        self.nc, self.a = nc, a
        sb = lambda name, shape, dt=F32: ctx.enter_context(nc.sbuf_tensor(name, shape, dt))
        dr = lambda name, shape, dt=F32: nc.dram_tensor(name, shape, dt, kind="Internal").ap()
        self.ident = sb("ident", [P, P])
        self.neg_half = sb("neg_half", [P, 2])
        self.rows = sb("rows", [P, NT, D])
        self.q_stack = dr("q_stack", [B + 1, D * NPART, T], BF16)
        self.k_stack = dr("k_stack", [B + 1, D * NPART, T], BF16)
        self.e_stack = dr("e_stack", [D * NPART, T], BF16)
        self.expert_in = dr("expert_in", [SLOT_TILES * P, D])
        self.expert_out = dr("expert_out", [SLOT_TILES * P, D])
        self.x3 = dr("x3", [B, T, D])
        self.zeros = sb("zeros", [P, D])
        self.vector_passed, self.pool_passed, self.sync_passed = (
            ctx.enter_context(nc.semaphore(x)) for x in ("vector_passed", "pool_passed", "sync_passed"))
        self.indirect = {phase: [ctx.enter_context(nc.semaphore(f"{phase}{u}")) for u in range(2)]
                         for phase in ("moe0_sent", "moe0_gathered", "moe1_sent", "moe1_gathered")}
        self.cleared = ctx.enter_context(nc.semaphore("cleared"))
        self.shear = dr("shear", [NQ, P, QUAD, W + 2 * P])


def setup(nc, c):
    with ExitStack() as ctx:
        sb, psum, sem = scope(nc, ctx, "setup")
        pads = sb("pads", [P, QUAD, P])
        zeros = sb("zeros", [P, NPART * T], BF16)
        filled, diagonal, written = sem("filled"), sem("diagonal"), sem("pads_written")
        block = ctx.enter_context(nc.Block())

        @block.gpsimd
        def _(pool):
            nc.gpsimd.memset(c.ident[:, :], 0.0).then_inc(filled, 1)
            nc.gpsimd.memset(c.neg_half[:, :], -0.5)
            pool.wait_ge(filled, 1)
            nc.gpsimd.affine_select(out=c.ident[:, :], in_=c.ident[:, :], compare_op=ALU.not_equal,
                                    fill=1.0, base=0, pattern=[[-1, P]], channel_multiplier=1)

        @block.vector
        def _(dve):
            nc.vector.memset(pads[:, :, 0:1], 0.0).then_inc(diagonal, 1)
            nc.vector.memset(pads[:, :, 1:], -BIG).then_inc(diagonal, 1)
            nc.vector.memset(zeros[:, :], 0.0).then_inc(diagonal, 1)
            nc.vector.memset(c.zeros[:, :], 0.0).then_inc(diagonal, 1)

        @block.scalar
        def _(act):
            act.wait_ge(written, 16 * (2 * NQ + 2))
            act.dma_start(c.expert_in.rearrange("(p s) d -> p s d", p=P), c.zeros[:, :].unsqueeze(1).broadcast_to(
                [P, SLOT_TILES, D])).then_inc(c.cleared, 16)

        @block.sync
        def _(sp):
            sp.wait_ge(diagonal, 4)
            for slot in range(NQ):
                sp.dma_start(c.shear[slot, :, :, P:2 * P], pads[:, :, :]).then_inc(written, 16)
                sp.dma_start(c.shear[slot, :, :, W + P:], pads[:, :, :]).then_inc(written, 16)
            for stack in (c.q_stack, c.k_stack):
                sp.dma_start(stack[B].rearrange("(p s) t -> p (s t)", p=P), zeros[:, :]).then_inc(written, 16)
            sp.wait_ge(written, 16 * (2 * NQ + 2))


def write_stack(sp, dst, parts, in_q, done):
    rows = dst.rearrange("(c s) t -> c s t", s=NPART)
    for j, (a, b) in enumerate(((0, 3), (3, 6), (6, 8))):
        src = parts[:, j:j + 1, :].broadcast_to([P, b - a, T]) if in_q else parts[:, 0:b - a, :]
        sp.dma_start(rows[:, a:b, :], src).then_inc(done, 16)


def project_heads(nc, c, values):
    a = c.a
    with ExitStack() as ctx:
        sb, psum, sem = scope(nc, ctx, "project")
        wq, wk, wv = (sb(n, [P, D]) for n in ("w_query", "w_key", "w_value"))
        rel = sb("rel_embed", [P, T])
        xt = [sb(f"xt{u}", [P, T]) for u in range(2)]
        parts = [[sb(f"parts_{n}{u}", [P, 3, T], BF16) for n in "qk"] for u in range(2)]
        rest = [[sb(f"rest_{n}{u}", [P, T]) for n in "qk"] for u in range(2)]
        rel_parts, rel_rest = sb("rel_parts", [P, 3, T], BF16), sb("rel_rest", [P, T])
        ps = [[psum(f"{n}{u}") for n in "qkv"] for u in range(2)]
        weights_in, x_in = sem("weights_in"), [sem(f"x_in{u}") for u in range(2)]
        projected, high, rest_done, mid, low = (sem(n) for n in ("projected", "high", "rest_done", "mid", "low"))
        rel_done, stacked = sem("rel_done"), [sem(f"stacked{u}") for u in range(2)]
        rel_stacked, ones_set, values_out = sem("rel_stacked"), sem("ones_set"), sem("values_out")
        block = ctx.enter_context(nc.Block())
        NI = B // 2

        @block.sync
        def _(sp):
            for w, name in ((wq, "wq_t"), (wk, "wk_t"), (wv, "wv_t"), (rel, "rel_t")):
                sp.dma_start(w[:, :], a[name]).then_inc(weights_in, 16)
            for u in range(2):
                sp.dma_start(xt[u][:, :], a["x_t"][:, u * T:(u + 1) * T]).then_inc(x_in[u], 16)
            sp.wait_ge(low, 1)
            write_stack(sp, c.e_stack, rel_parts, False, rel_stacked)

            def store(i, last=False):
                for u in range(2):
                    if not last:
                        sp.wait_ge(projected, 6 * i + 3 * u + 3)
                        sp.dma_start(xt[u][:, :], a["x_t"][:, bass.ds((2 * i + u + 2) * T, T)]).then_inc(x_in[u], 16)
                    sp.wait_ge(low, 4 * i + 2 * u + 3)
                    for n, stack in enumerate((c.q_stack, c.k_stack)):
                        dst = stack[bass.ds(2 * i + u, 1)].rearrange("o r t -> (o r) t")
                        write_stack(sp, dst, parts[u][n], n == 0, stacked[u])

            with sp.Fori(0, NI - 1) as i:
                store(i)
            store(NI - 1, last=True)
            for u in range(2):
                sp.wait_ge(x_in[u], 16 * NI)
                sp.wait_ge(stacked[u], 96 * NI)
            sp.wait_ge(rel_stacked, 48)

        @block.tensor
        def _(pe):
            pe.wait_ge(weights_in, 64)
            with pe.Fori(0, NI) as i:
                for u in range(2):
                    pe.wait_ge(x_in[u], 16 * i + 16)
                    pe.wait_ge(rest_done, 4 * i + 1)
                    nc.tensor.matmul(ps[u][0][:, 0:T], wq[:, :], xt[u][:, :], start=True, stop=True).then_inc(projected, 1)
                    nc.tensor.matmul(ps[u][1][:, 0:T], wk[:, :], xt[u][:, :], start=True, stop=True).then_inc(projected, 1)
                    pe.wait_ge(values_out, 2 * i + u)
                    for j in range(BLK):
                        mm = nc.tensor.matmul(ps[u][2][:, j * D:(j + 1) * D], xt[u][:, j * P:(j + 1) * P], wv[:, :],
                                              start=True, stop=True)
                    mm.then_inc(projected, 1)

        @block.scalar
        def _(act):
            act.wait_ge(ones_set, 1)
            with act.Fori(0, NI) as i:
                for u in range(2):
                    act.wait_ge(stacked[u], 96 * i)
                    for n in range(2):
                        act.wait_ge(projected, 6 * i + 3 * u + n + 1)
                        nc.scalar.copy(parts[u][n][:, 0, :], ps[u][n][:, 0:T]).then_inc(high, 1)
                    act.wait_ge(projected, 6 * i + 3 * u + 3)
                    src = ps[u][2][:, 0:BLK * D].rearrange("p (j h d) -> p j h d", j=BLK, h=NH)
                    nc.scalar.copy(values[:, bass.ds((2 * i + u) * BLK, BLK), :, 0:HD], src).then_inc(values_out, 1)

        @block.vector
        def _(dve):
            nc.vector.memset(values[:, :, :, HD:HD + 1], 1.0).then_inc(ones_set, 1)
            dve.wait_ge(weights_in, 64)
            nc.vector.tensor_copy(rel_parts[:, 0, :], rel[:, :]).then_inc(rel_done, 1)
            dve.wait_ge(rel_done, 1)
            nc.vector.tensor_tensor(rel_rest[:, :], rel[:, :], rel_parts[:, 0, :], ALU.subtract).then_inc(rest_done, 1)
            dve.wait_ge(rest_done, 1)
            nc.vector.tensor_copy(rel_parts[:, 1, :], rel_rest[:, :]).then_inc(mid, 1)
            with dve.Fori(0, NI) as i:
                for u in range(2):
                    for n in range(2):
                        dve.wait_ge(high, 4 * i + 2 * u + n + 1)
                        dve.wait_ge(low, 4 * i + 1)
                        nc.vector.tensor_tensor(rest[u][n][:, :], ps[u][n][:, 0:T], parts[u][n][:, 0, :],
                                                ALU.subtract).then_inc(rest_done, 1)
                    for n in range(2):
                        dve.wait_ge(rest_done, 4 * i + 2 * u + n + 2)
                        nc.vector.tensor_copy(parts[u][n][:, 1, :], rest[u][n][:, :]).then_inc(mid, 1)

        @block.gpsimd
        def _(pool):
            pool.wait_ge(mid, 1)
            nc.gpsimd.tensor_tensor(rel_parts[:, 2, :], rel_rest[:, :], rel_parts[:, 1, :], ALU.subtract).then_inc(low, 1)
            with pool.Fori(0, NI) as i:
                for u in range(2):
                    for n in range(2):
                        pool.wait_ge(mid, 4 * i + 2 * u + n + 2)
                        nc.gpsimd.tensor_tensor(parts[u][n][:, 2, :], rest[u][n][:, :], parts[u][n][:, 1, :],
                                                ALU.subtract).then_inc(low, 1)


def wait_past(eng, sem, value):
    if not isinstance(value, int) or value > 0:
        eng.wait_ge(sem, value)


def attend_relative(nc, c, values):
    a = c.a
    REL, LOAD, SLOTS, RING = NQ, NQ + 2, 2 * NQ, 4
    EXTRA = {4: "out2", 5: "out3", 7: "heads", 9: "project", 12: "out0", 13: "out1"}
    order = []
    for h in range(NH):
        order += [h] + ([EXTRA[h]] if h in EXTRA else [])
    ITEMS = len(order)
    absent = (0, 1, "out2", "out3", "heads", "project")
    MV = 32
    with ExitStack() as ctx:
        sb, psum, sem = scope(nc, ctx, "attend")
        wp, bias = sb("w_out", [P, D]), sb("b_out", [P, D])
        q_st = sb("q_heads", [P, SLOTS, 2, 2 + T], BF16)
        k_st = sb("k_heads", [P, SLOTS, 2, T], BF16)
        e_st = sb("e_heads", [P, NH // 2, T], BF16)
        raw = sb("raw_relative", [P, 2, QUAD, W])
        rel = sb("relative", [P, NQ, QUAD, W])
        score, prob, prob_t = (sb(n, [P, RING, W]) for n in ("score", "prob", "prob_t"))
        least = sb("least", [P, RING, BLK])
        x_in_sb = sb("x_rows", [P, BLK, D])
        xb = sb("x_plus_bias", [P, BLK, D])
        recip = sb("recip", [P, BLK, QUAD])
        v_now = [sb(f"values_now{v}", [P, BLK, NH, MV]) for v in range(2)]
        outs = sb("outs", [P, NQ, T])
        heads, heads_t = sb("heads", [P, BLK, NH, HD]), sb("heads_t", [P, T])
        y = sb("y", [P, BLK, D])
        stats, moments = sb("stats", [P, BLK, 6]), sb("moments", [P, BLK, 2])
        shifted, rstd = sb("shifted", [P, BLK]), sb("rstd", [P, BLK])
        e_bank, s_bank, t_bank, o_bank = ([psum(f"{n}{j}") for j in range(2)]
                                          for n in ("rel_bank", "score_bank", "turn_bank", "out_bank"))

        consts_in, x_in, first_set = sem("consts_in"), sem("x_in"), sem("first_set")
        q_in, k_in = ([sem(f"{n}_in{s}") for s in range(SLOTS)] for n in "qk")
        sheared_out, sheared_in = ([sem(f"sheared_{n}{s}") for s in range(NQ)] for n in ("out", "in"))
        rel_made, rel_moved, qk_made, summed, exped, pv_done = (
            sem(n) for n in ("rel_made", "rel_moved", "qk_made", "summed", "exped", "pv_done"))
        filled, drained, v_ready, outs_ready, recip_done, biased, zeroed = (
            sem(n) for n in ("filled", "drained", "v_ready", "outs_ready", "recip_done", "biased", "zeroed"))
        stats_done, moments_done, eps_added, rstd_done, rows_done = (
            sem(n) for n in ("stats_done", "moments_done", "eps_added", "rstd_done", "rows_done"))
        block = ctx.enter_context(nc.Block())

        def all_batches(eng, batch):
            batch(0, 0, True, False)
            with eng.Fori(0, B // 2 - 1) as i:
                batch(i, 1, False, False)
                batch(i + 1, 0, False, False)
            batch(B // 2 - 1, 1, False, True)

        def item(t, what):
            place = order.index(what)
            if isinstance(t, int) and t == 0:
                return place + 1 + sum(x in absent for x in order[place:])
            if isinstance(t, int) and t == B:
                return ITEMS * B + sum(x in absent for x in order[:place + 1])
            return ITEMS * t + place + 1

        def bank_of(what):
            return t_bank[order.index(what) % 2]

        def slot_of(v, quad, ahead):
            q = NQ * v + quad + ahead
            return q % SLOTS, q // SLOTS

        def load_stacks(sp, t, quad, slot):
            for stack, dst, done in ((c.q_stack, q_st[:, :, :, 2:], q_in), (c.k_stack, k_st, k_in)):
                rows = stack[bass.ds(t, 1)].rearrange("o (g r) t -> r (o g) t", r=P)
                sp.dma_start(dst[:, slot, :, :], rows[:, 2 * quad:2 * quad + 2, :]).then_inc(done[slot], 16)

        def write_shear(sp, slot):
            src, dst = raw[:, slot % 2, :, :], c.shear[slot]
            sp.dma_start(dst[:, :, 0:P], src[:, :, 0:P]).then_inc(sheared_out[slot], 16)
            sp.dma_start(dst[:, :, 2 * P:P + W], src[:, :, P:W]).then_inc(sheared_out[slot], 16)

        def read_shear(sp, slot):
            pitch = QUAD * (W + 2 * P)
            base = slot * P * pitch
            for off, lo, n in ((P, 0, P), (3 * P, P, T)):
                src = bass.AP(c.shear.tensor, base + off, [[pitch - 1, P], [W + 2 * P, QUAD], [1, n]])
                sp.dma_start(rel[:, slot, :, lo:lo + n], src).then_inc(sheared_in[slot], 16)

        @block.sync
        def _(sp):
            sp.dma_start(wp[:, :], a["wp_t"]).then_inc(consts_in, 16)
            sp.dma_start(bias[:, :], a["bp"].broadcast_to([P, D])).then_inc(consts_in, 16)
            sp.dma_start(e_st[:, :, :], c.e_stack.rearrange("(g r) t -> r g t", r=P)).then_inc(consts_in, 16)
            for quad in range(LOAD):
                load_stacks(sp, quad // NQ, quad % NQ, quad)
            for quad in range(REL):
                sp.wait_ge(rel_moved, QUAD * (quad + 1))
                write_shear(sp, quad)
                if quad:
                    sp.wait_ge(sheared_out[quad - 1], 32)
                    read_shear(sp, quad - 1)

            def batch(j, v, first, last):
                t = 2 * j + v
                wait_past(sp, biased, t)
                sp.dma_start(x_in_sb[:, :, :], a["x"][bass.ds(t, 1)].rearrange("o (j p) d -> p (o j) d", p=P)
                             ).then_inc(x_in, 16)
                for quad in range(NQ):
                    if not last:
                        wait_past(sp, qk_made, 16 * t + QUAD * quad)
                        slot, _ = slot_of(v, quad, LOAD)
                        load_stacks(sp, t + (quad + LOAD) // NQ, slot % NQ, slot)
                        sp.wait_ge(sheared_in[quad], 32 * t + 32)
                        sp.sem_inc(c.sync_passed, 1)
                        sp.wait_ge(rel_moved, 16 * t + QUAD * (quad + REL + 1))
                        sp.sem_inc(c.sync_passed, 1)
                        write_shear(sp, quad)
                    if quad == 0 or not last:
                        before = (quad - 1) % NQ
                        sp.wait_ge(sheared_out[before], 32 * (t + (quad > 0)) + 32)
                        if not (first and quad == 0):
                            sp.wait_ge(summed, 16 * t + QUAD * quad)
                            sp.sem_inc(c.sync_passed, 1)
                        read_shear(sp, before)

            all_batches(sp, batch)
            for slot in range(NQ):
                sp.wait_ge(sheared_in[slot], 32 * B)
            for slot in range(SLOTS):
                times = B // 2 + (slot < LOAD - NQ)
                sp.wait_ge(q_in[slot], 16 * times)
                sp.wait_ge(k_in[slot], 16 * times)

        @block.tensor
        def _(pe):
            pe.wait_ge(consts_in, 48)
            pe.wait_ge(first_set, 1)

            def relative(n, slot, h):
                wait_past(pe, rel_moved, n - 1)
                lo, q, e = 64 * (h % 2), q_st[:, slot, h // 2 % 2, 1:], e_st[:, h // 2, :]
                bank = e_bank[h % 2]
                nc.tensor.matmul(bank[:, 0:P], q[lo:lo + 64, 0:P], e[lo:lo + 64, P:T], start=True, stop=True)
                nc.tensor.matmul(bank[:, P:W], q[lo:lo + 64, P:T], e[lo:lo + 64, 0:T], start=True, stop=True
                                 ).then_inc(rel_made, 1)

            def scores(n, slot, h):
                wait_past(pe, summed, n - 1)
                lo, q, k = 64 * (h % 2), q_st[:, slot, h // 2 % 2, 2:], k_st[:, slot, h // 2 % 2, :]
                bank = s_bank[h % 2]
                nc.tensor.matmul(bank[:, 0:P], q[lo:lo + 64, 0:P], k[lo:lo + 64, 0:P], start=True, stop=True)
                nc.tensor.matmul(bank[:, P:W], q[lo:lo + 64, P:T], k[lo:lo + 64, 0:T], start=True, stop=True
                                 ).then_inc(qk_made, 1)

            def bank_free(t, what):
                alone = isinstance(t, int) and t in (0, B)
                wait_past(pe, drained, item(t, what) - (1 if alone else 2))

            def turn(n, h, t, at):
                bank_free(t, at)
                pe.wait_ge(exped, n + 1)
                bank = bank_of(at)
                for j in range(3):
                    mm = nc.tensor.transpose(bank[:, j * P:(j + 1) * P], prob[:, h % RING, j * P:(j + 1) * P], c.ident[:, :])
                mm.then_inc(filled, 1)

            def turn_outputs(t, quad, batch_of):
                what = f"out{quad}"
                bank_free(t, what)
                pe.wait_ge(outs_ready, 2 * batch_of + quad // 2 + 1)
                for j in range(BLK):
                    mm = nc.tensor.transpose(bank_of(what)[:, j * P:(j + 1) * P], outs[:, quad, j * P:(j + 1) * P], c.ident[:, :])
                mm.then_inc(filled, 1)

            def turn_heads(t):
                bank_free(t, "heads")
                pe.wait_ge(drained, item(t, "out3"))
                for j in range(BLK):
                    mm = nc.tensor.transpose(bank_of("heads")[:, j * P:(j + 1) * P],
                                             heads[:, j, :, :].rearrange("p h d -> p (h d)"), c.ident[:, :])
                mm.then_inc(filled, 1)

            def project(t):
                pe.wait_ge(drained, item(t, "heads"))
                bank_free(t, "project")
                for j in range(BLK):
                    mm = nc.tensor.matmul(bank_of("project")[:, j * D:(j + 1) * D], heads_t[:, j * P:(j + 1) * P], wp[:, :],
                                          start=True, stop=True)
                mm.then_inc(filled, 1)

            def extra(t, h):
                what = EXTRA.get(h)
                if what == "heads":
                    turn_heads(t)
                elif what == "project":
                    project(t)
                elif what:
                    quad = int(what[-1])
                    turn_outputs(t, quad, t if quad < 2 else t - 1)

            pe.sem_inc(filled, len(absent))
            for n in range(REL * QUAD):
                if n % QUAD == 0:
                    pe.wait_ge(q_in[n // QUAD], 16)
                relative(n, n // QUAD, n)

            def batch(j, v, first, last):
                t = 2 * j + v
                for h in range(NH):
                    n, quad = 16 * t + h, h // QUAD
                    here = slot_of(v, quad, 0)[0]
                    if not last:
                        ahead, more = slot_of(v, quad, REL)
                        if h % QUAD == 0:
                            pe.wait_ge(q_in[ahead], 16 * (j + more) + 16)
                        relative(n + REL * QUAD, ahead, h)
                    if h % QUAD == 0:
                        pe.wait_ge(k_in[here], 16 * j + 16)
                        pe.wait_ge(q_in[here], 16 * j + 16)
                    scores(n, here, h)
                    if not first or h >= 2:
                        turn(n - 2, (h - 2) % NH, t, h)
                    if not first or h >= 3:
                        mix(t, h, v)
                    if h in EXTRA and (not first or h > 9):
                        extra(t, h)

            def mix(t, h, v):
                m = (h - 3) % NH
                at = t - (h < 3)
                out_of = item(t, h - 1) if h else item(t - 1, NH - 1)
                pe.wait_ge(drained, out_of)
                if m == 0:
                    pe.wait_ge(v_ready, at + 1)
                if m % (NH // 2) == 0:
                    wait_past(pe, outs_ready, 2 * at + m // (NH // 2) - 1)
                lo, half = MV * (m % QUAD), m // QUAD % 2
                bank = o_bank[m // (NH // 2)]
                now = v_now[v if h >= 3 else 1 - v]
                pt = prob_t[:, m % RING, :]
                nc.tensor.matmul(bank[lo:lo + MV, half * T:(half + 1) * T], now[:, 0, m, :], pt[:, 0:T], start=True, stop=False)
                nc.tensor.matmul(bank[lo:lo + MV, half * T + P:(half + 1) * T], now[:, 1, m, :], pt[:, T:W],
                                 start=False, stop=True).then_inc(pv_done, 1)

            all_batches(pe, batch)
            for h in range(10):
                if h < 2:
                    turn(16 * B + h - 2, (h - 2) % NH, B, h)
                if h < 3:
                    mix(B, h, 0)
                if h in EXTRA:
                    extra(B, h)

        @block.scalar
        def _(act):
            def move_relative(n, half, h):
                act.wait_ge(rel_made, n + 1)
                nc.scalar.copy(raw[:, half, h % QUAD, :], e_bank[h % 2][:, 0:W]).then_inc(rel_moved, 1)

            def exponents(n, h, turned_before):
                act.wait_ge(summed, n + 1)
                wait_past(act, filled, turned_before)
                for j, (lo, hi) in enumerate(((0, P), (P, W))):
                    e = nc.scalar.activation(prob[:, h % RING, lo:hi], score[:, h % RING, lo:hi], ACT.Exp,
                                             bias=least[:, h % RING, j:j + 1], scale=-1.0)
                e.then_inc(exped, 1)

            def outputs_out(t, half, used):
                act.wait_ge(pv_done, 16 * t + 8 * half + 8)
                wait_past(act, filled, used)
                nc.scalar.copy(outs[:, 2 * half:2 * half + 2, :].rearrange("p q t -> p (q t)"), o_bank[half][:, :]
                               ).then_inc(outs_ready, 1)

            for n in range(REL * QUAD):
                quad = n // QUAD
                if quad >= 2 and n % QUAD == 0:
                    act.wait_ge(sheared_out[quad - 2], 32)
                move_relative(n, quad % 2, n)

            def batch(j, v, first, last):
                t = 2 * j + v
                for h in range(NH):
                    n, quad = 16 * t + h, h // QUAD
                    if not last:
                        if h % QUAD == 0:
                            two_before = (quad - 2) % NQ
                            act.wait_ge(sheared_out[two_before], 32 * (t + (quad >= 2)) + 32)
                        move_relative(n + REL * QUAD, quad % 2, h)
                    exponents(n, h, 0 if first and h < RING else item(t, h - 2) if h >= 2 else item(t - 1, NH - 2 + h))
                    if not first and h == 3:
                        outputs_out(t - 1, 1, item(t - 1, "out3"))
                    if h == 11:
                        outputs_out(t, 0, 0 if first else item(t - 1, "out1"))

            all_batches(act, batch)
            outputs_out(B - 1, 1, item(B - 1, "out3"))

        @block.vector
        def _(dve):
            nc.vector.memset(q_st[:, :, :, 0:2], 0.0).then_inc(first_set, 1)
            dve.sem_inc(drained, len(absent))

            def sum_scores(n, h, quad):
                dve.wait_ge(qk_made, n + 1)
                wait_past(dve, exped, n - 3)
                dve.sem_inc(c.vector_passed, 1)
                dve.wait_ge(sheared_in[0], 32)
                for j, (lo, hi) in enumerate(((0, P), (P, W))):
                    s = nc.vector.tensor_tensor_reduce(
                        score[:, h % RING, lo:hi], s_bank[h % 2][:, lo:hi], rel[:, quad, h % QUAD, lo:hi],
                        -SM_SCALE, 3.0e38, ALU.add, ALU.min, least[:, h % RING, j:j + 1])
                s.then_inc(summed, 1)

            def turn_out(n, h, t, at):
                dve.wait_ge(filled, item(t, at))
                wait_past(dve, pv_done, n - 3)
                nc.vector.tensor_copy(prob_t[:, h % RING, :], bank_of(at)[:, 0:W]).then_inc(drained, 1)

            def normalise_heads(t, quad, count):
                what = f"out{quad}"
                dve.wait_ge(filled, item(t, what))
                view = bank_of(what)[:, 0:T].rearrange("p (j h r) -> p j h r", j=BLK, h=QUAD)
                nc.vector.reciprocal(recip[:, :, :], view[:, :, :, HD]).then_inc(recip_done, 1)
                dve.wait_ge(recip_done, count + 1)
                for j in range(BLK):
                    m = nc.vector.tensor_tensor(heads[:, j, QUAD * quad:QUAD * (quad + 1), :], view[:, j, :, 0:HD],
                                                bcast(recip[:, j, :], HD), ALU.mult)
                m.then_inc(drained, 1)

            def extra(t, h):
                what = EXTRA.get(h)
                if what == "heads":
                    dve.wait_ge(filled, item(t, "heads"))
                    nc.vector.tensor_copy(heads_t[:, :], bank_of("heads")[:, 0:T]).then_inc(drained, 1)
                elif what == "project":
                    add_residual(t)
                elif what:
                    quad = int(what[-1])
                    normalise_heads(t, quad, NQ * (t - (quad >= 2)) + quad)

            def add_residual(t):
                dve.wait_ge(filled, item(t, "project"))
                dve.wait_ge(biased, t)
                wait_past(dve, rows_done, t - 1)
                nc.vector.tensor_tensor(y[:, :, :], bank_of("project")[:, 0:BLK * D].rearrange("p (j d) -> p j d", j=BLK),
                                        xb[:, :, :], ALU.add).then_inc(drained, 1)

            def statistics(t):
                dve.wait_ge(drained, item(t + 1, "project"))
                for j in range(BLK):
                    s = nc.vector.bn_stats(stats[:, j, :], y[:, j, :])
                s.then_inc(stats_done, 1)

            def aggregate(t):
                dve.wait_ge(stats_done, t + 1)
                dve.sem_inc(c.vector_passed, 1)
                dve.wait_ge(first_set, 1)
                for j in range(BLK):
                    s = nc.vector.bn_aggr(moments[:, j, :], stats[:, j, :])
                s.then_inc(moments_done, 1)

            def store_rows(t):
                dve.wait_ge(rstd_done, t + 1)
                for j in range(BLK):
                    s = nc.vector.tensor_scalar(c.rows[:, bass.ds(BLK * t + j, 1), :].rearrange("p o d -> p (o d)"), y[:, j, :],
                                                moments[:, j, 0:1], rstd[:, j:j + 1], ALU.subtract, ALU.mult)
                s.then_inc(rows_done, 1)

            def batch(j, v, first, last):
                t = 2 * j + v
                for h in range(NH):
                    n, quad = 16 * t + h, h // QUAD
                    if h % QUAD == 0:
                        dve.wait_ge(sheared_in[quad], 32 * t + 32)
                    sum_scores(n, h, quad)
                    if not first or h >= 2:
                        turn_out(n - 2, (h - 2) % NH, t, h)
                    if h in EXTRA and (not first or h > 9):
                        extra(t, h)
                    if not first and h == 10:
                        statistics(t - 1)
                    if not first and h == 11:
                        aggregate(t - 1)
                    if not first and h == 14:
                        store_rows(t - 1)

            all_batches(dve, batch)
            for h in range(10):
                if h < 2:
                    turn_out(16 * B + h - 2, (h - 2) % NH, B, h)
                if h in EXTRA:
                    extra(B, h)
            statistics(B - 1)
            aggregate(B - 1)
            store_rows(B - 1)

        @block.gpsimd
        def _(pool):
            for v in range(2):
                nc.gpsimd.memset(v_now[v][:, :, :, :], 0.0).then_inc(zeroed, 1)
            pool.wait_ge(zeroed, 2)

            def batch(j, v, first, last):
                t = 2 * j + v
                wait_past(pool, pv_done, 16 * (t - 1))
                for k in range(BLK):
                    copy = nc.gpsimd.tensor_copy(v_now[v][:, k, :, 0:HD + 1], values[:, bass.ds(BLK * t + k, 1), :, :].rearrange(
                        "p o h d -> p (o h) d"))
                copy.then_inc(v_ready, 1)
                pool.wait_ge(x_in, 16 * t + 16)
                if not first:
                    pool.wait_ge(drained, item(t, "project"))
                pool.wait_ge(consts_in, 48)
                nc.gpsimd.tensor_tensor(xb[:, :, :], x_in_sb[:, :, :],
                                        bias[:, :].unsqueeze(1).broadcast_to([P, BLK, D]), ALU.add).then_inc(biased, 1)
                if not first:
                    inverse_root(nc, pool, c, t - 1, moments[:, :, 1], moments_done, 1.0, LN_EPS, shifted, eps_added, rstd,
                                 rstd_done)

            all_batches(pool, batch)
            inverse_root(nc, pool, c, B - 1, moments[:, :, 1], moments_done, 1.0, LN_EPS, shifted, eps_added, rstd, rstd_done)


def inverse_root(nc, pool, c, t, value, ready, scale, eps, shifted, eps_added, out, out_done):
    pool.wait_ge(ready, t + 1)
    pool.sem_inc(c.pool_passed, 1)
    pool.wait_ge(ready, 1)
    nc.gpsimd.tensor_scalar(shifted[:, :], value, scale, eps, ALU.mult, ALU.add).then_inc(eps_added, 1)
    pool.wait_ge(eps_added, t + 1)
    nc.gpsimd.tensor_tensor(out[:, :], shifted[:, :], c.neg_half[:, :], ALU.pow).then_inc(out_done, 1)


TOPK = 2
H2 = 2 * P
GATE_EPS = 1e-9
RMS_EPS = 1.1920929e-07
WKV_EPS = 1e-8
GRP = 4
SLOT_TILES = 2 * NT + 20


class Count:

    def __init__(self, *names):
        self.names = names

    def __call__(self, i, name):
        return i * len(self.names) + (self.names.index(name) + 1)

    def before(self, i):
        return i * len(self.names)


def flat(ap):
    return ap.rearrange("p o d -> p (o d)")


def along(ap, k):
    return ap.unsqueeze(1).broadcast_to([ap.shape[0], k, ap.shape[1]])


class Experts:

    def __init__(self, nc, ctx, name, n, w1, w2):
        sb = lambda what, shape, dt=F32: ctx.enter_context(nc.sbuf_tensor(f"{name}_{what}", shape, dt))
        self.name, self.n = name, n
        self.steps = -(-(TOPK * NT + n) // 4) * 4
        self.table_len = self.steps + 4
        self.w = sb("w", [P, n, H2 + 2 + 2 * D])
        self.w1, self.w2 = self.w[:, :, 0:H2 + 2], self.w[:, :, H2 + 2:]
        self.w1_dram, self.w2_dram = w1, w2
        self.slots = sb("slots", [P, NT * TOPK], I32)
        self.gates = sb("gates", [P, NT, TOPK])
        self.mean, self.rstd = sb("mean", [P, NT]), sb("rstd", [P, NT])
        self.table = sb("table", [1, self.table_len], I32)


def row_stats(nc, c, tag, rows, mean, rstd, eps, rms=False, std=None):
    steps = ("sum_means", "spread", "halves", "mean", "inner", "square", "mean_square", "var", "moment", "rstd")
    with ExitStack() as ctx:
        sb, psum, sem = scope(nc, ctx, tag)
        stats = sb("stats", [P, NT, 6])
        sum_means, spread, halves, inner, square, mean_square, var, moment, root = (
            sb(x, [P, NT]) for x in ("sum_means", "spread", "halves", "inner", "square", "mean_square", "var", "moment", "root"))
        eps_sb = sb("eps", [P, 1])
        root = root if std is None else std
        stats_done, did, rooted = sem("stats_done"), sem("did"), sem("rooted")
        block = ctx.enter_context(nc.Block())
        vec = Count(*steps)

        @block.scalar
        def _(act):
            act.wait_ge(did, vec(0, "moment"))
            nc.scalar.activation(root[:, :], moment[:, :], ACT.Sqrt, bias=eps_sb[:, 0:1]).then_inc(rooted, 1)

        @block.vector
        def _(dve):
            nc.vector.memset(eps_sb[:, :], eps)
            for t in range(NT):
                nc.vector.bn_stats(stats[:, t, :], rows[:, t, :]).then_inc(stats_done, 1)
            dve.wait_ge(stats_done, NT)
            nc.vector.tensor_tensor(sum_means[:, :], stats[:, :, 1], stats[:, :, 4], ALU.add).then_inc(did, 1)
            nc.vector.tensor_tensor(spread[:, :], stats[:, :, 1], stats[:, :, 4], ALU.subtract).then_inc(did, 1)
            nc.vector.tensor_tensor(halves[:, :], stats[:, :, 2], stats[:, :, 5], ALU.add).then_inc(did, 1)
            dve.wait_ge(did, vec(0, "halves"))
            nc.vector.tensor_scalar(mean, sum_means[:, :], 0.5, None, ALU.mult).then_inc(did, 1)
            nc.vector.tensor_scalar(inner[:, :], halves[:, :], 1.0 / D, None, ALU.mult).then_inc(did, 1)
            nc.vector.tensor_tensor(square[:, :], spread[:, :], spread[:, :], ALU.mult).then_inc(did, 1)
            dve.wait_ge(did, vec(0, "square"))
            nc.vector.tensor_tensor(mean_square[:, :], mean, mean, ALU.mult).then_inc(did, 1)
            nc.vector.scalar_tensor_tensor(out=var[:, :], in0=square[:, :], scalar=0.25, in1=inner[:, :],
                                           op0=ALU.mult, op1=ALU.add).then_inc(did, 1)
            dve.wait_ge(did, vec(0, "var"))
            if rms:
                nc.vector.tensor_tensor(moment[:, :], var[:, :], mean_square[:, :], ALU.add).then_inc(did, 1)
            else:
                nc.vector.tensor_copy(moment[:, :], var[:, :]).then_inc(did, 1)
            dve.wait_ge(rooted, 1)
            nc.vector.reciprocal(rstd, root[:, :]).then_inc(did, 1)


def send_to_experts(nc, c, ex, shared):
    with ExitStack() as ctx:
        sb, psum, sem = scope(nc, ctx, f"{ex.name}_gate")
        logit, std = sb("logit", [P, NT, ex.n]), sb("std", [P, NT])
        row_stats(nc, c, f"{ex.name}_stats", c.rows, ex.mean[:, :], ex.rstd[:, :], RMS_EPS if shared else LN_EPS, shared, std)
        score_tokens(nc, c, ex, logit, std, shared)
        choose_experts(nc, c, ex, logit, shared)
    send_rows(nc, c, ex, shared)


def load_experts(nc, c, ex, scale, bias):
    n = ex.n
    with ExitStack() as ctx:
        sb, psum, sem = scope(nc, ctx, f"{ex.name}_load")
        per = scale.shape[1] // n
        factor = sb("factor", [P, scale.shape[1]])
        shift = sb("shift", [P, 1])
        hidden = psum("hidden_bias")[:, 0:2 * n].rearrange("p (e k) -> p e k", k=2)
        w_in, multiplied = sem("w_in"), sem("multiplied")
        block = ctx.enter_context(nc.Block())

        @block.sync
        def _(sp):
            sp.dma_start(ex.w1[:, :, 0:H2], ex.w1_dram.rearrange("e c h -> c e h")).then_inc(w_in, 16)
            for k in range(2):
                sp.dma_start(ex.w2[:, :, k * D:(k + 1) * D], ex.w2_dram[:, k * P:(k + 1) * P, :].rearrange("e p d -> p e d")
                             ).then_inc(w_in, 16)
            sp.dma_start(factor[:, :], scale).then_inc(w_in, 16)
            if bias is not None:
                sp.dma_start(shift[:, :], bias).then_inc(w_in, 16)

        loads = 64 + 16 * (bias is not None)

        @block.tensor
        def _(pe):
            if bias is not None:
                pe.wait_ge(w_in, loads)
                for e in range(n):
                    for k in range(2):
                        mm = nc.tensor.matmul(hidden[:, e, k:k + 1], ex.w1[:, e, k * P:(k + 1) * P], shift[:, :],
                                              start=True, stop=True)
                mm.then_inc(multiplied, 1)

        @block.vector
        def _(dve):
            dve.wait_ge(w_in, loads)
            if bias is not None:
                dve.wait_ge(multiplied, 1)
                nc.vector.tensor_copy(ex.w1[:, :, H2:], hidden[:, :, :])
            else:
                nc.vector.memset(ex.w1[:, :, H2:], 0.0)
            for e in range(n):
                nc.vector.tensor_scalar(ex.w1[:, e, 0:H2], ex.w1[:, e, 0:H2], factor[:, e * per:e * per + 1], None, ALU.mult)


def normalise(nc, c, ex, out, t, count, shared):
    for j in range(count):
        x, rstd = flat(c.rows[:, bass.ds(t + j, 1), :]), ex.rstd[:, bass.ds(t + j, 1)]
        if shared:
            s = nc.vector.tensor_scalar(out[:, j, :], x, rstd, None, ALU.mult)
        else:
            s = nc.vector.tensor_scalar(out[:, j, :], x, ex.mean[:, bass.ds(t + j, 1)], rstd, ALU.subtract, ALU.mult)
    return s


def score_tokens(nc, c, ex, logit, std, shared):
    a, n = c.a, ex.n
    with ExitStack() as ctx:
        sb, psum, sem = scope(nc, ctx, f"{ex.name}_score")
        router, router_bias = sb("router", [P, n]), sb("router_bias", [P, n])
        factor, shift = sb("factor", [P, 1]), sb("shift", [P, 1])
        z = [sb(f"z{u}", [P, GRP, D]) for u in range(2)]
        zt = [sb(f"zt{u}", [P, GRP * P]) for u in range(2)]
        turn_bank, logit_bank = ([psum(f"{x}{u}") for u in range(2)] for x in ("turn_bank", "logit_bank"))
        fold_bank = psum("fold_bank")
        weights_in, biased, folded = sem("weights_in"), sem("biased"), sem("folded")
        z_ready, turned, zt_done, scored, kept = (
            sem(x) for x in ("z_ready", "turned", "zt_done", "scored", "kept"))
        block = ctx.enter_context(nc.Block())
        loads = 16 if shared else 48
        groups = NT // GRP

        @block.sync
        def _(sp):
            if shared:
                sp.dma_start(router[:, :], a["router0"]).then_inc(weights_in, 16)
            else:
                sp.dma_start(router[:, :], a["router1_t"]).then_inc(weights_in, 16)
                sp.dma_start(factor[:, :], a["ln2_w"]).then_inc(weights_in, 16)
                sp.dma_start(shift[:, :], a["ln2_b"]).then_inc(weights_in, 16)

        @block.tensor
        def _(pe):
            pe.wait_ge(weights_in, loads)
            if not shared:
                nc.tensor.matmul(fold_bank[:, 0:n], shift[:, :].broadcast_to([P, P]), router[:, :],
                                 start=True, stop=True).then_inc(biased, 1)
            pe.wait_ge(folded, 1)

            def turn(g, u):
                pe.wait_ge(z_ready, g + 1)
                for j in range(GRP):
                    mm = nc.tensor.transpose(turn_bank[u][:, j * P:(j + 1) * P], z[u][:, j, :], c.ident[:, :])
                mm.then_inc(turned, 1)

            def score(g, u):
                pe.wait_ge(zt_done, g + 1)
                pe.wait_ge(kept, g)
                for j in range(GRP):
                    mm = nc.tensor.matmul(logit_bank[u][:, j * n:(j + 1) * n], zt[u][:, j * P:(j + 1) * P], router[:, :],
                                          start=True, stop=True)
                mm.then_inc(scored, 1)

            with pe.Fori(0, groups // 2) as i:
                for u in range(2):
                    pe.wait_ge(zt_done, 2 * i + u)
                    turn(2 * i + u, u)
                    score(2 * i + u, u)

        @block.scalar
        def _(act):
            with act.Fori(0, groups // 2) as i:
                for u in range(2):
                    act.wait_ge(turned, 2 * i + u + 1)
                    act.wait_ge(scored, 2 * i + u)
                    nc.scalar.copy(zt[u][:, :], turn_bank[u][:, :]).then_inc(zt_done, 1)

        @block.vector
        def _(dve):
            dve.wait_ge(weights_in, loads)
            if not shared:
                dve.wait_ge(biased, 1)
                nc.vector.tensor_copy(router_bias[:, :], fold_bank[:, 0:n])
                nc.vector.tensor_scalar(router[:, :], router[:, :], factor[:, 0:1], None, ALU.mult).then_inc(folded, 1)
            else:
                dve.sem_inc(folded, 1)
            def keep(g, u):
                dve.wait_ge(scored, g + 1)
                for j in range(GRP):
                    out = flat(logit[:, bass.ds(GRP * g + j, 1), :])
                    if shared:
                        s = nc.vector.tensor_scalar(out, logit_bank[u][:, j * n:(j + 1) * n],
                                                    std[:, bass.ds(GRP * g + j, 1)], None, ALU.mult)
                    else:
                        s = nc.vector.tensor_tensor(out, logit_bank[u][:, j * n:(j + 1) * n], router_bias[:, :], ALU.add)
                s.then_inc(kept, 1)

            def prepare(g, u):
                normalise(nc, c, ex, z[u], GRP * g, GRP, shared).then_inc(z_ready, 1)

            prepare(0, 0)
            with dve.Fori(0, groups // 2 - 1) as i:
                for u in range(2):
                    dve.wait_ge(turned, 2 * i + u)
                    prepare(2 * i + u + 1, 1 - u)
                    keep(2 * i + u, u)
            dve.wait_ge(turned, groups - 2)
            prepare(groups - 1, 1)
            keep(groups - 2, 0)
            keep(groups - 1, 1)


def choose_experts(nc, c, ex, logit, renormalise):
    n = ex.n
    names = ("peak", "centred", "total", "recip", "gate", "g0", "is0", "score0", "best0", "first0", "rest",
             "g1", "is1", "score1", "best1", "first1", "either", "per_tile", "scan", "count", "count_up", "count_int",
             "full", "tiles", "until", "begin", "gap", "gap_all", "earlier_tiles", "place", "placed0", "slot0",
             "placed1", "slot1", "gate_sum", "gate_eps", "gate_inv", "past", "expert", "last_expert")
    vec = Count(*names)
    with ExitStack() as ctx:
        sb, psum, sem = scope(nc, ctx, f"{ex.name}_choose")
        earlier_f, earlier, every = sb("earlier_f", [P, P]), sb("earlier", [P, P], BF16), sb("every", [P, P], BF16)
        rank_i, rank_f = sb("rank_int", [P, n], I32), sb("rank", [P, n])
        tile_i, tile_f = sb("tile_int", [1, ex.table_len], I32), sb("tile_no", [1, ex.table_len])
        peak, total, recip = (sb(x, [P, NT]) for x in ("peak", "total", "recip"))
        centred, e_x, gate, hit, score = (sb(x, [P, NT, n]) for x in ("centred", "e_x", "gate", "hit", "score"))
        best = sb("best", [P, NT])
        top = sb("top", [P, TOPK, NT])
        first = [sb(f"first{k}", [P, NT, n]) for k in range(TOPK)]
        either = sb("either", [P, NT, n], BF16)
        per_tile, scan, ones = (sb(x, [P, n, NT]) for x in ("per_tile", "scan", "ones"))
        count, count_up, tiles, until, begin, gap = (sb(x, [P, n]) for x in ("count", "count_up", "tiles", "until", "begin", "gap"))
        count_int, full = sb("count_int", [P, n], I32), sb("full", [P, n], I32)
        place, placed = sb("place", [P, NT, n]), sb("placed", [P, NT, n])
        slot_f = sb("slot_f", [P, NT])
        gate_sum, gate_inv = sb("gate_sum", [P, NT]), sb("gate_inv", [P, NT])
        past, expert = sb("past", [1, ex.table_len, n]), sb("expert", [1, ex.table_len])
        half = NT // 2
        rank_bank, tile_bank = ([psum(f"{x}{u}") for u in range(2)] for x in ("rank_bank", "tile_bank"))
        filled, made, vector_did, exped, ranked = sem("filled"), sem("made"), sem("vector_did"), sem("exped"), sem("ranked")
        block = ctx.enter_context(nc.Block())

        @block.gpsimd
        def _(pool):
            nc.gpsimd.iota(rank_i[:, :], pattern=[[-1, n]], base=n, channel_multiplier=0).then_inc(made, 1)
            nc.gpsimd.iota(tile_i[:, :], pattern=[[1, ex.table_len]], base=0, channel_multiplier=0).then_inc(made, 1)
            nc.gpsimd.memset(ones[:, :, :], 1.0).then_inc(made, 1)
            nc.gpsimd.memset(earlier_f[:, :], 1.0).then_inc(filled, 1)
            pool.wait_ge(filled, 1)
            nc.gpsimd.affine_select(out=earlier_f[:, :], in_=earlier_f[:, :], compare_op=ALU.is_ge, fill=0.0,
                                    base=-1, pattern=[[1, P]], channel_multiplier=-1).then_inc(made, 1)

        @block.scalar
        def _(act):
            act.wait_ge(vector_did, vec(0, "centred"))
            nc.scalar.activation(e_x[:, :, :], centred[:, :, :], ACT.Exp).then_inc(exped, 1)

        @block.tensor
        def _(pe):
            pe.wait_ge(vector_did, vec(0, "either"))
            for u in range(2):
                chosen = either[:, u * half:(u + 1) * half, :].rearrange("p j e -> p (j e)")
                nc.tensor.matmul(tile_bank[u][:, 0:half * n], every[:, :], chosen, start=True, stop=True)
                mm = nc.tensor.matmul(rank_bank[u][:, 0:half * n], earlier[:, :], chosen, start=True, stop=True)
            mm.then_inc(ranked, 1)

        @block.vector
        def _(dve):
            did = lambda name: dve.wait_ge(vector_did, vec(0, name))
            nc.vector.memset(every[:, :], 1.0)
            dve.wait_ge(made, 4)
            nc.vector.tensor_copy(earlier[:, :], earlier_f[:, :])
            nc.vector.tensor_copy(tile_f[:, :], tile_i[:, :])
            nc.vector.tensor_copy(rank_f[:, :], rank_i[:, :])
            nc.vector.tensor_reduce(peak[:, :], logit[:, 0:NT, :], AX.X, ALU.max).then_inc(vector_did, 1)
            did("peak")
            nc.vector.tensor_tensor(centred[:, :, :], logit[:, 0:NT, :], bcast(peak[:, :], n), ALU.subtract
                                    ).then_inc(vector_did, 1)
            dve.wait_ge(exped, 1)
            nc.vector.tensor_reduce(total[:, :], e_x[:, :, :], AX.X, ALU.add).then_inc(vector_did, 1)
            did("total")
            nc.vector.reciprocal(recip[:, :], total[:, :]).then_inc(vector_did, 1)
            did("recip")
            nc.vector.tensor_tensor(gate[:, :, :], e_x[:, :, :], bcast(recip[:, :], n), ALU.mult).then_inc(vector_did, 1)
            did("gate")
            for k in range(TOPK):
                nc.vector.tensor_reduce(top[:, k, :], gate[:, :, :], AX.X, ALU.max).then_inc(vector_did, 1)
                did(f"g{k}")
                nc.vector.tensor_tensor(hit[:, :, :], gate[:, :, :], bcast(top[:, k, :], n), ALU.is_equal
                                        ).then_inc(vector_did, 1)
                did(f"is{k}")
                nc.vector.tensor_tensor(score[:, :, :], hit[:, :, :], along(rank_f[:, :], NT), ALU.mult
                                        ).then_inc(vector_did, 1)
                did(f"score{k}")
                nc.vector.tensor_reduce(best[:, :], score[:, :, :], AX.X, ALU.max).then_inc(vector_did, 1)
                did(f"best{k}")
                nc.vector.tensor_tensor(first[k][:, :, :], along(rank_f[:, :], NT), bcast(best[:, :], n), ALU.is_equal
                                        ).then_inc(vector_did, 1)
                did(f"first{k}")
                if k == 0:
                    nc.vector.scalar_tensor_tensor(out=gate[:, :, :], in0=first[0][:, :, :], scalar=-2.0, in1=gate[:, :, :],
                                                   op0=ALU.mult, op1=ALU.add).then_inc(vector_did, 1)
                    did("rest")
            nc.vector.tensor_tensor(either[:, :, :], first[0][:, :, :], first[1][:, :, :], ALU.add).then_inc(vector_did, 1)
            dve.wait_ge(ranked, 1)
            for u in range(2):
                s = nc.vector.tensor_copy(per_tile[:, :, u * half:(u + 1) * half],
                                          tile_bank[u][:, 0:half * n].rearrange("p (j e) -> p e j", e=n))
            s.then_inc(vector_did, 1)
            did("per_tile")
            nc.vector.tensor_tensor_scan(scan[:, :, :].rearrange("p e j -> p (e j)"), ones[:, :, :].rearrange("p e j -> p (e j)"),
                                         per_tile[:, :, :].rearrange("p e j -> p (e j)"), 0.0, ALU.mult, ALU.add
                                         ).then_inc(vector_did, 1)
            nc.vector.tensor_reduce(count[:, :], per_tile[:, :, :], AX.X, ALU.add).then_inc(vector_did, 1)
            did("count")
            nc.vector.tensor_scalar(count_up[:, :], count[:, :], float(P - 1), None, ALU.add).then_inc(vector_did, 1)
            did("count_up")
            nc.vector.tensor_copy(count_int[:, :], count_up[:, :]).then_inc(vector_did, 1)
            did("count_int")
            nc.vector.tensor_scalar(full[:, :], count_int[:, :], P.bit_length() - 1, None, ALU.arith_shift_right
                                    ).then_inc(vector_did, 1)
            did("full")
            nc.vector.tensor_copy(tiles[:, :], full[:, :]).then_inc(vector_did, 1)
            did("tiles")
            nc.vector.tensor_tensor_scan(until[:, :], ones[:, 0, 0:n], tiles[:, :], 0.0, ALU.mult, ALU.add
                                         ).then_inc(vector_did, 1)
            did("until")
            nc.vector.tensor_tensor(begin[:, :], until[:, :], tiles[:, :], ALU.subtract).then_inc(vector_did, 1)
            did("begin")
            nc.vector.tensor_tensor(gap[:, :], scan[:, :, NT - 1], count[:, :], ALU.subtract).then_inc(vector_did, 1)
            did("gap")
            nc.vector.scalar_tensor_tensor(out=gap[:, :], in0=begin[:, :], scalar=float(P), in1=gap[:, :],
                                           op0=ALU.mult, op1=ALU.subtract).then_inc(vector_did, 1)
            nc.vector.tensor_tensor(scan[:, :, :], scan[:, :, :], per_tile[:, :, :], ALU.subtract).then_inc(vector_did, 1)
            did("earlier_tiles")
            for u in range(2):
                s = nc.vector.tensor_tensor(place[:, u * half:(u + 1) * half, :],
                                            rank_bank[u][:, 0:half * n].rearrange("p (j e) -> p j e", e=n),
                                            scan[:, :, u * half:(u + 1) * half].rearrange("p e j -> p j e"), ALU.add)
            s.then_inc(vector_did, 1)
            did("place")
            nc.vector.tensor_tensor(place[:, :, :], place[:, :, :], along(gap[:, :], NT), ALU.add).then_inc(made, 1)
            dve.wait_ge(made, 5)
            for k in range(TOPK):
                nc.vector.tensor_tensor(placed[:, :, :], first[k][:, :, :], place[:, :, :], ALU.mult).then_inc(vector_did, 1)
                did(f"placed{k}")
                nc.vector.tensor_reduce(slot_f[:, :], placed[:, :, :], AX.X, ALU.add).then_inc(vector_did, 1)
                did(f"slot{k}")
                nc.vector.tensor_copy(ex.slots[:, :].rearrange("p (j k) -> p j k", k=TOPK)[:, :, k], slot_f[:, :]
                                      ).then_inc(made, 1)
                dve.wait_ge(made, 6 + k)
            nc.vector.tensor_tensor(gate_sum[:, :], top[:, 0, :], top[:, 1, :], ALU.add).then_inc(vector_did, 1)
            did("gate_sum")
            nc.vector.tensor_scalar(gate_sum[:, :], gate_sum[:, :], GATE_EPS, None, ALU.add).then_inc(vector_did, 1)
            did("gate_eps")
            nc.vector.reciprocal(gate_inv[:, :], gate_sum[:, :]).then_inc(vector_did, 1)
            did("gate_inv")
            for k in range(TOPK):
                if renormalise:
                    nc.vector.tensor_tensor(ex.gates[:, :, k], top[:, k, :], gate_inv[:, :], ALU.mult)
                else:
                    nc.vector.tensor_copy(ex.gates[:, :, k], top[:, k, :])
            nc.vector.tensor_tensor(past[:, :, :], along(until[0:1, :], ex.table_len), bcast(tile_f[:, :], n), ALU.is_le
                                    ).then_inc(vector_did, 1)
            did("past")
            nc.vector.tensor_reduce(expert[:, :], past[:, :, :], AX.X, ALU.add).then_inc(vector_did, 1)
            did("expert")
            nc.vector.tensor_scalar(expert[:, :], expert[:, :], float(n - 1), None, ALU.min).then_inc(vector_did, 1)
            did("last_expert")
            nc.vector.tensor_copy(ex.table[:, :], expert[:, :])


def send_rows(nc, c, ex, shared):
    a = c.a
    with ExitStack() as ctx:
        sb, psum, sem = scope(nc, ctx, f"{ex.name}_send")
        at = [sb(f"at{u}", [P, BLK * TOPK], I32) for u in range(2)]
        z = [sb(f"z{u}", [P, BLK, D]) for u in range(2)]
        w1s, w2s, rms_w = sb("w1_shared", [P, 2, H2]), sb("w2_shared", [P, 4, D]), sb("rms_shared", [P, 2])
        zt = [sb(f"zt{u}", [P, T]) for u in range(2)]
        half_tanh, hid = sb("half_tanh", [P, 4, T]), [sb(f"hid{u}", [P, 4, T]) for u in range(2)]
        turn_bank = [psum(f"turn_bank{u}") for u in range(2)]
        acc_bank = [psum(f"acc_bank{u}") for u in range(2)]
        hid_bank = [psum(f"hid_bank{k}") for k in range(4)]
        weights_in, folded, at_set, z_ready, sent = sem("weights_in"), sem("folded"), sem("at_set"), sem("z_ready"), c.indirect[f"{ex.name}_sent"]
        turned, zt_done, hid_done, tanhed, hid_out, acc_done, acc_out = (
            sem(x) for x in ("turned", "zt_done", "hid_done", "tanhed", "hid_out", "acc_done", "acc_out"))
        block = ctx.enter_context(nc.Block())

        @block.gpsimd
        def _(pool):
            pool.wait_ge(c.cleared, 16)
            with pool.Fori(0, B // 2) as i:
                for u in range(2):
                    t = 2 * i + u
                    pool.wait_ge(sent[u], 16 * BLK * TOPK * i)
                    nc.gpsimd.tensor_copy(at[u][:, :], ex.slots[:, bass.ds(BLK * TOPK * t, BLK * TOPK)]).then_inc(at_set, 1)
                    pool.wait_ge(at_set, t + 1)
                    pool.wait_ge(z_ready, t + 1)
                    pool.sem_inc(c.pool_passed, 1)
                    pool.wait_ge(c.cleared, 16)
                    for m in range(BLK * TOPK):
                        nc.gpsimd.indirect_dma_start(c.expert_in, bass.IndirectOffsetOnAxis(at[u][:, m:m + 1], 0),
                                                     z[u][:, m // TOPK, :], None
                                                     ).then_inc(sent[u], 16)
            for u in range(2):
                pool.wait_ge(sent[u], 8 * BLK * TOPK * B)

        if not shared:
            @block.vector
            def _(dve):
                with dve.Fori(0, B // 2) as i:
                    for u in range(2):
                        dve.wait_ge(sent[u], 16 * BLK * TOPK * i)
                        normalise(nc, c, ex, z[u], BLK * (2 * i + u), BLK, shared).then_inc(z_ready, 1)
            return

        @block.sync
        def _(sp):
            sp.dma_start(w1s[:, :, :], a["w1_s"].rearrange("e c h -> c e h")).then_inc(weights_in, 16)
            sp.dma_start(w2s[:, :, :], a["w2_s"].rearrange("e (k p) d -> p (e k) d", p=P)).then_inc(weights_in, 16)
            sp.dma_start(rms_w[:, :], a["rms_w_s_t"]).then_inc(weights_in, 16)

        @block.tensor
        def _(pe):
            def turn(t, u):
                pe.wait_ge(z_ready, t + 1)
                for j in range(BLK):
                    mm = nc.tensor.transpose(turn_bank[u][:, j * P:(j + 1) * P], z[u][:, j, :], c.ident[:, :])
                mm.then_inc(turned, 1)

            pe.wait_ge(folded, 2)
            turn(0, 0)

            def hidden(t, u):
                pe.wait_ge(hid_out, t)
                for k in range(4):
                    nc.tensor.matmul(hid_bank[k][:, 0:T], w1s[:, k // 2, k % 2 * P:(k % 2 + 1) * P], zt[u][:, :],
                                     start=True, stop=True).then_inc(hid_done, 1)

            def output(t, u):
                wait_past(pe, acc_out, t)
                pe.wait_ge(hid_out, t + 1)
                for j in range(BLK):
                    for k in range(4):
                        mm = nc.tensor.matmul(acc_bank[u][:, j * D:(j + 1) * D], hid[u][:, k, j * P:(j + 1) * P],
                                              w2s[:, k, :], start=k == 0, stop=k == 3)
                mm.then_inc(acc_done, 1)

            pe.wait_ge(zt_done, 1)
            turn(1, 1)
            hidden(0, 0)
            with pe.Fori(0, B // 2 - 1) as i:
                for u in range(2):
                    t = 2 * i + u + 1
                    pe.wait_ge(zt_done, t + 1)
                    turn(t + 1, u)
                    hidden(t, 1 - u)
                    output(t - 1, u)
            pe.wait_ge(zt_done, B)
            hidden(B - 1, 1)
            output(B - 2, 0)
            output(B - 1, 1)

        @block.scalar
        def _(act):
            with act.Fori(0, B // 2) as i:
                for u in range(2):
                    t = 2 * i + u
                    act.wait_ge(turned, t + 1)
                    act.wait_ge(hid_out, t)
                    nc.scalar.copy(zt[u][:, :], turn_bank[u][:, 0:T]).then_inc(zt_done, 1)
                    for k in range(4):
                        act.wait_ge(hid_done, 4 * t + k + 1)
                        nc.scalar.activation(half_tanh[:, k, :], hid_bank[k][:, 0:T], ACT.Tanh, scale=0.5).then_inc(tanhed, 1)

        @block.vector
        def _(dve):
            dve.wait_ge(weights_in, 48)
            for e in range(2):
                s = nc.vector.tensor_scalar(w1s[:, e, :], w1s[:, e, :], rms_w[:, e:e + 1], None, ALU.mult)
            s.then_inc(folded, 1)
            nc.vector.tensor_scalar(w2s[:, :, :], w2s[:, :, :], 0.5, None, ALU.mult).then_inc(folded, 1)

            def add(t, u):
                dve.wait_ge(acc_done, t + 1)
                rows = c.rows[:, bass.ds(BLK * t, BLK), :].rearrange("p j d -> p (j d)")
                nc.vector.tensor_tensor(rows, rows, acc_bank[u][:, 0:BLK * D], ALU.add).then_inc(acc_out, 1)

            def hidden(t, u):
                wait_past(dve, acc_done, t - 1)
                for k in range(4):
                    dve.wait_ge(tanhed, 4 * t + k + 1)
                    s = nc.vector.scalar_tensor_tensor(out=hid[u][:, k, :], in0=half_tanh[:, k, :], scalar=1.0,
                                                       in1=hid_bank[k][:, 0:T], op0=ALU.add, op1=ALU.mult)
                s.then_inc(hid_out, 1)

            for u in range(2):
                normalise(nc, c, ex, z[u], BLK * u, BLK, shared).then_inc(z_ready, 1)
            hidden(0, 0)
            with dve.Fori(0, B // 2 - 1) as i:
                for u in range(2):
                    t = 2 * i + u + 1
                    dve.wait_ge(sent[u], 16 * BLK * TOPK * (i + 1))
                    dve.wait_ge(turned, t)
                    normalise(nc, c, ex, z[u], BLK * (t + 1), BLK, shared).then_inc(z_ready, 1)
                    hidden(t, 1 - u)
                    add(t - 1, u)
            hidden(B - 1, 1)
            add(B - 2, 0)
            add(B - 1, 1)


def run_experts(nc, c, ex, func, hidden_bias):
    with ExitStack() as ctx:
        sb, psum, sem = scope(nc, ctx, f"{ex.name}_run")
        RING = 4
        rows_sb, y = ([sb(f"{x}{r}", [P, D]) for r in range(RING)] for x in ("rows_sb", "y"))
        w_now = [sb(f"w_now{r}", [P, H2 + 2 + 2 * D]) for r in range(RING)]
        rows_t, hid = ([sb(f"{x}{u}", shape) for u in range(2)] for x, shape in (("rows_t", [P, P]), ("hid", [P, 2, P])))
        turn_bank, hid_bank, y_bank = ([psum(f"{x}{u}") for u in range(2)] for x in ("turn_bank", "hid_bank", "y_bank"))
        rows_in, rows_out = ([sem(f"{x}{r}") for r in range(RING)] for x in ("rows_in", "rows_out"))
        w_ready = [sem("w_even_ready"), sem("w_odd_ready")]
        turned, rows_ready, hid_made, hid_ready, y_made, y_ready = (
            sem(x) for x in ("turned", "rows_ready", "hid_made", "hid_ready", "y_made", "y_ready"))
        block = ctx.enter_context(nc.Block())
        steps = ex.steps

        def expert(eng, s):
            return eng.value_load(ex.table[0:1, bass.ds(s, 1)], min_val=0, max_val=ex.n - 1)

        @block.sync
        def _(sp):
            def load(s, u):
                sp.dma_start(rows_sb[u][:, :], c.expert_in[bass.ds(P * s, P), :]).then_inc(rows_in[u], 16)

            for r in range(RING):
                load(r, r)
            with sp.Fori(0, steps // RING) as i:
                for r in range(RING):
                    s = RING * i + r
                    sp.wait_ge(turned, s + 1)
                    load(s + RING, r)
                    sp.wait_ge(y_ready, s + 1)
                    sp.dma_start(c.expert_out[bass.ds(P * s, P), :], y[r][:, :]).then_inc(rows_out[r], 16)
            for r in range(RING):
                sp.wait_ge(rows_in[r], 16 * (steps // RING) + 16)
                sp.wait_ge(rows_out[r], 16 * (steps // RING))

        @block.tensor
        def _(pe):
            def turn(s, r, loaded):
                pe.wait_ge(rows_in[r], loaded)
                nc.tensor.transpose(turn_bank[r % 2][:, 0:P], rows_sb[r][:, :], c.ident[:, :]).then_inc(turned, 1)

            def hidden(i, r):
                s, u = RING * i + r, r % 2
                pe.wait_ge(w_ready[u], 2 * i + r // 2 + 1)
                pe.wait_ge(rows_ready, s + 1)
                for k in range(2):
                    mm = nc.tensor.matmul(hid_bank[u][:, k * P:(k + 1) * P], w_now[r][:, k * P:(k + 1) * P], rows_t[u][:, :],
                                          start=True, stop=True)
                mm.then_inc(hid_made, 1)

            for u in range(2):
                turn(u, u, 16)
            hidden(0, 0)
            with pe.Fori(0, steps // RING) as i:
                for r in range(RING):
                    s, u = RING * i + r, r % 2
                    pe.wait_ge(rows_ready, s + 1)
                    turn(s + 2, (r + 2) % RING, 16 * i + 16 * ((r + 2) // RING) + 16)
                    pe.wait_ge(hid_ready, s)
                    hidden(i + (r + 1) // RING, (r + 1) % RING)
                    pe.wait_ge(hid_ready, s + 1)
                    pe.wait_ge(y_ready, s)
                    for k in range(2):
                        w = w_now[r][:, H2 + 2 + k * D:H2 + 2 + (k + 1) * D]
                        mm = nc.tensor.matmul(y_bank[u][:, 0:D], hid[u][:, k, :], w, start=k == 0, stop=k == 1)
                    mm.then_inc(y_made, 1)

        @block.gpsimd
        def _(pool):
            def weights(s, r):
                e = expert(pool, s)
                nc.gpsimd.tensor_copy(w_now[r][:, :], flat(ex.w[:, bass.ds(e, 1), :])).then_inc(w_ready[0], 1)

            for r in range(0, RING, 2):
                weights(r, r)
            with pool.Fori(0, steps // RING) as i:
                for r in range(0, RING, 2):
                    s = RING * i + r
                    pool.wait_ge(y_made, s + 1)
                    weights(s + RING, r)

        @block.scalar
        def _(act):
            def activate(s, r):
                u = r % 2
                act.wait_ge(hid_made, s + 1)
                src = hid_bank[u][:, 0:2 * P].rearrange("p (k t) -> p k t", k=2)
                if hidden_bias:
                    for k in range(2):
                        e = nc.scalar.activation(hid[u][:, k, :], src[:, k, :], func, bias=w_now[r][:, H2 + k:H2 + k + 1])
                else:
                    e = nc.scalar.activation(hid[u][:, :, :], src, func)
                e.then_inc(hid_ready, 1)

            activate(0, 0)
            with act.Fori(0, steps // RING) as i:
                for r in range(RING):
                    s = RING * i + r
                    act.wait_ge(y_made, s)
                    activate(s + 1, (r + 1) % RING)

        @block.vector
        def _(dve):
            def rows_transposed(s, u):
                dve.wait_ge(turned, s + 1)
                nc.vector.tensor_copy(rows_t[u][:, :], turn_bank[u][:, 0:P]).then_inc(rows_ready, 1)

            def weights(s, r):
                e = expert(dve, s)
                nc.vector.tensor_copy(w_now[r][:, :], flat(ex.w[:, bass.ds(e, 1), :])).then_inc(w_ready[1], 1)

            for r in range(1, RING, 2):
                weights(r, r)
            for u in range(2):
                rows_transposed(u, u)
            with dve.Fori(0, steps // RING) as i:
                for r in range(RING):
                    s, u = RING * i + r, r % 2
                    dve.wait_ge(hid_made, s + 1)
                    rows_transposed(s + 2, u)
                    dve.wait_ge(y_made, s + 1)
                    dve.wait_ge(rows_out[r], 16 * i)
                    nc.vector.tensor_copy(y[r][:, :], y_bank[u][:, 0:D]).then_inc(y_ready, 1)
                    if r % 2:
                        weights(s + RING, r)


def combine(nc, c, ex, extra, out):
    with ExitStack() as ctx:
        sb, psum, sem = scope(nc, ctx, f"{ex.name}_combine")
        at = [sb(f"at{u}", [P, BLK * TOPK], I32) for u in range(2)]
        got = [sb(f"got{u}", [P, BLK * TOPK, D]) for u in range(2)]
        y, y1 = sb("y", [P, BLK, D]), sb("y1", [P, BLK, D])
        stats, moments = sb("stats", [P, BLK, 6]), sb("moments", [P, BLK, 2])
        eps, std, rstd = sb("eps", [P, 1]), sb("std", [P, BLK]), sb("rstd", [P, BLK])
        gathered, stored = c.indirect[f"{ex.name}_gathered"], sem("stored")
        at_set, eps_set, rooted, vector_did = (sem(x) for x in ("at_set", "eps_set", "rooted", "vector_did"))
        added = sem("added")
        block = ctx.enter_context(nc.Block())
        vec = Count("one", *(("two",) if extra is not None else ()), "stats", "moments", "rstd", "rows")

        @block.sync
        def _(sp):
            if out is None:
                return
            batches = 8
            chunk = batches * BLK
            view = out.rearrange("s (g n) d -> n s g d", n=NPG)
            for k in range(B // batches):
                sp.wait_ge(vector_did, vec(batches * (k + 1) - 1, "rows"))
                for n in range(NPG):
                    sp.dma_start(view[n][:, k * chunk:(k + 1) * chunk, :],
                                 c.rows[n * B:(n + 1) * B, k * chunk:(k + 1) * chunk, :]).then_inc(stored, 16)
            sp.wait_ge(stored, 16 * NPG * B // batches)

        @block.gpsimd
        def _(pool):
            with pool.Fori(0, B // 2) as i:
                t = 2 * i
                for u in range(2):
                    pool.wait_ge(added, t + u + 1)
                    nc.gpsimd.tensor_copy(at[u][:, :], ex.slots[:, bass.ds(BLK * TOPK * (t + u), BLK * TOPK)]
                                          ).then_inc(at_set, 1)
                    pool.wait_ge(at_set, t + u + 1)
                    pool.sem_inc(c.pool_passed, 1)
                    pool.wait_ge(added, 2)
                    for i in range(BLK * TOPK):
                        nc.gpsimd.indirect_dma_start(got[u][:, i, :], None, c.expert_out[0:ex.steps * P, :],
                                                     bass.IndirectOffsetOnAxis(at[u][:, i:i + 1], 0)
                                                     ).then_inc(gathered[u], 16)

        @block.scalar
        def _(act):
            act.wait_ge(eps_set, 1)
            with act.Fori(0, B // 2) as i:
                t = 2 * i
                for u in range(2):
                    act.wait_ge(vector_did, vec(t + u, "moments"))
                    nc.scalar.activation(std[:, :], moments[:, :, 1], ACT.Sqrt, bias=eps[:, 0:1]).then_inc(rooted, 1)

        @block.vector
        def _(dve):
            did = lambda now, name: dve.wait_ge(vector_did, vec(now, name))
            nc.vector.memset(eps[:, :], LN_EPS).then_inc(eps_set, 1)
            dve.sem_inc(added, 2)
            with dve.Fori(0, B // 2) as i:
                t = 2 * i
                for u in range(2):
                    now = t + u
                    dve.wait_ge(gathered[u], 8 * BLK * TOPK * t + 16 * BLK * TOPK)
                    dve.wait_ge(vector_did, vec.before(now))
                    for k in range(TOPK):
                        for j in range(BLK):
                            base = flat(c.rows[:, bass.ds(BLK * now + j, 1), :]) if k == 0 else y1[:, j, :]
                            s = nc.vector.scalar_tensor_tensor(
                                out=(y1 if k == 0 else y)[:, j, :], in0=got[u][:, TOPK * j + k, :],
                                scalar=ex.gates[:, bass.ds(BLK * now + j, 1), k], in1=base, op0=ALU.mult, op1=ALU.add)
                        if k == 0:
                            s.then_inc(vector_did, 1)
                            did(now, "one")
                    if extra is not None:
                        s.then_inc(vector_did, 1)
                        did(now, "two")
                        s = nc.vector.tensor_tensor(y[:, :, :], y[:, :, :], extra[:, bass.ds(BLK * now, BLK), :], ALU.add)
                    s.then_inc(added, 1)
                    dve.wait_ge(added, now + 3)
                    for j in range(BLK):
                        s = nc.vector.bn_stats(stats[:, j, :], y[:, j, :])
                    s.then_inc(vector_did, 1)
                    did(now, "stats")
                    dve.sem_inc(c.vector_passed, 1)
                    dve.wait_ge(added, 3)
                    for j in range(BLK):
                        s = nc.vector.bn_aggr(moments[:, j, :], stats[:, j, :])
                    s.then_inc(vector_did, 1)
                    dve.wait_ge(rooted, now + 1)
                    nc.vector.reciprocal(rstd[:, :], std[:, :]).then_inc(vector_did, 1)
                    did(now, "rstd")
                    for j in range(BLK):
                        row = flat(c.rows[:, bass.ds(BLK * now + j, 1), :])
                        s = nc.vector.tensor_scalar(row, y[:, j, :], moments[:, j, 0:1], rstd[:, j:j + 1],
                                                    ALU.subtract, ALU.mult)
                    s.then_inc(vector_did, 1)


def load_columns(sp, a, names, dst, done):
    for k, name in enumerate(names):
        sp.dma_start(dst[:, k:k + 1], a[name]).then_inc(done, 16)


def mix_time(nc, c, mean, rstd, twice):
    a = c.a
    names = ("mix_k", "mix_v", "mix_r", "rwkv_ln1_g", "rwkv_ln1_b", "time_decay", "time_first")
    vec = Count("ekv", "scan_a", "scan_b", "b_eps", "b_inv", "ratio", "gated")
    with ExitStack() as ctx:
        sb, psum, sem = scope(nc, ctx, "time")
        raw, w_now, w_old = (sb(x, [P, 3, D]) for x in ("w_raw", "w_now", "w_old"))
        w_out = sb("w_out", [P, D])
        cols, rest = sb("cols", [P, len(names)]), sb("rest", [P, 3])
        decay, keep = sb("decay", [P, 1]), sb("keep", [P, 1])
        decay_row = sb("decay_row", [P, T])
        z = [sb(f"z{u}", [P, BLK, D]) for u in range(2)]
        xn = [sb(f"xn{u}", [P, 1 + T]) for u in range(2)]
        e_k, half_tanh, gated = ([sb(f"{x}{u}", [P, T]) for u in range(2)] for x in ("e_k", "half_tanh", "gated"))
        ekv, scan_a, scan_b, b_eps, b_inv, ratio = (sb(x, [P, T]) for x in ("ekv", "scan_a", "scan_b", "b_eps", "b_inv", "ratio"))
        turn_bank, k_bank, v_bank, ro_bank = (
            [psum(f"{x}{u}") for u in range(2)] for x in ("turn_bank", "k_bank", "v_bank", "ro_bank"))
        loaded, decayed, folded, zero_set = sem("loaded"), sem("decayed"), sem("folded"), sem("zero_set")
        z_ready, turned, xn_ready, made, exped, tanhed, vector_did, o_made, o_out = (
            sem(x) for x in ("z_ready", "turned", "xn_ready", "made", "exped", "tanhed", "vector_did", "o_made", "o_out"))
        block = ctx.enter_context(nc.Block())
        gain, shift = cols[:, 3:4], cols[:, 4:5]
        first = cols[:, 6:7]
        loads = 16 * (4 + len(names))

        @block.sync
        def _(sp):
            for k, name in enumerate(("rwkv_wk", "rwkv_wv", "rwkv_wr")):
                sp.dma_start(raw[:, k, :], a[name]).then_inc(loaded, 16)
            sp.dma_start(w_out[:, :], a["rwkv_wo"]).then_inc(loaded, 16)
            load_columns(sp, a, names, cols, loaded)

        @block.tensor
        def _(pe):
            pe.wait_ge(folded, 3)

            def turn(t, u):
                pe.wait_ge(z_ready, t + 1)
                for j in range(BLK):
                    mm = nc.tensor.transpose(turn_bank[u][:, j * P:(j + 1) * P], z[u][:, j, :], c.ident[:, :])
                mm.then_inc(turned, 1)

            def project(t, u):
                pe.wait_ge(xn_ready, t + 1)
                for k, out in enumerate((k_bank[u][:, 0:T], v_bank[u][:, 0:T], ro_bank[u][:, 0:T])):
                    nc.tensor.matmul(out, w_now[:, k, :], xn[u][:, 1:], start=True, stop=False)
                    nc.tensor.matmul(out, w_old[:, k, :], xn[u][:, 0:T], start=False, stop=True).then_inc(made, 1)

            def output(t, u):
                pe.wait_ge(vector_did, vec(t, "gated"))
                for j in range(BLK):
                    mm = nc.tensor.matmul(ro_bank[u][:, T + j * D:T + (j + 1) * D], gated[u][:, j * P:(j + 1) * P],
                                          w_out[:, :], start=True, stop=True)
                mm.then_inc(o_made, 1)

            turn(0, 0)
            project(0, 0)
            turn(1, 1)
            with pe.Fori(0, B // 2 - 1) as i:
                for u in range(2):
                    t = 2 * i + u
                    pe.wait_ge(o_out, t)
                    project(t + 1, 1 - u)
                    turn(t + 2, u)
                    output(t, u)
            pe.wait_ge(o_out, B - 2)
            project(B - 1, 1)
            output(B - 2, 0)
            output(B - 1, 1)

        @block.scalar
        def _(act):
            act.wait_ge(loaded, loads)
            act.wait_ge(zero_set, 1)
            nc.scalar.activation(decay[:, :], cols[:, 5:6], ACT.Exp).then_inc(decayed, 1)
            act.wait_ge(decayed, 1)
            nc.scalar.activation(keep[:, :], decay[:, :], ACT.Exp, scale=-1.0).then_inc(decayed, 1)

            def affine(t, u):
                act.wait_ge(turned, t + 1)
                nc.scalar.activation(xn[u][:, 1:], turn_bank[u][:, 0:T], ACT.Identity, bias=shift, scale=gain).then_inc(xn_ready, 1)

            def exponents(t, u):
                act.wait_ge(made, 3 * t + 1)
                nc.scalar.activation(e_k[u][:, 0:1], k_bank[u][:, 0:1], ACT.Exp, bias=first)
                nc.scalar.activation(e_k[u][:, 1:], k_bank[u][:, 1:T], ACT.Exp).then_inc(exped, 1)
                act.wait_ge(made, 3 * t + 3)
                nc.scalar.activation(half_tanh[u][:, :], ro_bank[u][:, 0:T], ACT.Tanh, scale=0.5).then_inc(tanhed, 1)

            affine(0, 0)
            affine(1, 1)
            with act.Fori(0, B // 2 - 1) as i:
                for u in range(2):
                    t = 2 * i + u
                    act.wait_ge(vector_did, vec.before(t))
                    exponents(t, u)
                    affine(t + 2, u)
            for u in range(2):
                act.wait_ge(vector_did, vec.before(B - 2 + u))
                exponents(B - 2 + u, u)

        @block.vector
        def _(dve):
            did = lambda t, name: dve.wait_ge(vector_did, vec(t, name))
            nc.vector.memset(xn[0][:, 0:1], 0.0)
            nc.vector.memset(xn[1][:, 0:1], 0.0).then_inc(zero_set, 1)
            dve.wait_ge(loaded, loads)
            nc.vector.tensor_scalar(rest[:, :], cols[:, 0:3], -1.0, 1.0, ALU.mult, ALU.add).then_inc(folded, 1)
            dve.wait_ge(folded, 1)
            for k in range(3):
                nc.vector.tensor_scalar(w_now[:, k, :], raw[:, k, :], cols[:, k:k + 1], None, ALU.mult)
                nc.vector.tensor_scalar(w_old[:, k, :], raw[:, k, :], rest[:, k:k + 1], None, ALU.mult)
            nc.vector.tensor_scalar(w_out[:, :], w_out[:, :], 0.5, None, ALU.mult).then_inc(folded, 1)
            dve.wait_ge(decayed, 2)
            nc.vector.tensor_copy(decay_row[:, :], keep[:, 0:1].broadcast_to([P, T])).then_inc(folded, 1)
            dve.wait_ge(folded, 3)

            def prepare(t, u):
                normalise_rows(nc, c.rows, mean, rstd, z[u], BLK * t, BLK).then_inc(z_ready, 1)

            def mix(t, u):
                dve.wait_ge(exped, t + 1)
                dve.wait_ge(made, 3 * t + 2)
                nc.vector.tensor_tensor(ekv[:, :], e_k[u][:, :], v_bank[u][:, 0:T], ALU.mult).then_inc(vector_did, 1)
                did(t, "ekv")
                nc.vector.tensor_tensor_scan(scan_a[:, :], decay_row[:, :], ekv[:, :], 0.0, ALU.mult, ALU.add
                                             ).then_inc(vector_did, 1)
                nc.vector.tensor_tensor_scan(scan_b[:, :], decay_row[:, :], e_k[u][:, :], 0.0, ALU.mult, ALU.add
                                             ).then_inc(vector_did, 1)
                did(t, "scan_b")
                nc.vector.tensor_scalar(b_eps[:, :], scan_b[:, :], WKV_EPS, None, ALU.add).then_inc(vector_did, 1)
                did(t, "b_eps")
                nc.vector.reciprocal(b_inv[:, :], b_eps[:, :]).then_inc(vector_did, 1)
                did(t, "b_inv")
                nc.vector.tensor_tensor(ratio[:, :], scan_a[:, :], b_inv[:, :], ALU.mult).then_inc(vector_did, 1)
                dve.wait_ge(tanhed, t + 1)
                did(t, "ratio")
                nc.vector.scalar_tensor_tensor(out=gated[u][:, :], in0=half_tanh[u][:, :], scalar=1.0, in1=ratio[:, :],
                                               op0=ALU.add, op1=ALU.mult).then_inc(vector_did, 1)

            def add(t, u):
                dve.wait_ge(o_made, t + 1)
                out = ro_bank[u][:, T:T + BLK * D]
                rows = c.rows[:, bass.ds(BLK * t, BLK), :].rearrange("p j d -> p (j d)")
                nc.vector.scalar_tensor_tensor(out=twice[:, bass.ds(BLK * t, BLK), :].rearrange("p j d -> p (j d)"), in0=rows,
                                               scalar=2.0, in1=out, op0=ALU.mult, op1=ALU.add)
                nc.vector.tensor_tensor(rows, rows, out, ALU.add).then_inc(o_out, 1)

            prepare(0, 0)
            prepare(1, 1)
            mix(0, 0)
            with dve.Fori(0, B // 2 - 1) as i:
                for u in range(2):
                    t = 2 * i + u
                    dve.wait_ge(turned, t + 1)
                    prepare(t + 2, u)
                    add(t, u)
                    mix(t + 1, 1 - u)
            add(B - 2, 0)
            mix(B - 1, 1)
            add(B - 1, 1)


def normalise_rows(nc, rows, mean, rstd, out, t, count):
    for j in range(count):
        s = nc.vector.tensor_scalar(out[:, j, :], flat(rows[:, bass.ds(t + j, 1), :]), mean[:, bass.ds(t + j, 1)],
                                    rstd[:, bass.ds(t + j, 1)], ALU.subtract, ALU.mult)
    return s


def mix_channels(nc, c, mean, rstd, total):
    a = c.a
    NK = 4 * D // P
    names = ("rwkv_ln2_g", "rwkv_ln2_b")
    with ExitStack() as ctx:
        sb, psum, sem = scope(nc, ctx, "channel")
        w_k, w_v, w_r = sb("w_k", [P, NK * P]), sb("w_v", [P, NK, D]), sb("w_r", [P, D])
        cols = sb("cols", [P, len(names)])
        z = [sb(f"z{u}", [P, BLK, D]) for u in range(2)]
        yn = [sb(f"yn{u}", [P, 1 + T]) for u in range(2)]
        both = [sb(f"both{u}", [P, T]) for u in range(2)]
        kk = [sb(f"kk{u}", [P, NK, T]) for u in range(2)]
        relu = sb("relu", [P, NK, T])
        half_tanh, gated = sb("half_tanh", [P, T]), sb("gated", [P, T])
        turn_bank = [psum(f"turn_bank{u}") for u in range(2)]
        k_bank = [psum(f"k_bank{k}") for k in range(NK)]
        r_bank, o_bank = psum("r_bank"), psum("o_bank")
        loaded, folded, zero_set = sem("loaded"), sem("folded"), sem("zero_set")
        z_ready, turned, yn_ready, both_ready, r_made, k_made, rectified, squared, tanhed, o_made, gated_done, o_out = (
            sem(x) for x in ("z_ready", "turned", "yn_ready", "both_ready", "r_made", "k_made", "rectified", "squared", "tanhed", "o_made",
                             "gated_done", "o_out"))
        block = ctx.enter_context(nc.Block())
        loads = 16 * (3 + len(names))

        @block.sync
        def _(sp):
            sp.dma_start(w_k[:, :], a["rwkv_wfk"]).then_inc(loaded, 16)
            sp.dma_start(w_v[:, :, :], a["rwkv_wfv"].rearrange("(k p) d -> p k d", p=P)).then_inc(loaded, 16)
            sp.dma_start(w_r[:, :], a["rwkv_wfr"]).then_inc(loaded, 16)
            load_columns(sp, a, names, cols, loaded)

        @block.tensor
        def _(pe):
            pe.wait_ge(folded, 2)

            def turn(t, u):
                pe.wait_ge(z_ready, t + 1)
                for j in range(BLK):
                    mm = nc.tensor.transpose(turn_bank[u][:, j * P:(j + 1) * P], z[u][:, j, :], c.ident[:, :])
                mm.then_inc(turned, 1)

            def keys(t, u):
                pe.wait_ge(tanhed, t)
                pe.wait_ge(yn_ready, t + 1)
                for j in range(BLK):
                    mm = nc.tensor.matmul(r_bank[:, j * D:(j + 1) * D], yn[u][:, 1 + j * P:1 + (j + 1) * P], w_r[:, :],
                                          start=True, stop=True)
                mm.then_inc(r_made, 1)
                pe.wait_ge(both_ready, t + 1)
                for k in range(NK):
                    pe.wait_ge(rectified, NK * t)
                    nc.tensor.matmul(k_bank[k][:, 0:T], w_k[:, k * P:(k + 1) * P], both[u][:, :], start=True, stop=True
                                     ).then_inc(k_made, 1)

            def values(t, u):
                pe.wait_ge(o_out, t)
                pe.wait_ge(squared, t + 1)
                for j in range(BLK):
                    for k in range(NK):
                        mm = nc.tensor.matmul(o_bank[:, j * D:(j + 1) * D], kk[u][:, k, j * P:(j + 1) * P], w_v[:, k, :],
                                              start=k == 0, stop=k == NK - 1)
                mm.then_inc(o_made, 1)

            turn(0, 0)
            turn(1, 1)
            keys(0, 0)
            with pe.Fori(0, B // 2 - 1) as i:
                for u in range(2):
                    t = 2 * i + u
                    turn(t + 2, u)
                    keys(t + 1, 1 - u)
                    values(t, u)
            keys(B - 1, 1)
            values(B - 2, 0)
            values(B - 1, 1)

        @block.scalar
        def _(act):
            act.wait_ge(loaded, loads)
            act.wait_ge(zero_set, 1)

            def affine(t, u):
                act.wait_ge(turned, t + 1)
                nc.scalar.activation(yn[u][:, 1:], turn_bank[u][:, 0:T], ACT.Identity, bias=cols[:, 1:2],
                                     scale=cols[:, 0:1]).then_inc(yn_ready, 1)

            def gate(t):
                act.wait_ge(squared, t)
                for k in range(NK):
                    act.wait_ge(k_made, NK * t + k + 1)
                    nc.scalar.activation(relu[:, k, :], k_bank[k][:, 0:T], ACT.Relu).then_inc(rectified, 1)
                act.wait_ge(r_made, t + 1)
                act.wait_ge(gated_done, t)
                nc.scalar.activation(half_tanh[:, :], r_bank[:, 0:BLK * D], ACT.Tanh, scale=0.5).then_inc(tanhed, 1)

            affine(0, 0)
            affine(1, 1)
            gate(0)
            with act.Fori(0, B // 2 - 1) as i:
                for u in range(2):
                    t = 2 * i + u
                    act.wait_ge(both_ready, t + 1)
                    affine(t + 2, u)
                    gate(t + 1)
            gate(B - 1)

        @block.gpsimd
        def _(pool):
            def add_old(t, u):
                pool.wait_ge(yn_ready, t + 1)
                nc.gpsimd.tensor_tensor(both[u][:, :], yn[u][:, 1:], yn[u][:, 0:T], ALU.add).then_inc(both_ready, 1)

            add_old(0, 0)
            add_old(1, 1)
            with pool.Fori(0, B // 2 - 1) as i:
                for u in range(2):
                    pool.wait_ge(k_made, NK * (2 * i + u) + NK)
                    add_old(2 * i + u + 2, u)

        @block.vector
        def _(dve):
            nc.vector.memset(yn[0][:, 0:1], 0.0)
            nc.vector.memset(yn[1][:, 0:1], 0.0).then_inc(zero_set, 1)
            dve.wait_ge(loaded, loads)
            nc.vector.tensor_scalar(w_k[:, :], w_k[:, :], 0.5, None, ALU.mult).then_inc(folded, 1)
            nc.vector.tensor_scalar(w_v[:, :, :], w_v[:, :, :], 0.5, None, ALU.mult).then_inc(folded, 1)

            def prepare(t, u):
                normalise_rows(nc, c.rows, mean, rstd, z[u], BLK * t, BLK).then_inc(z_ready, 1)

            def square(t, u):
                dve.wait_ge(rectified, NK * t + NK)
                nc.vector.tensor_tensor(kk[u][:, :, :], relu[:, :, :], relu[:, :, :], ALU.mult).then_inc(squared, 1)

            def add(t, u):
                dve.wait_ge(tanhed, t + 1)
                dve.wait_ge(o_made, t + 1)
                nc.vector.scalar_tensor_tensor(out=gated[:, :], in0=half_tanh[:, :], scalar=1.0, in1=o_bank[:, 0:BLK * D],
                                               op0=ALU.add, op1=ALU.mult).then_inc(gated_done, 1)
                dve.wait_ge(gated_done, t + 1)
                sums = total[:, bass.ds(BLK * t, BLK), :].rearrange("p j d -> p (j d)")
                nc.vector.tensor_tensor(sums, sums, gated[:, :], ALU.add).then_inc(o_out, 1)

            prepare(0, 0)
            prepare(1, 1)
            square(0, 0)
            with dve.Fori(0, B // 2 - 1) as i:
                for u in range(2):
                    t = 2 * i + u
                    dve.wait_ge(turned, t + 1)
                    prepare(t + 2, u)
                    square(t + 1, 1 - u)
                    dve.wait_ge(o_out, t)
                    add(t, u)
            square(B - 1, 1)
            add(B - 2, 0)
            dve.wait_ge(o_out, B - 1)
            add(B - 1, 1)


def keep_rows(nc, c, total, mean, rstd):
    CH = 8
    with ExitStack() as ctx:
        sb, psum, sem = scope(nc, ctx, "keep")
        ready, stored = sem("ready"), sem("stored")
        block = ctx.enter_context(nc.Block())
        x3 = c.x3.rearrange("b (j p) d -> p (b j) d", p=P)

        @block.vector
        def _(dve):
            with dve.Fori(0, NT // CH) as i:
                for j in range(CH):
                    at = CH * i + j
                    s = nc.vector.tensor_scalar(flat(c.rows[:, bass.ds(at, 1), :]), flat(total[:, bass.ds(at, 1), :]),
                                                mean[:, bass.ds(at, 1)], rstd[:, bass.ds(at, 1)], ALU.subtract, ALU.mult)
                s.then_inc(ready, 1)

        @block.sync
        def _(sp):
            for i in range(NT // CH):
                sp.wait_ge(ready, i + 1)
                sp.dma_start(x3[:, i * CH:(i + 1) * CH, :], c.rows[:, i * CH:(i + 1) * CH, :]).then_inc(stored, 16)
            sp.wait_ge(stored, 16 * (NT // CH))


def recur(nc, c):
    with ExitStack() as ctx:
        sb, psum, sem = scope(nc, ctx, "recur")
        twice = sb("twice", [P, NT, D])
        mean, rstd = sb("mean", [P, NT]), sb("rstd", [P, NT])
        row_stats(nc, c, "recur1", c.rows, mean[:, :], rstd[:, :], LN_EPS)
        mix_time(nc, c, mean, rstd, twice)
        row_stats(nc, c, "recur2", c.rows, mean[:, :], rstd[:, :], LN_EPS)
        mix_channels(nc, c, mean, rstd, twice)
        row_stats(nc, c, "recur3", twice, mean[:, :], rstd[:, :], LN_EPS)
        keep_rows(nc, c, twice, mean, rstd)


def load_groups(nc, dst, src, tag):
    with ExitStack() as ctx:
        sb, psum, sem = scope(nc, ctx, tag)
        loaded = sem("loaded")
        block = ctx.enter_context(nc.Block())
        view = src.rearrange("s (g n) d -> n s g d", n=NPG)

        @block.sync
        def _(sp):
            for n in range(NPG):
                sp.dma_start(dst[n * B:(n + 1) * B, :, :], view[n]).then_inc(loaded, 16)
            sp.wait_ge(loaded, 16 * NPG)


def attend_batches(nc, c, mean, rstd):
    a = c.a
    HB = 4
    SLOTS = 4
    STEPS = NT // SLOTS
    C = SLOTS * P
    soft = Count("peak", "centred")
    with ExitStack() as ctx:
        sb, psum, sem = scope(nc, ctx, "batch")
        w_in, w_out = sb("w_in", [P, 3 * D]), sb("w_out", [P, D])
        w_out_b = sb("w_out_b", [P, HB, D])
        b_in, cols = sb("b_in", [P, 3]), sb("cols", [P, 2])
        out_bias, row_bias = sb("out_bias", [P, D]), sb("row_bias", [P, D])
        of_b, of_a = sb("of_b", [P, HB]), sb("of_a", [P, HB])
        q_shift, k_shift = sb("q_shift", [P, HB]), sb("k_shift", [P, HB])
        column_a = sb("column_a", [P, NH, HD])
        causal_f, causal = sb("causal_f", [P, NPG * P]), sb("causal", [P, NPG * P], BF16)
        ident_bf = sb("ident_bf", [P, P], BF16)
        of_head = sb("of_head", [P, HB, HB])
        z = sb("z", [P, SLOTS, D])
        hn = [sb(f"hn{v}", [P, C]) for v in range(2)]
        q_blocks, k_blocks, hn_blocks = ([sb(f"{x}{v}", [P, SLOTS * NPG, HB, B]) for v in range(2)]
                                         for x in ("q_blocks", "k_blocks", "hn_blocks"))
        v_blocks = [sb(f"v_blocks{s}", [P, NPG, D]) for s in range(SLOTS)]
        centred, e_x, prob = ([sb(f"{x}{u}", [P, NPG * HB, B]) for u in range(2)] for x in ("centred", "e_x", "prob"))
        peak, total = sb("peak", [P, NPG * HB]), sb("total", [P, NPG * HB])
        recip = [sb(f"recip_{u}", [P, NPG * HB]) for u in range(2)]
        prob_t, out_t = sb("prob_t", [P, NPG * P]), sb("out_t", [P, HB, NPG, B])
        fresh = sb("fresh", [P, D])
        turn_bank, q_bank, k_bank, v_bank, s_bank, p_bank, o_bank, x_bank = (
            psum(x) for x in ("turn_bank", "q_bank", "k_bank", "v_bank", "s_bank", "p_bank", "o_bank", "x_bank"))
        loaded, made, folded = sem("loaded"), sem("made"), sem("folded")
        hn_spread = sem("hn_spread")
        z_ready, turned, hn_ready, q_made, k_made, q_ready, k_ready = (
            sem(x) for x in ("z_ready", "turned", "hn_ready", "q_made", "k_made", "q_ready", "k_ready"))
        s_made, v_made, v_ready, softened, exped, totalled, recip_done, normed = (
            sem(x) for x in ("s_made", "v_made", "v_ready", "softened", "exped", "totalled", "recip_done", "normed"))
        p_turned, p_out, o_made, o_out, x_made, x_out, rows_done = (
            sem(x) for x in ("p_turned", "p_out", "o_made", "o_out", "x_made", "x_out", "rows_done"))
        block = ctx.enter_context(nc.Block())
        names = ("attn1_ln_w", "attn1_ln_b")
        loads = 16 * 6

        @block.sync
        def _(sp):
            sp.dma_start(w_in[:, :], a["in_proj_t"]).then_inc(loaded, 16)
            sp.dma_start(b_in[:, :], a["in_proj_b"]).then_inc(loaded, 16)
            sp.dma_start(w_out[:, :], a["out_proj_t"]).then_inc(loaded, 16)
            sp.dma_start(out_bias[:, :], a["out_proj_b"].broadcast_to([P, D])).then_inc(loaded, 16)
            load_columns(sp, a, names, cols, loaded)

        @block.gpsimd
        def _(pool):
            nc.gpsimd.memset(of_a[:, :], 1.0).then_inc(made, 1)
            pool.wait_ge(made, 1)
            nc.gpsimd.affine_select(out=of_a[:, :], in_=of_a[:, :], compare_op=ALU.is_ge, fill=0.0, base=0,
                                    pattern=[[-P // HB, HB]], channel_multiplier=1).then_inc(made, 1)
            pool.wait_ge(made, 2)
            nc.gpsimd.affine_select(out=of_a[:, :], in_=of_a[:, :], compare_op=ALU.is_ge, fill=0.0, base=P // HB - 1,
                                    pattern=[[P // HB, HB]], channel_multiplier=-1).then_inc(made, 1)
            work = of_head[:, :, :]
            nc.gpsimd.memset(work, 1.0).then_inc(made, 1)
            pool.wait_ge(made, 4)
            nc.gpsimd.affine_select(out=work, in_=work, compare_op=ALU.is_ge, fill=0.0, base=0,
                                    pattern=[[-HB * HD, HB], [-HD, HB]], channel_multiplier=1).then_inc(made, 1)
            pool.wait_ge(made, 5)
            nc.gpsimd.affine_select(out=work, in_=work, compare_op=ALU.is_ge, fill=0.0, base=HD - 1,
                                    pattern=[[HB * HD, HB], [HD, HB]], channel_multiplier=-1).then_inc(made, 1)
            nc.gpsimd.memset(column_a[:, :, :], 1.0).then_inc(made, 1)
            pool.wait_ge(made, 7)
            col = column_a[:, :, :].rearrange("p (x y) d -> p x (y d)", x=HB)
            nc.gpsimd.affine_select(out=col, in_=col, compare_op=ALU.is_ge, fill=0.0, base=0,
                                    pattern=[[-P // HB, HB], [0, P // HB]], channel_multiplier=1).then_inc(made, 1)
            pool.wait_ge(made, 8)
            nc.gpsimd.affine_select(out=col, in_=col, compare_op=ALU.is_ge, fill=0.0, base=P // HB - 1,
                                    pattern=[[P // HB, HB], [0, P // HB]], channel_multiplier=-1).then_inc(made, 1)
            nc.gpsimd.memset(causal_f[:, :], 0.0).then_inc(made, 1)
            pool.wait_ge(made, 10)
            for b in range(HB):
                s = nc.gpsimd.affine_select(out=causal_f[b * B:(b + 1) * B, :], in_=causal_f[b * B:(b + 1) * B, :],
                                            compare_op=ALU.is_ge, fill=-BIG, base=0, pattern=[[0, NPG * HB], [-1, B]],
                                            channel_multiplier=1)
            s.then_inc(made, 1)

            def normalise_probs(g, u):
                pool.wait_ge(recip_done, g + 1)
                nc.gpsimd.tensor_tensor(prob[u][:, :, :], e_x[u][:, :, :], bcast(recip[u][:, :], B), ALU.mult
                                        ).then_inc(normed, 1)

            def spread(f, v):
                pool.wait_ge(hn_ready, f + 1)
                pool.sem_inc(c.pool_passed, 1)
                pool.wait_ge(made, 11)
                rows = hn[v][:, :].rearrange("p (n s) -> p n s", s=B).unsqueeze(2).broadcast_to([P, SLOTS * NPG, HB, B])
                nc.gpsimd.tensor_copy(hn_blocks[v][:, :, :, :], rows).then_inc(hn_spread, 1)

            def step(f, v, first=False, last=False):
                for s in range(SLOTS):
                    g = SLOTS * f + s
                    if not first or s >= 2:
                        pool.wait_ge(p_turned, g - 1)
                    normalise_probs(g, s % 2)
                    if s == 1 and not last:
                        spread(f + 1, 1 - v)

            spread(0, 0)
            step(0, 0, first=True)
            with pool.Fori(0, (STEPS - 2) // 2) as i:
                step(2 * i + 1, 1)
                step(2 * i + 2, 0)
            step(STEPS - 1, 1, last=True)

        def positions(ap, s):
            return ap[:, s * P:(s + 1) * P]

        @block.tensor
        def _(pe):
            pe.wait_ge(loaded, loads)
            nc.tensor.matmul(x_bank[:, 0:D], b_in[:, 2:3].broadcast_to([P, P]), w_out[:, :], start=True, stop=True
                             ).then_inc(folded, 1)
            pe.wait_ge(folded, 4)

            def turn(f):
                pe.wait_ge(z_ready, f + 1)
                for s in range(SLOTS):
                    mm = nc.tensor.transpose(positions(turn_bank, s), z[:, s, :], c.ident[:, :])
                mm.then_inc(turned, 1)

            def project(f, v):
                pe.wait_ge(hn_ready, f + 1)
                pe.wait_ge(q_ready, f)
                nc.tensor.matmul(q_bank[:, :], w_in[:, 0:D], hn[v][:, :], start=True, stop=True).then_inc(q_made, 1)
                pe.wait_ge(k_ready, f)
                nc.tensor.matmul(k_bank[:, :], w_in[:, D:2 * D], hn[v][:, :], start=True, stop=True).then_inc(k_made, 1)

            def scores(g, s, v):
                pe.wait_ge(softened, soft.before(g))
                nc.tensor.matmul(s_bank[:, :], ident_bf[:, :], causal[:, :], start=True, stop=False)
                for n in range(NPG):
                    q, k = (x[v][:, s * NPG + n, :, :].rearrange("p h s -> p (h s)") for x in (q_blocks, k_blocks))
                    mm = nc.tensor.matmul(s_bank[:, n * P:(n + 1) * P], q, k, start=False, stop=n == NPG - 1)
                mm.then_inc(s_made, 1)

            def value(g, s, v):
                pe.wait_ge(v_ready, g)
                for n in range(NPG):
                    rows = hn_blocks[v][:, s * NPG + n, :, :].rearrange("p h s -> p (h s)")
                    mm = nc.tensor.matmul(v_bank[:, n * D:(n + 1) * D], rows, w_in[:, 2 * D:],
                                          start=True, stop=True)
                mm.then_inc(v_made, 1)

            def turn_probs(g, u):
                pe.wait_ge(normed, g + 1)
                pe.wait_ge(p_out, g)
                flat_p = prob[u][:, :, :].rearrange("p h s -> p (h s)")
                for n in range(NPG):
                    mm = nc.tensor.transpose(p_bank[:, n * P:(n + 1) * P], flat_p[:, n * P:(n + 1) * P], c.ident[:, :])
                mm.then_inc(p_turned, 1)

            def mix(g, s):
                pe.wait_ge(p_out, g + 1)
                pe.wait_ge(o_out, g)
                for n in range(NPG):
                    mm = nc.tensor.matmul(o_bank[:, n * P:(n + 1) * P], v_blocks[s][:, n, :], prob_t[:, n * P:(n + 1) * P],
                                          start=True, stop=True)
                mm.then_inc(o_made, 1)

            def output(g):
                pe.wait_ge(o_out, g + 1)
                pe.wait_ge(x_out, g)
                for b in range(HB):
                    mm = nc.tensor.matmul(x_bank[:, 0:D], out_t[:, b, :, :].rearrange("p n s -> p (n s)"), w_out_b[:, b, :],
                                          start=b == 0, stop=b == HB - 1)
                mm.then_inc(x_made, 1)

            def step(f, v, first=False, last=False):
                for s in range(SLOTS):
                    g = SLOTS * f + s
                    back = not first or s >= 2
                    if back:
                        turn_probs(g - 2, s % 2)
                    if s == 0:
                        pe.wait_ge(q_ready, f + 1)
                        pe.wait_ge(k_ready, f + 1)
                        pe.wait_ge(hn_spread, f + 1)
                    scores(g, s, v)
                    value(g, s, v)
                    if not last:
                        if s == 1:
                            turn(f + 1)
                        if s == 2:
                            project(f + 1, 1 - v)
                    if back:
                        mix(g - 2, (s - 2) % SLOTS)
                    if not first or s >= 3:
                        output(g - 3)

            turn(0)
            project(0, 0)
            step(0, 0, first=True)
            with pe.Fori(0, (STEPS - 2) // 2) as i:
                step(2 * i + 1, 1)
                step(2 * i + 2, 0)
            step(STEPS - 1, 1, last=True)
            for s in range(2):
                turn_probs(NT - 2 + s, s)
                mix(NT - 2 + s, SLOTS - 2 + s)
                output(NT - 3 + s)
            output(NT - 1)

        @block.scalar
        def _(act):
            act.wait_ge(loaded, loads)
            act.wait_ge(folded, 3)

            def affine(f, v):
                act.wait_ge(turned, f + 1)
                nc.scalar.activation(hn[v][:, :], turn_bank[:, :], ACT.Identity, bias=cols[:, 1:2], scale=cols[:, 0:1]
                                     ).then_inc(hn_ready, 1)

            def place_queries(f, v):
                act.wait_ge(q_made, f + 1)
                for b in range(HB):
                    e = nc.scalar.activation(q_blocks[v][:, :, b, :], q_bank[:, :].rearrange("p (n s) -> p n s", s=B),
                                             ACT.Identity, bias=q_shift[:, b:b + 1], scale=of_b[:, b:b + 1])
                e.then_inc(q_ready, 1)

            def probs_out(g):
                act.wait_ge(p_turned, g + 1)
                act.wait_ge(o_made, g)
                nc.scalar.copy(prob_t[:, :], p_bank[:, :]).then_inc(p_out, 1)

            def exponents(g, u):
                act.wait_ge(softened, soft(g, "centred"))
                nc.scalar.activation(e_x[u][:, :, :], centred[u][:, :, :], ACT.Exp, scale=SM_SCALE).then_inc(exped, 1)

            def outputs_out(g):
                act.wait_ge(o_made, g + 1)
                act.wait_ge(x_made, g)
                nc.scalar.copy(out_t[:, :, :, :], o_bank[:, :].rearrange("p (n h s) -> p h n s", n=NPG, h=HB)
                               ).then_inc(o_out, 1)

            def step(f, v, first=False, last=False):
                for s in range(SLOTS):
                    g = SLOTS * f + s
                    back = not first or s >= 2
                    if back:
                        probs_out(g - 2)
                        act.wait_ge(normed, g - 1)
                    exponents(g, s % 2)
                    if not last:
                        if s == 1:
                            affine(f + 1, 1 - v)
                        if s == 2:
                            place_queries(f + 1, 1 - v)
                    if back:
                        outputs_out(g - 2)

            affine(0, 0)
            place_queries(0, 0)
            step(0, 0, first=True)
            with act.Fori(0, (STEPS - 2) // 2) as i:
                step(2 * i + 1, 1)
                step(2 * i + 2, 0)
            step(STEPS - 1, 1, last=True)
            for s in range(2):
                probs_out(NT - 2 + s)
                outputs_out(NT - 2 + s)

        @block.vector
        def _(dve):
            dve.wait_ge(made, 11)
            nc.vector.tensor_reduce(of_b[:, :], of_head[:, :, :].rearrange("p x y -> p y x"), AX.X, ALU.add).then_inc(folded, 1)
            nc.vector.tensor_copy(causal[:, :], causal_f[:, :])
            nc.vector.tensor_copy(ident_bf[:, :], c.ident[:, :])
            dve.wait_ge(loaded, loads)
            dve.wait_ge(folded, 2)
            nc.vector.tensor_tensor(row_bias[:, :], x_bank[:, 0:D], out_bias[:, :], ALU.add)
            for b in range(HB):
                nc.vector.tensor_scalar(w_out_b[:, b, :], w_out[:, :], of_b[:, b:b + 1], None, ALU.mult)
            nc.vector.tensor_scalar(q_shift[:, :], of_b[:, :], b_in[:, 0:1], None, ALU.mult).then_inc(folded, 1)
            nc.vector.tensor_scalar(k_shift[:, :], of_a[:, :], b_in[:, 1:2], None, ALU.mult).then_inc(folded, 1)
            dve.wait_ge(folded, 4)

            def prepare(f):
                for s in range(SLOTS):
                    at = SLOTS * f + s
                    m = nc.vector.tensor_scalar(z[:, s, :], flat(c.rows[:, bass.ds(at, 1), :]), mean[:, bass.ds(at, 1)],
                                                rstd[:, bass.ds(at, 1)], ALU.subtract, ALU.mult)
                m.then_inc(z_ready, 1)

            def place_keys(f, v):
                dve.wait_ge(k_made, f + 1)
                for h in range(HB):
                    m = nc.vector.tensor_scalar(k_blocks[v][:, :, h, :], k_bank[:, :].rearrange("p (n s) -> p n s", s=B),
                                                of_a[:, h:h + 1], k_shift[:, h:h + 1], ALU.mult, ALU.add)
                m.then_inc(k_ready, 1)

            def sums(g, u):
                dve.wait_ge(exped, g + 1)
                nc.vector.tensor_reduce(total[:, :], e_x[u][:, :, :], AX.X, ALU.add).then_inc(totalled, 1)
                dve.wait_ge(totalled, g + 1)
                nc.vector.reciprocal(recip[u][:, :], total[:, :]).then_inc(recip_done, 1)

            def soften(g, u):
                dve.wait_ge(s_made, g + 1)
                s_view = s_bank[:, :].rearrange("p (h s) -> p h s", s=B)
                nc.vector.tensor_reduce(peak[:, :], s_view, AX.X, ALU.max).then_inc(softened, 1)
                dve.wait_ge(softened, soft(g, "peak"))
                nc.vector.tensor_tensor(centred[u][:, :, :], s_view, bcast(peak[:, :], B), ALU.subtract).then_inc(softened, 1)

            def place_values(g, s):
                dve.wait_ge(v_made, g + 1)
                nc.vector.tensor_tensor(v_blocks[s][:, :, :], v_bank[:, :].rearrange("p (n d) -> p n d", d=D),
                                        along(column_a[:, :, :].rearrange("p h d -> p (h d)"), NPG), ALU.mult
                                        ).then_inc(v_ready, 1)

            def add(g):
                dve.wait_ge(x_made, g + 1)
                dve.wait_ge(rows_done, g)
                nc.vector.tensor_tensor(fresh[:, :], x_bank[:, 0:D], row_bias[:, :], ALU.add).then_inc(x_out, 1)
                dve.wait_ge(x_out, g + 1)
                row = flat(c.rows[:, bass.ds(g, 1), :])
                nc.vector.tensor_tensor(row, row, fresh[:, :], ALU.add).then_inc(rows_done, 1)

            def step(f, v, first=False, last=False):
                for s in range(SLOTS):
                    g = SLOTS * f + s
                    if not first or s >= 1:
                        sums(g - 1, (s - 1) % 2)
                    soften(g, s % 2)
                    place_values(g, s)
                    if not last:
                        if s == 0:
                            dve.wait_ge(turned, f + 1)
                            prepare(f + 1)
                        if s == 3:
                            place_keys(f + 1, 1 - v)
                    if not first or s >= 3:
                        add(g - 3)

            prepare(0)
            place_keys(0, 0)
            step(0, 0, first=True)
            with dve.Fori(0, (STEPS - 2) // 2) as i:
                step(2 * i + 1, 1)
                step(2 * i + 2, 0)
            step(STEPS - 1, 1, last=True)
            sums(NT - 1, 1)
            for s in range(3):
                add(NT - 3 + s)


def build(nc, a, out):
    with ExitStack() as ctx:
        c = Core(nc, ctx, a)
        setup(nc, c)
        with nc.sbuf_tensor("values", [P, NT, NH, HD + 1], F32) as values:
            project_heads(nc, c, values)
            attend_relative(nc, c, values)
        with ExitStack() as first:
            ex = Experts(nc, first, "moe0", 14, a["w1_0"], a["w2_0"])
            load_experts(nc, c, ex, a["rms_w_t"], None)
            send_to_experts(nc, c, ex, True)
            run_experts(nc, c, ex, ACT.Silu, False)
            combine(nc, c, ex, None, None)
        recur(nc, c)
        load_groups(nc, c.rows, c.x3, "groups_in")
        with nc.sbuf_tensor("attend1_mean", [P, NT], F32) as mean, nc.sbuf_tensor("attend1_rstd", [P, NT], F32) as rstd:
            row_stats(nc, c, "attend1", c.rows, mean[:, :], rstd[:, :], LN_EPS)
            attend_batches(nc, c, mean, rstd)
        with ExitStack() as second:
            ex = Experts(nc, second, "moe1", 8, a["w1_1"], a["w2_1"])
            residual = second.enter_context(nc.sbuf_tensor("residual", [P, NT, D], F32))
            load_groups(nc, residual, c.x3, "residual_in")
            load_experts(nc, c, ex, a["ln2_w"], a["ln2_b"])
            send_to_experts(nc, c, ex, False)
            run_experts(nc, c, ex, ACT.Gelu, True)
            combine(nc, c, ex, residual, out)


def kernel(**inputs):
    import numpy as _np
    import concourse.bacc as _bacc
    from concourse import mybir as _mybir
    from concourse.bass_utils import run_bass_kernel_spmd as _run

    nc = _bacc.Bacc("TRN2", target_bir_lowering=False, num_devices=1)
    take = lambda name: _np.asarray(inputs[name])
    column = lambda name: take(name)[:, None]
    laid_out = {
        "x": take("L0_attn_x"), "x_t": take("L0_attn_x").reshape(TOK, D).T,
        "wq_t": take("L0_attn_Wq").T, "wk_t": take("L0_attn_Wk").T, "wv_t": take("L0_attn_Wv").T,
        "wp_t": take("L0_attn_Wp").T, "bp": take("L0_attn_bp")[None], "rel_t": take("L0_attn_rel_embed").T,
        "router0": take("L0_ffn_router_w"), "rms_w_t": take("L0_ffn_rms_w").T, "w1_0": take("L0_ffn_w1"),
        "w2_0": take("L0_ffn_w2"), "rms_w_s_t": take("L0_ffn_rms_w_s").T, "w1_s": take("L0_ffn_w1_s"),
        "w2_s": take("L0_ffn_w2_s"),
        "rwkv_ln1_g": column("L1_attn_ln1_g"), "rwkv_ln1_b": column("L1_attn_ln1_b"),
        "rwkv_wk": take("L1_attn_Wk"), "rwkv_wv": take("L1_attn_Wv"), "rwkv_wr": take("L1_attn_Wr"),
        "rwkv_wo": take("L1_attn_Wo"), "time_decay": column("L1_attn_time_decay"),
        "time_first": column("L1_attn_time_first"), "mix_k": column("L1_attn_mix_k"),
        "mix_v": column("L1_attn_mix_v"), "mix_r": column("L1_attn_mix_r"),
        "rwkv_ln2_g": column("L1_attn_ln2_g"), "rwkv_ln2_b": column("L1_attn_ln2_b"),
        "rwkv_wfk": take("L1_attn_Wfk"), "rwkv_wfv": take("L1_attn_Wfv"), "rwkv_wfr": take("L1_attn_Wfr"),
        "attn1_ln_w": column("L1_ffn_ln1_w"), "attn1_ln_b": column("L1_ffn_ln1_b"),
        "in_proj_t": take("L1_ffn_in_proj_w").T, "in_proj_b": take("L1_ffn_in_proj_b").reshape(3, D).T,
        "out_proj_t": take("L1_ffn_out_proj_w").T, "out_proj_b": take("L1_ffn_out_proj_b")[None],
        "ln2_w": column("L1_ffn_ln2_w"), "ln2_b": column("L1_ffn_ln2_b"), "router1_t": take("L1_ffn_router_w").T,
        "w1_1": take("L1_ffn_w1"), "w2_1": take("L1_ffn_w2"),
    }
    arrays = {f"in_{name}": _np.ascontiguousarray(x) for name, x in laid_out.items()}
    a = {name: nc.dram_tensor(f"in_{name}", x.shape, _mybir.dt.from_np(x.dtype), kind="ExternalInput").ap()
         for name, x in laid_out.items()}
    out = nc.dram_tensor("out_0", (B, T, D), F32, kind="ExternalOutput").ap()
    build(nc, a, out)
    r = _run(nc, [arrays], core_ids=[0])
    return r.results[0]["out_0"]
```
